# Optimizing a Trainium2 kernel written in Bass

```python
import numpy as np
import jax
import jax.numpy as jnp

def _softmax(x, axis=-1):
    return jax.nn.softmax(x, axis=axis)

def _gelu(x):
    return jax.nn.gelu(x, approximate=True)

def _silu(x):
    return jax.nn.silu(x)

def _sigmoid(x):
    return jax.nn.sigmoid(x)

def _layernorm(x, axis=-1, eps=1e-05):
    m = jnp.mean(x, axis=axis, keepdims=True)
    v = jnp.var(x, axis=axis, keepdims=True)
    return (x - m) / jnp.sqrt(v + eps)

def _scatter_add(tgt, idx, src, axis=0):
    return tgt.at[idx].add(src)

def _segment_sum(src, seg, n):
    return jax.ops.segment_sum(src, seg, n)
kernel_name = 'mk_gps_d1_gnn_r8_907385'

def setup_inputs(seed: int=0):
    np.random.seed(seed)
    _w = jnp.asarray

    def _rec_inputs():
        import jax
        import jax.numpy as jnp
        _gk = jax.random.key(seed)
        x = -0.0002117 + 1 * jax.random.normal(jax.random.fold_in(_gk, 1), (6250, 512), jnp.float32)
        src = jax.random.randint(jax.random.fold_in(_gk, 2), (100000,), 0, 6250, jnp.int32)
        dst = jnp.minimum((6250 * jax.random.uniform(jax.random.fold_in(_gk, 3), (100000,)) ** 2.0).astype(jnp.int32), 49999)
        _o = jnp.argsort(dst, stable=True)
        src = src[_o]
        dst = dst[_o]
        return (x, src, dst)
    x, src, dst = _rec_inputs()

    def _L0_gnn_setup():
        import jax, jax.numpy as jnp
        import numpy as np
        N = 6250
        E = 50000
        D_IN = 512
        D_HID = 256
        D_OUT = 512
        key = jax.random.key(seed)
        k1, k2, k3, k4 = jax.random.split(key, 4)
        x = jax.random.normal(k1, (N, D_IN), dtype=jnp.float32)
        edge_index = jax.random.randint(k2, (2, E), 0, N, dtype=jnp.int64)
        W1 = jax.random.normal(k3, (D_IN, D_HID), dtype=jnp.float32) * (1.0 / np.sqrt(D_IN))
        b1 = jnp.zeros((D_HID,), dtype=jnp.float32)
        W2 = jax.random.normal(k4, (D_HID, D_OUT), dtype=jnp.float32) * (1.0 / np.sqrt(D_HID))
        b2 = jnp.zeros((D_OUT,), dtype=jnp.float32)
        return {'x': x, 'edge_index': edge_index, 'W1': W1, 'b1': b1, 'W2': W2, 'b2': b2}
    _L0_gnn_all = _L0_gnn_setup()
    _L0_gnn_in = {k: v for k, v in _L0_gnn_all.items() if k in ('W1', 'b1', 'W2', 'b2')}
    del _L0_gnn_all

    def _L0_mix_setup():
        import jax, jax.numpy as jnp
        import numpy as np
        B, T, DIM = (32, 392, 512)
        EMB = 512
        M = 256
        EPS_ATTN = 1e-08
        EPS_LN = 0.001

        def layernorm(x, g, b):
            mu = jnp.mean(x, axis=-1, keepdims=True)
            var = jnp.var(x, axis=-1, keepdims=True)
            return (x - mu) / jnp.sqrt(var + EPS_LN) * g + b

        def prm_exp(x, w):
            xd = jnp.sum(x * x, axis=-1, keepdims=True) / 2.0
            wtx = jnp.einsum('bti,mi->btm', x, w)
            return jnp.exp(wtx - xd) / jnp.sqrt(jnp.float32(M))
        key = jax.random.key(seed)
        ks = jax.random.split(key, 16)
        s_in = 1.0 / np.sqrt(DIM)
        s_emb = 1.0 / np.sqrt(EMB)
        x = jax.random.normal(ks[0], (B, T, DIM), dtype=jnp.float32)
        kqv_w = jax.random.normal(ks[1], (DIM, 3 * EMB), dtype=jnp.float32) * s_in
        kqv_b = jnp.zeros((3 * EMB,), dtype=jnp.float32)
        proj_w = jax.random.normal(ks[2], (EMB, EMB), dtype=jnp.float32) * s_emb
        proj_b = jnp.zeros((EMB,), dtype=jnp.float32)
        n1_g = jnp.ones((DIM,), dtype=jnp.float32)
        n1_b = jnp.zeros((DIM,), dtype=jnp.float32)
        n2_g = jnp.ones((EMB,), dtype=jnp.float32)
        n2_b = jnp.zeros((EMB,), dtype=jnp.float32)
        mlp_w1 = jax.random.normal(ks[3], (EMB, EMB), dtype=jnp.float32) * s_emb
        mlp_b1 = jnp.zeros((EMB,), dtype=jnp.float32)
        mlp_w2 = jax.random.normal(ks[4], (EMB, EMB), dtype=jnp.float32) * s_emb
        mlp_b2 = jnp.zeros((EMB,), dtype=jnp.float32)
        a = jax.random.normal(ks[5], (EMB, M), dtype=jnp.float32)
        q, _ = jnp.linalg.qr(a)
        w = q.T * jnp.sqrt(jnp.float32(M))
        return {'x': x, 'kqv_w': kqv_w, 'kqv_b': kqv_b, 'proj_w': proj_w, 'proj_b': proj_b, 'n1_g': n1_g, 'n1_b': n1_b, 'n2_g': n2_g, 'n2_b': n2_b, 'mlp_w1': mlp_w1, 'mlp_b1': mlp_b1, 'mlp_w2': mlp_w2, 'mlp_b2': mlp_b2, 'w': w}
    _L0_mix_all = _L0_mix_setup()
    _L0_mix_in = {k: v for k, v in _L0_mix_all.items() if k in ('kqv_w', 'kqv_b', 'proj_w', 'proj_b', 'n1_g', 'n1_b', 'n2_g', 'n2_b', 'mlp_w1', 'mlp_b1', 'mlp_w2', 'mlp_b2', 'w')}
    del _L0_mix_all

    def _L0_ffn_setup():
        import jax, jax.numpy as jnp
        import numpy as np

        def _haar_dwt2(x):
            a = x[:, ::2, ::2]
            b = x[:, ::2, 1::2]
            c = x[:, 1::2, ::2]
            d = x[:, 1::2, 1::2]
            ll = (a + b + c + d) * 0.5
            lh = (a + b - c - d) * 0.5
            hl = (a - b + c - d) * 0.5
            hh = (a - b - c + d) * 0.5
            return (ll, lh, hl, hh)

        def _haar_idwt2(ll, lh, hl, hh):
            a = (ll + lh + hl + hh) * 0.5
            b = (ll + lh - hl - hh) * 0.5
            c = (ll - lh + hl - hh) * 0.5
            d = (ll - lh - hl + hh) * 0.5
            B, H2, W2 = ll.shape
            out = jnp.zeros((B, 2 * H2, 2 * W2), ll.dtype)
            out = out.at[:, ::2, ::2].set(a)
            out = out.at[:, ::2, 1::2].set(b)
            out = out.at[:, 1::2, ::2].set(c)
            out = out.at[:, 1::2, 1::2].set(d)
            return out

        def _interp_linear_last(x, m):
            n = x.shape[-1]
            pos = jnp.linspace(0.0, 1.0, m, dtype=x.dtype) * (n - 1)
            i0 = jnp.clip(jnp.floor(pos).astype(jnp.int32), 0, n - 2)
            w = pos - i0.astype(x.dtype)
            return x[..., i0] * (1.0 - w) + x[..., i0 + 1] * w
        key = jax.random.key(seed)
        k0, k1, k2 = jax.random.split(key, 3)
        b, f, c, hidden = (128, 256, 512, 256)
        x = jax.random.normal(k0, (b, f, c), dtype=jnp.float32)
        fc1_w = jax.random.normal(k1, (hidden, c), dtype=jnp.float32) * 0.02
        fc1_b = jnp.zeros((hidden,), dtype=jnp.float32)
        fc2_w = jax.random.normal(k2, (c // 2, hidden), dtype=jnp.float32) * 0.02
        fc2_b = jnp.zeros((c // 2,), dtype=jnp.float32)
        return {'x': x, 'fc1_w': fc1_w, 'fc1_b': fc1_b, 'fc2_w': fc2_w, 'fc2_b': fc2_b}
    _L0_ffn_all = _L0_ffn_setup()
    _L0_ffn_in = {k: v for k, v in _L0_ffn_all.items() if k in ('fc1_w', 'fc1_b', 'fc2_w', 'fc2_b')}
    del _L0_ffn_all
    return {'x': x, 'src': src, 'dst': dst, 'L0_gnn_W1': _L0_gnn_in['W1'], 'L0_gnn_b1': _L0_gnn_in['b1'], 'L0_gnn_W2': _L0_gnn_in['W2'], 'L0_gnn_b2': _L0_gnn_in['b2'], 'L0_mix_kqv_w': _L0_mix_in['kqv_w'], 'L0_mix_kqv_b': _L0_mix_in['kqv_b'], 'L0_mix_proj_w': _L0_mix_in['proj_w'], 'L0_mix_proj_b': _L0_mix_in['proj_b'], 'L0_mix_n1_g': _L0_mix_in['n1_g'], 'L0_mix_n1_b': _L0_mix_in['n1_b'], 'L0_mix_n2_g': _L0_mix_in['n2_g'], 'L0_mix_n2_b': _L0_mix_in['n2_b'], 'L0_mix_mlp_w1': _L0_mix_in['mlp_w1'], 'L0_mix_mlp_b1': _L0_mix_in['mlp_b1'], 'L0_mix_mlp_w2': _L0_mix_in['mlp_w2'], 'L0_mix_mlp_b2': _L0_mix_in['mlp_b2'], 'L0_mix_w': _L0_mix_in['w'], 'L0_ffn_fc1_w': _L0_ffn_in['fc1_w'], 'L0_ffn_fc1_b': _L0_ffn_in['fc1_b'], 'L0_ffn_fc2_w': _L0_ffn_in['fc2_w'], 'L0_ffn_fc2_b': _L0_ffn_in['fc2_b']}

def reference(x, src, dst, L0_gnn_W1, L0_gnn_b1, L0_gnn_W2, L0_gnn_b2, L0_mix_kqv_w, L0_mix_kqv_b, L0_mix_proj_w, L0_mix_proj_b, L0_mix_n1_g, L0_mix_n1_b, L0_mix_n2_g, L0_mix_n2_b, L0_mix_mlp_w1, L0_mix_mlp_b1, L0_mix_mlp_w2, L0_mix_mlp_b2, L0_mix_w, L0_ffn_fc1_w, L0_ffn_fc1_b, L0_ffn_fc2_w, L0_ffn_fc2_b):
    import jax
    import jax.numpy as jnp

    def _L0_gnn_ref(x, edge_index, W1, b1, W2, b2):
        import jax, jax.numpy as jnp
        import numpy as np
        N = 6250
        E = 50000
        D_IN = 512
        D_HID = 256
        D_OUT = 512
        h = jax.nn.relu(x @ W1 + b1) @ W2 + b2
        row, col = (edge_index[0], edge_index[1])
        agg = jax.ops.segment_sum(h[col], row, num_segments=h.shape[0])
        return h + agg

    def _L0_mix_ref(x, kqv_w, kqv_b, proj_w, proj_b, n1_g, n1_b, n2_g, n2_b, mlp_w1, mlp_b1, mlp_w2, mlp_b2, w):
        import jax, jax.numpy as jnp
        import numpy as np
        B, T, DIM = (32, 392, 512)
        EMB = 512
        M = 256
        EPS_ATTN = 1e-08
        EPS_LN = 0.001

        def layernorm(x, g, b):
            mu = jnp.mean(x, axis=-1, keepdims=True)
            var = jnp.var(x, axis=-1, keepdims=True)
            return (x - mu) / jnp.sqrt(var + EPS_LN) * g + b

        def prm_exp(x, w):
            xd = jnp.sum(x * x, axis=-1, keepdims=True) / 2.0
            wtx = jnp.einsum('bti,mi->btm', x, w)
            return jnp.exp(wtx - xd) / jnp.sqrt(jnp.float32(M))
        h = layernorm(x, n1_g, n1_b)
        kqv = h @ kqv_w + kqv_b
        k, q, v = jnp.split(kqv, 3, axis=-1)
        kp = prm_exp(k, w)
        qp = prm_exp(q, w)
        D = jnp.einsum('btm,bm->bt', qp, jnp.sum(kp, axis=1))[..., None]
        kptv = jnp.einsum('btn,btm->bnm', v, kp)
        y = jnp.einsum('btm,bnm->btn', qp, kptv) / (D + EPS_ATTN)
        y = v + (y @ proj_w + proj_b)
        h2 = layernorm(y, n2_g, n2_b)
        h2 = jax.nn.gelu(h2 @ mlp_w1 + mlp_b1, approximate=False)
        h2 = h2 @ mlp_w2 + mlp_b2
        return y + h2

    def _L0_ffn_ref(x, fc1_w, fc1_b, fc2_w, fc2_b):
        import jax, jax.numpy as jnp
        import numpy as np

        def _haar_dwt2(x):
            a = x[:, ::2, ::2]
            b = x[:, ::2, 1::2]
            c = x[:, 1::2, ::2]
            d = x[:, 1::2, 1::2]
            ll = (a + b + c + d) * 0.5
            lh = (a + b - c - d) * 0.5
            hl = (a - b + c - d) * 0.5
            hh = (a - b - c + d) * 0.5
            return (ll, lh, hl, hh)

        def _haar_idwt2(ll, lh, hl, hh):
            a = (ll + lh + hl + hh) * 0.5
            b = (ll + lh - hl - hh) * 0.5
            c = (ll - lh + hl - hh) * 0.5
            d = (ll - lh - hl + hh) * 0.5
            B, H2, W2 = ll.shape
            out = jnp.zeros((B, 2 * H2, 2 * W2), ll.dtype)
            out = out.at[:, ::2, ::2].set(a)
            out = out.at[:, ::2, 1::2].set(b)
            out = out.at[:, 1::2, ::2].set(c)
            out = out.at[:, 1::2, 1::2].set(d)
            return out

        def _interp_linear_last(x, m):
            n = x.shape[-1]
            pos = jnp.linspace(0.0, 1.0, m, dtype=x.dtype) * (n - 1)
            i0 = jnp.clip(jnp.floor(pos).astype(jnp.int32), 0, n - 2)
            w = pos - i0.astype(x.dtype)
            return x[..., i0] * (1.0 - w) + x[..., i0 + 1] * w
        b, f, c = x.shape
        ll, lh, hl, hh = _haar_dwt2(x)
        ll_up = _interp_linear_last(ll, c)
        h = jax.nn.gelu(jnp.einsum('bfc,hc->bfh', ll_up, fc1_w) + fc1_b, approximate=False)
        ll_new = jnp.einsum('bfh,oh->bfo', h, fc2_w) + fc2_b
        return _haar_idwt2(ll_new, lh, hl, hh)
    edge_index = jnp.stack([src, dst])
    xn = _layernorm(x, axis=-1)
    x = x + _L0_gnn_ref(xn, edge_index, L0_gnn_W1, L0_gnn_b1, L0_gnn_W2, L0_gnn_b2) + _L0_mix_ref(xn[None], L0_mix_kqv_w, L0_mix_kqv_b, L0_mix_proj_w, L0_mix_proj_b, L0_mix_n1_g, L0_mix_n1_b, L0_mix_n2_g, L0_mix_n2_b, L0_mix_mlp_w1, L0_mix_mlp_b1, L0_mix_mlp_w2, L0_mix_mlp_b2, L0_mix_w)[0]
    x = x + _L0_ffn_ref(_layernorm(x, axis=-1)[None], L0_ffn_fc1_w, L0_ffn_fc1_b, L0_ffn_fc2_w, L0_ffn_fc2_b)[0]
    return x

_drawn_inputs = setup_inputs


def setup_inputs(seed=0):
    import zlib

    import numpy as np

    out = dict(_drawn_inputs(seed))
    spreads = {'L0_gnn_b1': (0.0, 0.1),
     'L0_gnn_b2': (0.0, 0.1),
     'L0_mix_kqv_b': (0.0, 0.494),
     'L0_mix_proj_b': (0.0, 0.524),
     'L0_mix_n1_g': (1.0, 0.536),
     'L0_mix_n1_b': (0.0, 0.532),
     'L0_mix_n2_g': (1.0, 0.6),
     'L0_mix_n2_b': (0.0, 0.8),
     'L0_mix_mlp_b1': (0.0, 0.8),
     'L0_mix_mlp_b2': (0.0, 0.613),
     'L0_ffn_fc1_b': (0.0, 0.8),
     'L0_ffn_fc2_b': (0.0, 0.8)}
    factors = {'L0_ffn_fc1_w': 8.0, 'L0_ffn_fc2_w': 8.0}
    for name, (base, spread) in spreads.items():
        noise = np.random.default_rng([zlib.crc32(name.encode()), seed]).standard_normal(out[name].shape)
        drawn = base * np.exp(spread * noise) if base else spread * noise
        out[name] = jnp.asarray(drawn.astype(out[name].dtype))
    for name, factor in factors.items():
        out[name] = (out[name] * factor).astype(out[name].dtype)
    return out
```

```python
from contextlib import ExitStack

import numpy as np
import concourse.bass as bass
from concourse import mybir

F32, F16, I32, U16 = mybir.dt.float32, mybir.dt.float16, mybir.dt.int32, mybir.dt.uint16
ALU, ACT = mybir.AluOpType, mybir.ActivationFunctionType

N, D, E = 6250, 512, 100000
P, NT = 125, 50
STEPS = NT // 2
HID, M, HL = 256, 256, 256
KC, KH = D // 128, HID // 128
RW = HID + 1
EC = E // P
EH = EC // 2
GROUPS = (E + NT * 127) // 128
SG = 20
GB = 11
BATCHES = 3
LAST = GROUPS - GB * BATCHES * STEPS
ROUND = 12582912.0
EPS1, EPS2, EPS_ATTN = 1e-5, 1e-3, 1e-8
assert 0 < LAST <= GB and EC % (2 * SG) == 0


class Step:

    def __init__(self, phase, j, s):
        self.phase, self.j, self.s = phase, j, s
        self.u = j * 2 + s
        self.g = self.u + 25 * phase

    def uses(self, s=None):
        s = self.s if s is None else s
        return self.j + (13 - s) * self.phase


def phase_steps(eng, phase, emit):
    with eng.Fori(0, STEPS // 2) as j:
        emit(Step(phase, j, 0), False)
        emit(Step(phase, j, 1), False)
    emit(Step(phase, STEPS // 2, 0), True)


def build_program(nc, d):
    ctx = ExitStack()
    with ctx:
        def sb(name, words, dt=F32):
            return ctx.enter_context(nc.sbuf_tensor("sb_" + name, [128, words], dt))

        def sem(name):
            return ctx.enter_context(nc.semaphore("s_" + name))

        events = {}

        def ev(name):
            if name not in events:
                events[name] = sem("ev_" + name)
            return events[name]

        ACC = sb("acc", NT * RW)
        KQV = sb("kqv", KC * 3 * D)
        LATE = sb("late", 8192)
        STEP = sb("step", 14300)
        EDGE = sb("edge", 2 * 800 + 800 + 6 * SG)
        CONST = sb("const", 8900)

        def carver(region):
            at = [0]

            def take(*shape, dt=F32):
                n = int(np.prod(shape))
                words = n if dt in (F32, I32) else (n + 1) // 2
                v = region[:, at[0]:at[0] + words]
                at[0] += (words + 7) // 8 * 8
                assert at[0] <= region.shape[1] + 7, (at[0], region.shape)
                if dt is not F32:
                    v = v.bitcast(dt)
                    if dt is F16:
                        v = v[:, 0:n]
                if len(shape) == 2:
                    v = v.rearrange("p (a b) -> p a b", b=shape[1])
                elif len(shape) == 3:
                    v = v.rearrange("p (a b c) -> p a b c", b=shape[1], c=shape[2])
                return v
            return take

        acc = ACC[:, :].rearrange("p (t f) -> p t f", f=RW)
        onehot_a = ACC[:, 0:32 * EC // 2].bitcast(F16).rearrange("p (b j) -> p b j", j=EC)
        kqv_w = KQV[:, :].rearrange("p (c n) -> p c n", c=KC)
        ring = KQV[:, 0:2 * GB * RW].rearrange("p (h k f) -> p h k f", k=GB, f=RW)
        late = carver(LATE)
        proj_w, mlp1_w, mlp2_w = late(KC, D), late(KC, D), late(KC, D)
        gnn2_w, fc1e, fc2_w = late(KH, D), late(2, HL), late(2, HL)
        onehot_b = LATE[:, 0:18 * EC // 2].bitcast(F16).rearrange("p (b j) -> p b j", j=EC)

        def onehot(b):
            return onehot_a[0:P, b] if b < 32 else onehot_b[0:P, b - 32]

        edge = carver(EDGE)
        slot_of, payload = edge(EC, dt=I32), edge(EC, 2, dt=I32)
        stage_slot, stage_pay = edge(2, SG, dt=I32), edge(2, 2 * SG, dt=I32)

        const = carver(CONST)
        ident = const(128)
        w_t, gnn1_w = const(KC, M), const(KC, HID)
        pmat = const(KH, D)
        b1_bc, bv_bc, bvp_bc, mb2_bc, b2_bc, fb2_bc = (
            const(HID), const(D), const(D), const(D), const(D), const(HL))
        ones = const(128)
        neg_half = const(1)
        eps_c = const(2)
        n1g, n1b, n2g, n2b = const(KC), const(KC), const(KC), const(KC)
        kqb, m1b, f1b = const(2 * KC), const(KC), const(2)
        iota_p = const(P)
        group_off = const(GROUPS, dt=I32)
        sum_x, nmean, ssq = const(NT), const(NT), const(NT)
        s1, s12, rs2, nm1, nm12, tmp_a, tmp_b = (const(NT) for _ in range(7))
        mv = const(NT, 2)
        stat6 = const(2, 6)
        less = const(P, dt=F16)
        strip = const(178, dt=F16)
        ones_h = const(2, dt=F16)
        upper = const(128)
        totals, n_groups, base, end_g = const(1), const(1), const(1), const(1)
        ks_bc = const(M)
        zero_row = const(512)
        mvs, tiny, pool_tiny = const(2, 2), const(1), const(2)
        nms = const(STEPS)

        s0 = carver(STEP)
        src_i, dst_i, src_f, blk_q, blk_h = (
            s0(EC, dt=I32), s0(EC, dt=I32), s0(EC), s0(EC), s0(EC, dt=F16))
        count, incl, first, first_h, pos = s0(EC), s0(EC), s0(EC), s0(EC, dt=F16), s0(EC)
        pick = s0(NT, P, dt=F16)
        iota_g, past = s0(GROUPS), s0(GROUPS, dt=F16)
        vb4 = s0(KC, 128)
        xs = KQV[:, 0:10 * D].rearrange("p (h i f) -> p h i f", h=2, i=5)
        s1_ = carver(STEP)
        x_in, hh = s1_(2, 2, D), s1_(2, 2, D)
        hT = s1_(2, KC, 2 * P)
        kT, sq, sqa, sqb = s1_(KC, 2 * P), s1_(KC, 2 * P), s1_(2, 2 * P), s1_(2 * P)
        kp, kps, rt = s1_(2, M), s1_(2, M), s1_(2, HID)
        nxd = s1_(2)
        qpn, qpT = s1_(2, M), s1_(KH, 2 * P)
        y_out = s1_(2, 2, D)
        den, rden = s1_(2), s1_(2)
        junk = s1_(2, M)
        hk, kptv = x_in[:, 0].rearrange("p a (b c) -> p (a b) c", c=M), x_in[:, 1].rearrange("p a (b c) -> p (a b) c", c=M)
        s3_ = carver(STEP)
        x3, y3, h3, hT3 = s3_(2, 2, D), s3_(2, 2, D), s3_(2, 2, D), s3_(2, KC, 2 * P)
        gT3, z3 = s3_(KC, 2 * P), s3_(2, 2, D)
        hit, idx, lane_f = s3_(2, GB, P), s3_(2, GB, 2, dt=I32), s3_(2, GB)
        s4_ = carver(STEP)
        z4, x4, accs, accT = s4_(2, 2, D), s4_(2, 2, D), s4_(2, 2, RW), s4_(2, KH, 2 * P)
        t4, ll, llT, gT4, xn4 = s4_(2, D), s4_(2, HL), s4_(2, P), s4_(2, P), s4_(D)
        dlt = s4_(2, HL)
        o4 = s4_(2, 2, D)
        quarter = s4_(2, HL)
        interp, fc1_t = s4_(KC, HL), s4_(KC, HL)

        bank = [ctx.enter_context(nc.psum_tensor(f"bank{i}", [128, 512], F32)) for i in range(8)]
        BA, BB, BC, BD, BE, BF, BG, BH = bank

        def rows(t):
            return t.rearrange("(p t) f -> p t f", t=NT)

        x_d, out_d = rows(d["x"]), rows(d["out"])
        table = nc.dram_tensor("hidden_rows", [N, RW], F32).ap()
        y_d = nc.dram_tensor("y_rows", [N, D], F32).ap()
        z_d = nc.dram_tensor("z_rows", [N, D], F32).ap()
        x1_d = nc.dram_tensor("x1_rows", [N, D], F32).ap()
        sorted_d = nc.dram_tensor("sorted_edges", [128 * GROUPS, 2], I32).ap()
        sorted_v = sorted_d.rearrange("(p g) e -> p g e", g=GROUPS)
        chunks = lambda t: t.rearrange("(c p) n -> p c n", p=128)
        col = lambda t: t.rearrange("(c p) -> p c", p=128)

        all_engines = sem("phase_end")
        pair = lambda name: [sem(name + "0"), sem(name + "1")]
        e_in, c_in, w_in, late_in, prefill = (sem(n) for n in (
            "edges_in", "sort_consts_in", "weights_in", "late_in", "blank_slots"))
        xs_in, x_ld, y_ld, z_ld, x1_ld = (pair(n) for n in (
            "stat_x_in", "x_in", "y_in", "z_in", "x1_in"))
        r_st, y_st, z_st, x1_st, o_st = (sem("r_stored"), *(pair(n) for n in (
            "y_stored", "z_stored", "x1_stored", "out_stored")))
        idx_in, scattered, gathered = (pair(n) for n in ("idx_in", "scattered", "gathered"))
        st_sum, st_mean, st_free = sem("stat_sums"), sem("stat_means"), sem("stat_x_used")
        rank_mm, rank_used, staged = sem("rank_products"), sem("ranks_used"), sem("scatter_staged")
        (h_rows, tr, h_t, feat, feat_c, sqs, xd, nx, wx, ex, r_mm, r_up, r_ok, kadd, hk_mm, qn, qt, qtc,
         y_mm, y_ok, zadd, z_ok, m_mm, hits, g_mm) = (sem(n) for n in (
            "h_rows", "h_transposed", "hT", "features", "features_copied", "square_sums", "xd", "xd_copied",
            "w_products", "exps", "r_products", "r_read", "r_rows", "kp_added", "hk_products", "q_scaled",
            "q_transposed", "qT", "y_products", "y_rows", "z_sums", "z_rows", "mlp2_products", "one_hots",
            "group_products"))
        g_add, lanes_read, ring_free = pair("group_added"), pair("lanes_read"), pair("ring_used")
        a_cp, a_mm = sem("acc_staged"), sem("w2_products")
        accs_tr, accs_deg, x1_ok = pair("acc_stage_transposed"), pair("degrees_used"), pair("x1_rows")
        xo, llr, ll_tr, ll_t, f1, gl, f2, dl, xu, o_ok = (sem(n) for n in (
            "odd_scaled", "ll_rows", "ll_transposed", "llT", "fc1", "gelu", "fc2", "delta", "x1_plus_xn",
            "out_rows"))

        block = ctx.enter_context(nc.Block())

        def phase_end(eng, n):
            eng.drain().then_inc(all_engines, 1)
            eng.wait_ge(all_engines, 4 * n)

        ev_fc = sem("fc_in")
        a_t_slot = pair("accT_slot")
        dve_self, pool_self = sem("dve_self"), sem("pool_self")

        @block.sync
        def _(sp):
            sp.dma_start(src_i[0:P], d["src"].rearrange("(p j) -> p j", p=P)).then_inc(e_in, 16)
            sp.dma_start(dst_i[0:P], d["dst"].rearrange("(p j) -> p j", p=P)).then_inc(e_in, 16)
            for t, s in ((less[0:P], "less"), (upper[:, :], "upper"), (pick[:, :, :], "pick"),
                         (iota_g[:, :], "iota_g"), (iota_p[:, :], "iota_p"), (ident[:, :], "ident")):
                sp.dma_start(t, d["c_" + s]).then_inc(c_in, 16)
            sp.dma_start(sorted_d.rearrange("(p g) e -> p (g e)", g=GROUPS),
                         d["c_blank"].partition_broadcast(128)).then_inc(prefill, 16)

            def stat_load(j, s):
                sp.wait_ge(st_free, j * 2 + s)
                sp.dma_start(xs[0:P, s], x_d[:, bass.ds(j * 10 + 5 * s, 5), :]).then_inc(xs_in[s], 16)
            with sp.Fori(0, 5) as j:
                stat_load(j, 0)
                stat_load(j, 1)
            sp.wait_ge(st_free, 10)
            for t, s in ((kqv_w, chunks(d["L0_mix_kqv_w"])), (w_t, chunks(d["w_t"])),
                         (gnn1_w, chunks(d["L0_gnn_W1"])), (n1g, col(d["L0_mix_n1_g"])),
                         (n1b, col(d["L0_mix_n1_b"])), (kqb, col(d["L0_mix_kqv_b"][0:2 * D])),
                         (b1_bc, d["L0_gnn_b1"].partition_broadcast(128)),
                         (bv_bc, d["L0_mix_kqv_b"][2 * D:3 * D].partition_broadcast(128)),
                         (bvp_bc, d["L0_mix_proj_b"].partition_broadcast(128)),
                         (mb2_bc, d["L0_mix_mlp_b2"].partition_broadcast(128)),
                         (b2_bc, d["L0_gnn_b2"].partition_broadcast(128)),
                         (fb2_bc, d["L0_ffn_fc2_b"].partition_broadcast(128)),
                         (n2g, col(d["L0_mix_n2_g"])), (n2b, col(d["L0_mix_n2_b"])),
                         (m1b, col(d["L0_mix_mlp_b1"])), (f1b, col(d["L0_ffn_fc1_b"]))):
                sp.dma_start(t[:], s, allow_slow_non_contiguous=True).then_inc(w_in, 16)
            phase_end(sp, 1)

            for t, s in ((proj_w, chunks(d["L0_mix_proj_w"])), (mlp1_w, chunks(d["L0_mix_mlp_w1"])),
                         (mlp2_w, chunks(d["L0_mix_mlp_w2"])), (gnn2_w, chunks(d["L0_gnn_W2"])),
                         (fc2_w, chunks(d["fc2_t"]))):
                sp.dma_start(t[:], s).then_inc(late_in, 16)

            def load_x(j, s):
                sp.dma_start(x_in[0:P, s], x_d[:, bass.ds(j * 4 + 2 * s, 2), :]).then_inc(x_ld[s], 16)

            def attention_io(phase, store):
                for s in (0, 1):
                    load_x(0, s)

                def step(t, more):
                    if more:
                        after = t.j + 1
                        sp.wait_ge(h_rows, t.g + 1)
                        load_x(after, t.s)
                    store(t)
                with sp.Fori(0, STEPS // 2 - 1) as j:
                    step(Step(phase, j, 0), True)
                    step(Step(phase, j, 1), True)
                step(Step(phase, STEPS // 2 - 1, 0), True)
                step(Step(phase, STEPS // 2 - 1, 1), False)
                step(Step(phase, STEPS // 2, 0), False)

            table_v = rows(table)

            def store_r(t):
                sp.wait_ge(r_ok, t.u + 1)
                sp.dma_start(table_v[:, bass.ds(t.u * 2, 2), :], acc[0:P, bass.ds(t.u * 2, 2), :]).then_inc(r_st, 16)
            attention_io(0, store_r)
            sp.wait_ge(r_st, 16 * STEPS)
            phase_end(sp, 2)

            def store_y(t):
                sp.wait_ge(y_ok, t.u + 1)
                sp.dma_start(rows(y_d)[:, bass.ds(t.u * 2, 2), :], y_out[0:P, t.s]).then_inc(y_st[t.s], 16)
            attention_io(1, store_y)
            sp.wait_ge(y_st[0], 16 * 13)
            sp.wait_ge(y_st[1], 16 * 12)
            phase_end(sp, 3)

            for s in (0, 1):
                sp.wait_ge(scattered[s], 16 * EC // 2)

            def load_xd(j, s):
                sp.dma_start(x3[0:P, s], x_d[:, bass.ds(j * 4 + 2 * s, 2), :]).then_inc(x_ld[s], 16)

            def load_yd(j, s):
                sp.dma_start(y3[0:P, s], rows(y_d)[:, bass.ds(j * 4 + 2 * s, 2), :]).then_inc(y_ld[s], 16)

            def load_idx(t, i, first_group, n):
                par, uses = i % 2, t.j * 3 + i // 2
                sp.wait_ge(gathered[par], uses * (16 * GB))
                sp.wait_ge(lanes_read[par], uses)
                sp.dma_start(idx[:, par, 0:n], sorted_v[:, bass.ds(first_group, n), :]).then_inc(idx_in[par], 16)

            def mlp_io(t, more, last=False):
                for k in range(BATCHES):
                    i = t.s * BATCHES + k
                    load_idx(t, i, t.j * (2 * BATCHES * GB) + i * GB, GB)
                if last:
                    load_idx(t, BATCHES, GROUPS - LAST, LAST)
                if more:
                    after = t.j + 1
                    sp.wait_ge(zadd, t.u + 1)
                    load_xd(after, t.s)
                    sp.wait_ge(h_rows, t.g + 1)
                    load_yd(after, t.s)
                sp.wait_ge(z_ok, t.u + 1)
                sp.dma_start(rows(z_d)[:, bass.ds(t.u * 2, 2), :], z3[0:P, t.s]).then_inc(z_st[t.s], 16)
            for s in (0, 1):
                load_xd(0, s)
                load_yd(0, s)
            with sp.Fori(0, STEPS // 2 - 1) as j:
                mlp_io(Step(2, j, 0), True)
                mlp_io(Step(2, j, 1), True)
            mlp_io(Step(2, STEPS // 2 - 1, 0), True)
            mlp_io(Step(2, STEPS // 2 - 1, 1), False)
            mlp_io(Step(2, STEPS // 2, 0), False, last=True)
            sp.wait_ge(z_st[0], 16 * 13)
            sp.wait_ge(z_st[1], 16 * 12)
            phase_end(sp, 4)

            def tail_io(src, src_v, sems, used, store):
                def load(j, s):
                    sp.dma_start(src[0:P, s], src_v[:, bass.ds(j * 4 + 2 * s, 2), :]).then_inc(sems[s], 16)
                load(0, 0)
                load(0, 1)

                def step(t, more):
                    if more:
                        after = t.j + 1
                        sp.wait_ge(*used(t))
                        load(after, t.s)
                    store(t)
                with sp.Fori(0, STEPS // 2 - 1) as j:
                    step(Step(0, j, 0), True)
                    step(Step(0, j, 1), True)
                step(Step(0, STEPS // 2 - 1, 0), True)
                step(Step(0, STEPS // 2 - 1, 1), False)
                step(Step(0, STEPS // 2, 0), False)

            def store_x1(t):
                sp.wait_ge(x1_ok[t.s], t.j + 1)
                sp.dma_start(rows(x1_d)[:, bass.ds(t.u * 2, 2), :], x4[0:P, t.s]).then_inc(x1_st[t.s], 16)
            sp.dma_start(interp, chunks(d["c_interp"])).then_inc(ev_fc, 16)
            sp.dma_start(fc1_t, chunks(d["fc1_t"])).then_inc(ev_fc, 16)
            tail_io(z4, rows(z_d), z_ld, lambda t: (x1_ok[t.s], t.j + 1), store_x1)
            sp.wait_ge(x1_st[0], 16 * 13)
            sp.wait_ge(x1_st[1], 16 * 12)
            phase_end(sp, 5)

            def store_out(t):
                sp.wait_ge(o_ok, t.u + 1)
                sp.dma_start(out_d[:, bass.ds(t.u * 2, 2), :], o4[0:P, t.s]).then_inc(o_st[t.s], 16)
            tail_io(z4, rows(x1_d), x1_ld, lambda t: (xu, t.u + 1), store_out)
            sp.wait_ge(o_st[0], 16 * 13)
            sp.wait_ge(o_st[1], 16 * 12)

        @block.gpsimd
        def _(pool):
            pool.wait_ge(ev("slots"), 1)
            pool.wait_ge(prefill, 16)

            def carry_waits(n):
                pool.wait_ge(pool_self, n + 1)
                pool.tensor_tensor(pool_tiny[0:1, 1:2], pool_tiny[0:1, 0:1], pool_tiny[0:1, 0:1],
                                   ALU.add).then_inc(pool_self, 1)

            pool.memset(pool_tiny[:, :], 0.0).then_inc(pool_self, 1)

            def scatter(j, s):
                pool.wait_ge(scattered[s], j * (16 * SG))
                c = (j * 2 + s) * SG
                pool.tensor_copy(stage_slot[0:P, s], slot_of[0:P, bass.ds(c, SG)]).then_inc(staged, 1)
                pool.tensor_copy(stage_pay[0:P, s], payload.rearrange("p j e -> p (j e)")[0:P, bass.ds(c * 2, 2 * SG)]).then_inc(staged, 1)
                pool.wait_ge(staged, (j * 2 + s) * 2 + 2)
                carry_waits(j * 2 + s)
                for k in range(SG):
                    pool.indirect_dma_start(
                        out=sorted_d, out_offset=bass.IndirectOffsetOnAxis(ap=stage_slot[0:P, s, k:k + 1], axis=0),
                        in_=stage_pay[0:P, s, 2 * k:2 * k + 2], in_offset=None).then_inc(scattered[s], 16)
            with pool.Fori(0, EC // SG // 2) as j:
                scatter(j, 0)
                scatter(j, 1)

            def gather(uses, par, n=GB):
                pool.wait_ge(idx_in[par], uses * 16 + 16)
                pool.wait_ge(ring_free[par], uses)
                carry_waits(uses * 2 + (EC // SG + par))
                for k in range(n):
                    pool.indirect_dma_start(
                        out=ring[:, par, k], out_offset=None, in_=table,
                        in_offset=bass.IndirectOffsetOnAxis(ap=idx[:, par, k, 0:1], axis=0)).then_inc(gathered[par], 16)
            pool.wait_ge(all_engines, 4 * 3)
            with pool.Fori(0, STEPS // 2 * BATCHES) as j:
                gather(j, 0)
                gather(j, 1)
            n = STEPS // 2 * BATCHES
            gather(n, 0)
            gather(n, 1)
            gather(n + 1, 0)
            gather(n + 1, 1, LAST)

            pool.wait_ge(all_engines, 4 * 4)

            def stage_acc(t, last):
                pool.wait_ge(accs_tr[t.s], t.j)
                pool.wait_ge(accs_deg[t.s], t.j)
                pool.tensor_copy(accs[0:P, t.s], acc[0:P, bass.ds(t.u * 2, 2), :]).then_inc(a_cp, 1)
            phase_steps(pool, 0, stage_acc)

        @block.tensor
        def _(pe):
            pe.wait_ge(ev("onehot"), 1)
            for b in range(NT):
                for h, bk in ((0, BA), (1, BB)):
                    last = pe.matmul(bk[:, 0:EH], strip[0:P, 49 - b:177 - b], onehot(b)[:, h * EH:(h + 1) * EH],
                                     start=b == 0, stop=b == NT - 1)
            last.then_inc(ev("pe_count"), 1)
            pe.wait_ge(c_in, 6 * 16)
            pe.wait_ge(ev("groups"), 1)
            pe.matmul(BC[:, 0:1], upper[:, :], n_groups[:, :], start=True, stop=True).then_inc(ev("pe_base"), 1)
            pe.wait_ge(ev("past"), 1)
            gh = GROUPS // 2
            pe.matmul(BD[0:1, 0:gh], ones_h[0:NT, 0:1], past[0:NT, 0:gh], start=True, stop=True)
            pe.matmul(BE[0:1, 0:gh], ones_h[0:NT, 0:1], past[0:NT, gh:GROUPS], start=True, stop=True).then_inc(
                ev("pe_tiles"), 1)
            pe.wait_ge(ev("first"), 1)
            for b in range(NT):
                for h in (0, 1):
                    bk = (BA, BB, BF, BG)[b % 2 * 2 + h]
                    if b >= 2:
                        pe.wait_ge(rank_used, 2 * (b - 2) + h + 1)
                    cols = slice(h * EH, (h + 1) * EH)
                    pe.matmul(bk[0:P, 0:EH], less[0:P, :], onehot(b)[:, cols], start=True, stop=False)
                    pe.matmul(bk[0:P, 0:EH], pick[:, b, :], first_h[:, cols], start=False, stop=True).then_inc(rank_mm, 1)
            pe.wait_ge(ev("bias_in"), 1)
            for c in range(2 * KC):
                for k in range(KC):
                    pe.matmul(BC[:, c:c + 1], kqv_w[:, k, c * 128:(c + 1) * 128], n1b[:, k:k + 1],
                              start=k == 0, stop=k == KC - 1)
            for k in range(KC):
                last = pe.matmul(BD[:, :], vb4[:, k, :], kqv_w[:, k, 2 * D:3 * D], start=k == 0, stop=k == KC - 1)
            last.then_inc(ev("pe_bias"), 1)
            phase_end(pe, 1)

            def transposes(t, rows_sb):
                pe.wait_ge(h_rows, t.g + 1)
                pe.wait_ge(h_t, t.g * 2)
                for bk, cs in ((BF, (0, 1)), (BG, (2, 3))):
                    for i, c in enumerate(cs):
                        for m in (0, 1):
                            last = pe.transpose(bk[:, i * 250 + m * P:i * 250 + m * P + P],
                                                rows_sb[0:P, t.s, m, c * 128:(c + 1) * 128], ident[0:P, 0:P])
                    last.then_inc(tr, 1)

            def next_step(t):
                return Step(t.phase, t.j, 1) if t.s == 0 else Step(t.phase, t.j + 1, 0)

            def features(t, w, off, rhs):
                for i, bk in ((0, BA), (1, BB)):
                    pe.wait_ge(h_t, t.g * 2 + 2)
                    pe.wait_ge(feat_c, t.g * 2 + i)
                    for c in (2 * i, 2 * i + 1):
                        for k in range(KC):
                            last = pe.matmul(bk[:, (c % 2) * 250:(c % 2) * 250 + 2 * P],
                                             w[:, k, off + c * 128:off + (c + 1) * 128], rhs[:, t.s, k, :],
                                             start=k == 0, stop=k == KC - 1)
                    last.then_inc(feat, 1)

            def w_products(t):
                pe.wait_ge(feat_c, t.g * 2 + 2)
                pe.wait_ge(ex, t.g * 2)
                for m in (0, 1):
                    for k in range(KC):
                        last = pe.matmul(BE[0:P, m * M:(m + 1) * M], kT[:, k, m * P:(m + 1) * P], w_t[:, k, :],
                                         start=k == 0, stop=k == KC - 1)
                last.then_inc(wx, 1)
                pe.wait_ge(sqs, t.g + 1)
                for m in (0, 1):
                    last = pe.matmul(BG[0:P, 508 + m:509 + m], sqb[:, m * P:(m + 1) * P], neg_half[:, 0:1],
                                     start=True, stop=True)
                last.then_inc(xd, 1)

            for bk in (BC, BD):
                pe.matmul(bk[:, :], zero_row[0:1, 0:128], zero_row[0:1, 0:512], start=True, stop=False)
            transposes(Step(0, 0, 0), hh)

            def r_product(t, m, bk):
                for k in range(KC):
                    last = pe.matmul(bk[0:P, 0:HID], hT[:, t.s, k, m * P:(m + 1) * P], gnn1_w[:, k, :],
                                     start=k == 0, stop=k == KC - 1)
                last.then_inc(r_mm, 1)

            def phase1(t, last):
                pe.wait_ge(r_up, t.u * 2)
                features(t, kqv_w, 0, hT)
                r_product(t, 0, BH)
                w_products(t)
                r_product(t, 1, BA)
                if not last:
                    pe.wait_ge(nx, t.g + 1)
                    transposes(next_step(t), hh)
                pe.wait_ge(ex, t.g * 2 + 2)
                for k in range(KC):
                    for m in (0, 1):
                        mm = pe.matmul((BC, BD)[k // 2][:, (k % 2) * M:(k % 2 + 1) * M],
                                       hh[0:P, t.s, m, k * 128:(k + 1) * 128], kp[0:P, m, :],
                                       start=False, stop=False)
                mm.then_inc(hk_mm, 1)
            phase_steps(pe, 0, phase1)
            for bk in (BC, BD):
                mm = pe.matmul(bk[:, :], zero_row[0:1, 0:128], zero_row[0:1, 0:512], start=False, stop=True)
            mm.then_inc(ev("pe_hk"), 1)
            pe.wait_ge(kadd, STEPS)
            for m in (0, 1):
                mm = pe.matmul(BE[:, 0:M], ones[0:P, :], kps[0:P, m, :], start=m == 0, stop=m == 1)
            mm.then_inc(ev("pe_ksum"), 1)
            pe.wait_ge(ev("hk"), 1)
            for c in range(KC):
                bk = (BA, BB)[c // 2][:, (c % 2) * M:(c % 2 + 1) * M]
                for k in range(KC):
                    pe.matmul(bk, kqv_w[:, k, 2 * D + c * 128:2 * D + (c + 1) * 128], hk[:, k, :],
                              start=k == 0, stop=False)
                mm = pe.matmul(bk, bv_bc[0:1, c * 128:(c + 1) * 128], ks_bc[0:1, :], start=False, stop=True)
            mm.then_inc(ev("pe_kptv"), 1)
            pe.wait_ge(ev("kptv"), 1)
            pe.wait_ge(late_in, 5 * 16)
            for m in range(KH):
                for c in range(KC):
                    mm = pe.matmul((BF, BH)[m][:, :], kptv[:, c, m * 128:(m + 1) * 128], proj_w[:, c, :],
                                   start=c == 0, stop=c == KC - 1)
            mm.then_inc(ev("pe_pmat"), 1)
            for c in range(KC):
                for k in range(KC):
                    mm = pe.matmul(BG[:, c:c + 1], mlp1_w[:, k, c * 128:(c + 1) * 128], n2b[:, k:k + 1],
                                   start=k == 0, stop=k == KC - 1)
            mm.then_inc(ev("pe_mbias"), 1)
            phase_end(pe, 2)

            transposes(Step(1, 0, 0), hh)

            def v_product(t, m, bk):
                for k in range(KC):
                    pe.matmul(bk[0:P, :], hT[:, t.s, k, m * P:(m + 1) * P], kqv_w[:, k, 2 * D:3 * D],
                              start=k == 0, stop=False)

            def phase2(t, last):
                features(t, kqv_w, D, hT)
                pe.wait_ge(y_ok, t.u)
                v_product(t, 0, BC)
                w_products(t)
                v_product(t, 1, BD)
                pe.wait_ge(qn, t.u + 1)
                pe.wait_ge(qtc, t.u)
                for c in range(KH):
                    for m in (0, 1):
                        mm = pe.transpose(BH[:, c * 250 + m * P:c * 250 + (m + 1) * P],
                                          qpn[0:P, m, c * 128:(c + 1) * 128], ident[0:P, 0:P])
                mm.then_inc(qt, 1)
                if not last:
                    pe.wait_ge(nx, t.g + 1)
                    transposes(next_step(t), hh)
                pe.wait_ge(qtc, t.u + 1)
                for m, bk in ((0, BC), (1, BD)):
                    for c in range(KH):
                        mm = pe.matmul(bk[0:P, :], qpT[:, c, m * P:(m + 1) * P], pmat[:, c, :],
                                       start=False, stop=c == KH - 1)
                mm.then_inc(y_mm, 1)
            phase_steps(pe, 1, phase2)
            phase_end(pe, 3)

            transposes(Step(2, 0, 0), h3)

            def groups(t, k, n=GB):
                i = t.s * BATCHES + k
                par, uses = i % 2, t.j * 3 + i // 2
                pe.wait_ge(hits, t.j * (2 * BATCHES) + i + 1)
                pe.wait_ge(gathered[par], uses * (16 * GB) + 16 * n)
                for g in range(n):
                    at = i * GB + g
                    pe.wait_ge(g_add[at % 2], t.j * (BATCHES * GB) + at // 2)
                    mm = pe.matmul((BE, BH)[at % 2][0:P, 0:RW], hit[:, par, g, :], ring[:, par, g, :],
                                   start=True, stop=True)
                    mm.then_inc(g_mm, 1)
                pe.drain().then_inc(ring_free[par], 1)

            def phase3(t, last):
                features(t, mlp1_w, 0, hT3)
                groups(t, 0)
                pe.wait_ge(feat_c, t.g * 2 + 2)
                pe.wait_ge(z_ok, t.u)
                for m, bk in ((0, BC), (1, BD)):
                    for k in range(KC):
                        mm = pe.matmul(bk[0:P, :], gT3[:, k, m * P:(m + 1) * P], mlp2_w[:, k, :],
                                       start=k == 0, stop=k == KC - 1)
                mm.then_inc(m_mm, 1)
                groups(t, 1)
                if not last:
                    transposes(next_step(t), h3)
                groups(t, 2)
                if last:
                    groups(t, 3, LAST)
            phase_steps(pe, 2, phase3)
            phase_end(pe, 4)

            pe.wait_ge(ev_fc, 32)
            for i in range(2):
                for k in range(KC):
                    mm = pe.matmul(BE[:, i * HL:(i + 1) * HL], interp[:, k, i * 128:(i + 1) * 128], fc1_t[:, k, :],
                                   start=k == 0, stop=k == KC - 1)
            mm.then_inc(ev("pe_fc1"), 1)

            def acc_transposes(t):
                bk = (BF, BG)[t.s]
                pe.wait_ge(a_cp, t.u + 1)
                pe.wait_ge(a_t_slot[t.s], t.j)
                for c in range(KH):
                    for m in (0, 1):
                        mm = pe.transpose(bk[:, c * 250 + m * P:c * 250 + (m + 1) * P],
                                          accs[0:P, t.s, m, c * 128:(c + 1) * 128], ident[0:P, 0:P])
                mm.then_inc(accs_tr[t.s], 1)

            def phase4(t, last):
                if not last:
                    acc_transposes(next_step(t))
                pe.wait_ge(a_t_slot[t.s], t.j + 1)
                pe.wait_ge(x1_ok[t.s], t.j)
                for m in (0, 1):
                    bk = ((BC, BD), (BA, BB))[t.s][m]
                    for c in range(KH):
                        mm = pe.matmul(bk[0:P, :], accT[:, t.s, c, m * P:(m + 1) * P], gnn2_w[:, c, :],
                                       start=c == 0, stop=c == KH - 1)
                mm.then_inc(a_mm, 1)
            acc_transposes(Step(0, 0, 0))
            phase_steps(pe, 0, phase4)
            phase_end(pe, 5)

            def ll_transposes(t):
                pe.wait_ge(llr, t.u + 1)
                pe.wait_ge(ll_t, t.u)
                for c in (0, 1):
                    mm = pe.transpose(BF[:, c * P:(c + 1) * P], ll[0:P, t.s, c * 128:(c + 1) * 128], ident[0:P, 0:P])
                mm.then_inc(ll_tr, 1)

            def phase5(t, last):
                pe.wait_ge(ll_t, t.u + 1)
                pe.wait_ge(gl, t.u)
                for h in (0, 1):
                    for i in (0, 1):
                        mm = pe.matmul(BH[:, h * P:(h + 1) * P], fc1e[:, i, h * 128:(h + 1) * 128], llT[:, i, :],
                                       start=i == 0, stop=i == 1)
                mm.then_inc(f1, 1)
                if not last:
                    ll_transposes(next_step(t))
                pe.wait_ge(gl, t.u + 1)
                pe.wait_ge(dl, t.u)
                for c in (0, 1):
                    mm = pe.matmul(BC[0:P, 0:HL], gT4[:, c, :], fc2_w[:, c, :], start=c == 0, stop=c == 1)
                mm.then_inc(f2, 1)
            ll_transposes(Step(0, 0, 0))
            phase_steps(pe, 0, phase5)

        @block.scalar
        def _(act):
            act.wait_ge(ev("consts"), 1)

            def stats(j, s):
                act.wait_ge(xs_in[s], j * 16 + 16)
                c = j * 10 + 5 * s
                for i in range(5):
                    act.activation(xs[0:P, s, i], xs[0:P, s, i], ACT.Copy,
                                   accum_out=sum_x[0:P, bass.ds(c + i, 1)]).then_inc(st_sum, 1)
                act.wait_ge(st_sum, (c + 5))
                act.activation(nmean[0:P, bass.ds(c, 5)], sum_x[0:P, bass.ds(c, 5)], ACT.Copy,
                               scale=-1.0 / D).then_inc(st_mean, 1)
                act.wait_ge(st_mean, j * 2 + s + 1)
                for i in range(5):
                    last = act.activation(xs[0:P, s, i], xs[0:P, s, i], ACT.Square, bias=nmean[0:P, bass.ds(c + i, 1)],
                                          accum_out=ssq[0:P, bass.ds(c + i, 1)])
                last.then_inc(st_free, 1)
            with act.Fori(0, 5) as j:
                stats(j, 0)
                stats(j, 1)
            act.wait_ge(st_free, 10)
            act.activation(tmp_a[0:P, :], ssq[0:P, :], ACT.Sqrt, scale=1.0 / D, bias=eps_c[0:P, 0:1]).then_inc(ev("a_s1"), 1)
            act.wait_ge(ev("v_var2"), 1)
            act.activation(rs2[0:P, :], tmp_b[0:P, :], ACT.Sqrt, bias=eps_c[0:P, 1:2]).then_inc(ev("a_s2"), 1)
            phase_end(act, 1)

            def copy_hT(t, dst):
                for i, bk in ((0, BF), (1, BG)):
                    act.wait_ge(tr, t.g * 2 + i + 1)
                    act.copy(dst[:, t.s, 2 * i:2 * i + 2, :].rearrange("p a b -> p (a b)"), bk[:, 0:500]).then_inc(h_t, 1)

            def copy_features(t, biases, off):
                act.wait_ge(wx, t.g)
                act.wait_ge(sqs, t.g)
                for i, bk in ((0, BA), (1, BB)):
                    act.wait_ge(feat, t.g * 2 + i + 1)
                    for c in (2 * i, 2 * i + 1):
                        last = act.activation(kT[:, c, :], bk[:, (c % 2) * 250:(c % 2) * 250 + 250], ACT.Identity,
                                              bias=biases[:, off + c:off + c + 1])
                    last.then_inc(feat_c, 1)

            def exps(t, used):
                act.wait_ge(wx, t.g + 1)
                act.wait_ge(xd, t.g + 1)
                act.copy(nxd[0:P, :], BG[0:P, 508:510]).then_inc(nx, 1)
                act.wait_ge(nx, t.g + 1)
                used(t)
                for m in (0, 1):
                    act.activation(kp[0:P, m], BE[0:P, m * M:(m + 1) * M], ACT.Exp, bias=nxd[0:P, m:m + 1]).then_inc(ex, 1)

            def next_step(t):
                return Step(t.phase, t.j, 1) if t.s == 0 else Step(t.phase, t.j + 1, 0)

            copy_hT(Step(0, 0, 0), hT)

            def phase1(t, last):
                copy_features(t, kqb, 0)

                def used(t):
                    act.wait_ge(hk_mm, t.u)
                    act.wait_ge(kadd, t.u)
                exps(t, used)
                if not last:
                    copy_hT(next_step(t), hT)
            phase_steps(act, 0, phase1)
            phase_end(act, 2)

            copy_hT(Step(1, 0, 0), hT)

            def phase2(t, last):
                copy_features(t, kqb, KC)
                exps(t, lambda t: act.wait_ge(qn, t.u))
                act.wait_ge(qt, t.u + 1)
                act.wait_ge(y_mm, t.u)
                act.copy(qpT.rearrange("p a b -> p (a b)"), BH[:, 0:500]).then_inc(qtc, 1)
                if not last:
                    copy_hT(next_step(t), hT)
            phase_steps(act, 1, phase2)
            phase_end(act, 3)

            act.activation(tmp_a[0:P, :], mv[0:P, :, 1], ACT.Sqrt, bias=eps_c[0:P, 1:2]).then_inc(ev("a_s3"), 1)
            act.wait_ge(ev("v_s3"), 1)

            def norm_rows(t):
                act.wait_ge(y_ld[t.s], t.j * 16 + 16)
                act.wait_ge(tr, t.g * 2 - 2)
                for m in (0, 1):
                    last = act.activation(h3[0:P, t.s, m], y3[0:P, t.s, m], ACT.Identity,
                                          scale=s12[0:P, bass.ds(t.u * 2 + m, 1)], bias=nm12[0:P, bass.ds(t.u * 2 + m, 1)])
                last.then_inc(h_rows, 1)
            norm_rows(Step(2, 0, 0))
            copy_hT(Step(2, 0, 0), hT3)

            def phase3(t, last):
                if not last:
                    norm_rows(next_step(t))
                act.wait_ge(m_mm, t.u)
                for i, bk in ((0, BA), (1, BB)):
                    act.wait_ge(feat, t.g * 2 + i + 1)
                    for c in (2 * i, 2 * i + 1):
                        mm = act.activation(gT3[:, c, :], bk[:, (c % 2) * 250:(c % 2) * 250 + 250], ACT.Gelu,
                                            bias=m1b[:, c:c + 1])
                    mm.then_inc(feat_c, 1)
                if not last:
                    copy_hT(next_step(t), hT3)
            phase_steps(act, 2, phase3)
            phase_end(act, 4)

            act.wait_ge(ev("pe_fc1"), 1)
            act.activation(fc1e.rearrange("p a b -> p (a b)"), BE[:, :], ACT.Copy, scale=0.5).then_inc(ev("a_fc1"), 1)

            def copy_accT(t):
                act.wait_ge(accs_tr[t.s], t.j + 1)
                act.copy(accT[:, t.s].rearrange("p a b -> p (a b)"), (BF, BG)[t.s][:, 0:500]).then_inc(a_t_slot[t.s], 1)
            copy_accT(Step(0, 0, 0))

            def phase4(t, last):
                if not last:
                    act.wait_ge(a_mm, t.u)
                    copy_accT(next_step(t))
            phase_steps(act, 0, phase4)
            phase_end(act, 5)

            act.activation(tmp_a[0:P, :], mv[0:P, :, 1], ACT.Sqrt, bias=eps_c[0:P, 0:1]).then_inc(ev("a_s4"), 1)
            act.wait_ge(ev("v_s4"), 1)

            def odd(t):
                act.wait_ge(x1_ld[t.s], t.j * 16 + 16)
                act.wait_ge(llr, t.u)
                act.activation(xn4[0:P], z4[0:P, t.s, 1], ACT.Identity,
                               scale=s12[0:P, bass.ds(t.u * 2 + 1, 1)], bias=nms[0:P, bass.ds(t.u, 1)]).then_inc(xo, 1)

            def copy_llT(t):
                act.wait_ge(ll_tr, t.u + 1)
                act.wait_ge(f1, t.u)
                act.copy(llT.rearrange("p a b -> p (a b)"), BF[:, 0:2 * P]).then_inc(ll_t, 1)
            odd(Step(0, 0, 0))
            copy_llT(Step(0, 0, 0))

            def phase5(t, last):
                if not last:
                    odd(next_step(t))
                act.wait_ge(f1, t.u + 1)
                act.wait_ge(f2, t.u)
                for h in (0, 1):
                    mm = act.activation(gT4[:, h, :], BH[:, h * P:(h + 1) * P], ACT.Gelu, bias=f1b[:, h:h + 1])
                mm.then_inc(gl, 1)
                if not last:
                    copy_llT(next_step(t))
                act.wait_ge(o_st[t.s], t.j * 16)
                for m in (0, 1):
                    mm = act.activation(o4[0:P, t.s, m], z4[0:P, t.s, m], ACT.Identity,
                                        scale=s1[0:P, bass.ds(t.u * 2 + m, 1)], bias=nm12[0:P, bass.ds(t.u * 2 + m, 1)])
                mm.then_inc(xu, 1)
            phase_steps(act, 0, phase5)

        @block.vector
        def _(dve):
            n_self = [0]

            def seq(inst):
                n_self[0] += 1
                inst.then_inc(dve_self, 1)
                dve.wait_ge(dve_self, n_self[0])

            def ts(out, in0, a, op0, b=None, op1=ALU.bypass):
                seq(dve.tensor_scalar(out, in0, a, b, op0, op1))

            dve.memset(ones[:, :], 1.0)
            dve.memset(ones_h[:, :], 1.0)
            dve.memset(neg_half[:, :], -0.5)
            dve.memset(zero_row[:, :], 0.0)
            dve.memset(eps_c[:, 0:1], EPS1)
            seq(dve.memset(eps_c[:, 1:2], EPS2))
            seq(dve.memset(strip[0:P, :], 0.0))
            seq(dve.memset(strip[0:P, 49:50], 1.0))
            seq(dve.memset(strip[0:P, 113:114], 1.0))
            dve.drain().then_inc(ev("consts"), 1)
            dve.wait_ge(e_in, 32)
            seq(dve.tensor_copy(src_f[0:P], src_i[0:P]))
            ts(blk_q[0:P], src_f[0:P], 1.0 / NT, ALU.mult, -0.49, ALU.add)
            ts(blk_q[0:P], blk_q[0:P], ROUND, ALU.add, ROUND, ALU.subtract)
            seq(dve.scalar_tensor_tensor(out=blk_h[0:P], in0=blk_q[0:P], scalar=-float(NT), in1=src_f[0:P],
                                         op0=ALU.mult, op1=ALU.add))
            for b in range(NT):
                last = dve.tensor_scalar(onehot(b), blk_h[0:P], float(b), None, ALU.is_equal)
            last.then_inc(ev("onehot"), 1)
            dve.tensor_copy(payload[0:P, :, 0], dst_i[0:P])
            dve.tensor_copy(payload[0:P, :, 1], blk_q[0:P])
            dve.wait_ge(ev("pe_count"), 1)
            dve.tensor_copy(count[:, 0:EH], BA[:, 0:EH])
            seq(dve.tensor_copy(count[:, EH:EC], BB[:, 0:EH]))
            seq(dve.tensor_tensor_scan(incl[:, :], count[:, :], count[:, :], 0.0, ALU.add, ALU.max))
            ts(n_groups[:, :], incl[:, EC - 1:EC], 1.0 / 128, ALU.mult, 127.0 / 128 - 0.5 + 1.0 / 256, ALU.add)
            ts(n_groups[:, :], n_groups[:, :], ROUND, ALU.add, ROUND, ALU.subtract)
            dve.drain().then_inc(ev("groups"), 1)
            dve.wait_ge(ev("pe_base"), 1)
            seq(dve.tensor_copy(base[:, :], BC[:, 0:1]))
            seq(dve.tensor_tensor(end_g[:, :], base[:, :], n_groups[:, :], ALU.add))
            dve.wait_ge(c_in, 6 * 16)
            dve.tensor_scalar(past[:, :], iota_g[:, :], end_g[:, 0:1], None, ALU.is_ge).then_inc(ev("past"), 1)
            seq(dve.tensor_tensor(first[:, :], incl[:, :], count[:, :], ALU.subtract))
            ts(base[:, :], base[:, :], 128.0, ALU.mult)
            ts(first[:, :], first[:, :], base[:, 0:1], ALU.add)
            ts(count[:, :], first[:, :], 1.0 / 128, ALU.mult, -0.5 + 1.0 / 256, ALU.add)
            ts(count[:, :], count[:, :], ROUND, ALU.add, ROUND, ALU.subtract)
            dve.tensor_copy(first_h[0:64], count[0:64])
            seq(dve.scalar_tensor_tensor(out=first_h[64:128], in0=count[64:128], scalar=-128.0, in1=first[64:128],
                                         op0=ALU.mult, op1=ALU.add))
            dve.drain().then_inc(ev("first"), 1)
            dve.wait_ge(ev("pe_tiles"), 1)
            gh = GROUPS // 2
            for h, bk in ((0, BD), (1, BE)):
                last = dve.tensor_scalar(group_off[0:1, h * gh:(h + 1) * gh], bk[0:1, 0:gh], float(NT - 1), float(RW),
                                         ALU.min, ALU.mult)
            last.then_inc(ev("offsets"), 1)
            for b in range(NT):
                for h in (0, 1):
                    bk = (BA, BB, BF, BG)[b % 2 * 2 + h]
                    cols = slice(h * EH, (h + 1) * EH)
                    if b:
                        dve.wait_ge(rank_used, 2 * b + h - 1)
                    dve.wait_ge(rank_mm, 2 * b + h + 1)
                    dve.copy_predicated(pos[0:P, cols], onehot(b)[:, cols].bitcast(U16), bk[0:P, 0:EH]).then_inc(rank_used, 1)
            dve.wait_ge(rank_used, 2 * NT)
            ts(src_f[0:P], pos[0:P], 1.0 / 128, ALU.mult, -0.5 + 1.0 / 256, ALU.add)
            ts(src_f[0:P], src_f[0:P], ROUND, ALU.add, ROUND, ALU.subtract)
            seq(dve.scalar_tensor_tensor(out=pos[0:P], in0=src_f[0:P], scalar=-128.0, in1=pos[0:P],
                                         op0=ALU.mult, op1=ALU.add))
            seq(dve.scalar_tensor_tensor(out=slot_of[0:P], in0=pos[0:P], scalar=float(GROUPS), in1=src_f[0:P],
                                         op0=ALU.mult, op1=ALU.add))
            dve.drain().then_inc(ev("slots"), 1)

            dve.wait_ge(w_in, 16 * 16)
            for k in range(KC):
                dve.tensor_copy(vb4[:, k, :], n1b[:, k:k + 1].to_broadcast([128, 128]))
            dve.drain().then_inc(ev("bias_in"), 1)
            dve.wait_ge(ev("pe_bias"), 1)
            dve.tensor_tensor(kqb[:, :], kqb[:, :], BC[:, 0:2 * KC], ALU.add)
            seq(dve.tensor_tensor(bv_bc[:, :], bv_bc[:, :], BD[:, :], ALU.add))
            dve.tensor_tensor(bvp_bc[:, :], bvp_bc[:, :], bv_bc[:, :], ALU.add)
            for k in range(KC):
                dve.tensor_scalar(kqv_w[:, k, :], kqv_w[:, k, :], n1g[:, k:k + 1], None, ALU.mult)
            dve.memset(acc[0:P, :, HID:RW], 1.0)
            dve.wait_ge(ev("a_s1"), 1)
            seq(dve.reciprocal(s1[0:P, :], tmp_a[0:P, :]))
            ts(tmp_b[0:P, :], ssq[0:P, :], 1.0 / D, ALU.mult)
            seq(dve.tensor_tensor(tmp_b[0:P, :], tmp_b[0:P, :], s1[0:P, :], ALU.mult))
            seq(dve.tensor_tensor(tmp_b[0:P, :], tmp_b[0:P, :], s1[0:P, :], ALU.mult))
            dve.drain().then_inc(ev("v_var2"), 1)
            dve.wait_ge(ev("a_s2"), 1)
            seq(dve.reciprocal(s12[0:P, :], rs2[0:P, :]))
            seq(dve.tensor_tensor(s12[0:P, :], s12[0:P, :], s1[0:P, :], ALU.mult))
            seq(dve.tensor_tensor(nm12[0:P, :], nmean[0:P, :], s12[0:P, :], ALU.mult))
            phase_end(dve, 1)

            class Chain:

                def __init__(self, name, per):
                    self.sem, self.per = sem(name), per

                def start(self, t):
                    self.t, self.n = t, 0

                def __call__(self, inst):
                    self.n += 1
                    inst.then_inc(self.sem, 1)

                def wait(self):
                    dve.wait_ge(self.sem, self.t.u * self.per + self.n)

            def next_step(t):
                return Step(t.phase, t.j, 1) if t.s == 0 else Step(t.phase, t.j + 1, 0)

            def norm_rows(t):
                dve.wait_ge(x_ld[t.s], t.uses() * 16 + 16)
                for m in (0, 1):
                    last = dve.tensor_scalar(hh[0:P, t.s, m], x_in[0:P, t.s, m], s12[0:P, bass.ds(t.u * 2 + m, 1)],
                                             nm12[0:P, bass.ds(t.u * 2 + m, 1)], ALU.mult, ALU.add)
                last.then_inc(h_rows, 1)

            def square_sums(t, own):
                dve.wait_ge(feat_c, t.g * 2 + 2)
                flat = lambda v: v.rearrange("p a b -> p (a b)")
                own(dve.tensor_tensor(flat(sq), flat(kT), flat(kT), ALU.mult))
                own.wait()
                own(dve.tensor_tensor(flat(sqa), flat(sq[:, 0:2]), flat(sq[:, 2:4]), ALU.add))
                own.wait()
                dve.wait_ge(xd, t.g)
                dve.tensor_tensor(sqb[:, :], sqa[:, 0], sqa[:, 1], ALU.add).then_inc(sqs, 1)

            own1 = Chain("dve_own1", 2)
            dve.memset(kps[0:P], 0.0)
            norm_rows(Step(0, 0, 0))

            def phase1(t, last):
                own1.start(t)
                if not last:
                    dve.wait_ge(hk_mm, t.u)
                    norm_rows(next_step(t))
                square_sums(t, own1)
                for m, bk in ((0, BH), (1, BA)):
                    dve.wait_ge(r_mm, t.u * 2 + m + 1)
                    dve.scalar_tensor_tensor(out=rt[0:P, m], in0=bk[0:P, 0:HID], scalar=rs2[0:P, bass.ds(t.u * 2 + m, 1)],
                                             in1=b1_bc[0:P, :], op0=ALU.mult, op1=ALU.add).then_inc(r_up, 1)
                dve.wait_ge(r_up, t.u * 2 + 2)
                dve.tensor_scalar(acc[0:P, bass.ds(t.u * 2, 2), 0:HID], rt[0:P], 0.0, None, ALU.max).then_inc(r_ok, 1)
                dve.wait_ge(ex, t.g * 2 + 2)
                dve.wait_ge(kadd, t.u)
                dve.tensor_tensor(kps[0:P], kps[0:P], kp[0:P], ALU.add).then_inc(kadd, 1)
            phase_steps(dve, 0, phase1)

            dve.wait_ge(ev("pe_ksum"), 1)
            for i, bk in ((0, BC), (1, BD)):
                dve.tensor_copy(hk[:, 2 * i:2 * i + 2, :].rearrange("p a b -> p (a b)"), bk[:, :])
            dve.tensor_copy(ks_bc[:, :], BE[:, 0:M])
            dve.drain().then_inc(ev("hk"), 1)
            dve.wait_ge(ev("pe_kptv"), 1)
            for i, bk in ((0, BA), (1, BB)):
                dve.tensor_copy(kptv[:, 2 * i:2 * i + 2, :].rearrange("p a b -> p (a b)"), bk[:, :])
            dve.drain().then_inc(ev("kptv"), 1)
            dve.wait_ge(ev("pe_pmat"), 1)
            for m, bk in ((0, BF), (1, BH)):
                dve.tensor_copy(pmat[:, m, :], bk[:, :])
            dve.wait_ge(ev("pe_mbias"), 1)
            dve.tensor_tensor(m1b[:, :], m1b[:, :], BG[:, 0:KC], ALU.add)
            for k in range(KC):
                dve.tensor_scalar(mlp1_w[:, k, :], mlp1_w[:, k, :], n2g[:, k:k + 1], None, ALU.mult)
            phase_end(dve, 2)

            def row_stats(rows_sb, t, own):
                for m in (0, 1):
                    own(dve.bn_stats(stat6[0:P, m, :], rows_sb[:, m, :]))
                own.wait()
                own(dve.tensor_scalar(tiny[0:1, 0:1], stat6[0:1, 0, 0:1], 1.0, None, ALU.mult))
                for m in (0, 1):
                    own(dve.bn_aggr(mvs[0:P, m, :], stat6[0:P, m, :]))
                own.wait()
                return dve.tensor_copy(mv[0:P, bass.ds(t.u * 2, 2), :], mvs[0:P])

            own2 = Chain("dve_own2", 13)
            norm_rows(Step(1, 0, 0))

            def phase2(t, last):
                own2.start(t)
                if not last:
                    dve.wait_ge(tr, t.g * 2)
                    norm_rows(next_step(t))
                square_sums(t, own2)
                for m in (0, 1):
                    dve.wait_ge(ex, t.g * 2 + m + 1)
                    own2(dve.scalar_tensor_tensor(out=junk[0:P, m], in0=kp[0:P, m], scalar=1.0, in1=ks_bc[0:P, :],
                                                  op0=ALU.mult, op1=ALU.mult, accum_out=den[0:P, m:m + 1]))
                own2.wait()
                own2(dve.tensor_scalar(den[0:P, :], den[0:P, :], 256.0 * EPS_ATTN, None, ALU.add))
                own2.wait()
                own2(dve.reciprocal(rden[0:P, :], den[0:P, :]))
                own2.wait()
                dve.wait_ge(qt, t.u)
                for m in (0, 1):
                    mm = dve.tensor_scalar(qpn[0:P, m], kp[0:P, m], rden[0:P, m:m + 1], None, ALU.mult)
                mm.then_inc(qn, 1)
                dve.wait_ge(y_mm, t.u + 1)
                dve.wait_ge(y_st[t.s], t.j * 16)
                for m, bk in ((0, BC), (1, BD)):
                    own2(dve.tensor_tensor(y_out[0:P, t.s, m], bk[0:P, :], bvp_bc[0:P, :], ALU.add))
                own2.wait()
                row_stats(y_out[0:P, t.s], t, own2).then_inc(y_ok, 1)
            phase_steps(dve, 1, phase2)
            phase_end(dve, 3)

            def scales(root_done, eps_name):
                dve.wait_ge(ev(root_done), 1)
                seq(dve.reciprocal(s12[0:P, :], tmp_a[0:P, :]))
                seq(dve.scalar_tensor_tensor(out=nm12[0:P, :], in0=mv[0:P, :, 0], scalar=-1.0, in1=s12[0:P, :],
                                             op0=ALU.mult, op1=ALU.mult))

            scales("a_s3", None)
            dve.drain().then_inc(ev("v_s3"), 1)
            own3 = Chain("dve_own3", 2)

            def one_hots(t, i, n=GB):
                par, uses = i % 2, t.j * 3 + i // 2
                dve.wait_ge(idx_in[par], uses * 16 + 16)
                dve.tensor_copy(lane_f[:, par, 0:n], idx[:, par, 0:n, 1]).then_inc(lanes_read[par], 1)
                dve.wait_ge(lanes_read[par], uses + 1)
                dve.wait_ge(ring_free[par], uses)
                dve.tensor_tensor(hit[:, par, 0:n, :], iota_p.unsqueeze(1).to_broadcast([128, n, P]),
                                  lane_f[:, par, 0:n].unsqueeze(2).to_broadcast([128, n, P]),
                                  ALU.is_equal).then_inc(hits, 1)

            def add_groups(t, i, n=GB):
                first_group = t.j * (2 * BATCHES * GB) + i * GB
                _, offs = nc.values_load_multi_w_load_instructions(
                    group_off[0:1, bass.ds(first_group, n)], engines=[mybir.EngineType.DVE],
                    min_val=0, max_val=(NT - 1) * RW)
                flat_acc = ACC[0:P, :]
                for g in range(n):
                    at = i * GB + g
                    bk = (BE, BH)[at % 2]
                    dve.wait_ge(g_mm, first_group + g + 1)
                    dve.wait_ge(g_add[1 - at % 2], t.j * (BATCHES * GB) + (at + 1) // 2)
                    dst = flat_acc[:, bass.ds(offs[g], RW)]
                    dve.tensor_tensor(dst, dst, bk[0:P, 0:RW], ALU.add).then_inc(g_add[at % 2], 1)

            one_hots(Step(2, 0, 0), 0)

            def phase3(t, last):
                own3.start(t)
                i = t.s * BATCHES
                dve.wait_ge(x_ld[t.s], t.uses() * 16 + 16)
                dve.wait_ge(y_ld[t.s], t.j * 16 + 16)
                dve.wait_ge(z_st[t.s], t.j * 16)
                dve.tensor_tensor(z3[0:P, t.s], x3[0:P, t.s], y3[0:P, t.s], ALU.add).then_inc(zadd, 1)
                dve.wait_ge(zadd, t.u + 1)
                own3(dve.tensor_tensor(z3[0:P, t.s], z3[0:P, t.s], mb2_bc[0:P, :].unsqueeze(1).to_broadcast([P, 2, D]),
                                       ALU.add))
                one_hots(t, i + 1)
                add_groups(t, i)
                one_hots(t, i + 2)
                own3.wait()
                dve.wait_ge(m_mm, t.u + 1)
                for m, bk in ((0, BC), (1, BD)):
                    mm = dve.tensor_tensor(z3[0:P, t.s, m], z3[0:P, t.s, m], bk[0:P, :], ALU.add)
                    if m == 0:
                        own3(mm)
                mm.then_inc(z_ok, 1)
                add_groups(t, i + 1)
                if last:
                    one_hots(t, i + 3, LAST)
                elif t.s == 0:
                    one_hots(t, i + 3)
                else:
                    one_hots(Step(2, t.j + 1, 0), 0)
                add_groups(t, i + 2)
                if last:
                    add_groups(t, i + 3, LAST)
            phase_steps(dve, 2, phase3)
            phase_end(dve, 4)

            own4 = Chain("dve_own4", 7)

            def phase4(t, last):
                own4.start(t)
                dve.wait_ge(z_ld[t.s], t.j * 16 + 16)
                dve.wait_ge(a_cp, t.u + 1)
                for m in (0, 1):
                    mm = dve.scalar_tensor_tensor(out=z4[0:P, t.s, m], in0=b2_bc[0:P, :],
                                                  scalar=accs[0:P, t.s, m, HID:RW], in1=z4[0:P, t.s, m],
                                                  op0=ALU.mult, op1=ALU.add)
                mm.then_inc(accs_deg[t.s], 1)
                dve.wait_ge(accs_deg[t.s], t.j + 1)
                dve.wait_ge(a_mm, t.u + 1)
                dve.wait_ge(x1_st[t.s], t.j * 16)
                for m in (0, 1):
                    bk = ((BC, BD), (BA, BB))[t.s][m]
                    own4(dve.tensor_tensor(x4[0:P, t.s, m], z4[0:P, t.s, m], bk[0:P, :], ALU.add))
                own4.wait()
                row_stats(x4[0:P, t.s], t, own4).then_inc(x1_ok[t.s], 1)
            phase_steps(dve, 0, phase4)
            phase_end(dve, 5)

            scales("a_s4", None)
            dve.tensor_scalar(s1[0:P, :], s12[0:P, :], 1.0, None, ALU.add)
            pairs = nm12[0:P, :].rearrange("p (u m) -> p u m", m=2)
            dve.tensor_tensor(nms[0:P, :], pairs[:, :, 0], pairs[:, :, 1], ALU.add)
            dve.tensor_scalar(fb2_bc[:, :], fb2_bc[:, :], 0.5, None, ALU.mult)
            dve.drain().then_inc(ev("v_s4"), 1)
            own5 = Chain("dve_own5", 2)

            def ll_rows(t, own):
                dve.wait_ge(xo, t.u + 1)
                own(dve.scalar_tensor_tensor(out=t4[0:P, 0], in0=z4[0:P, t.s, 0], scalar=s12[0:P, bass.ds(t.u * 2, 1)],
                                             in1=xn4[0:P], op0=ALU.mult, op1=ALU.add))
                own.wait()
                cols = t4[0:P, 0].rearrange("p (c m) -> p c m", m=2)
                dve.wait_ge(ll_tr, t.u - 1 if t.s or not isinstance(t.j, int) or t.j else 0)
                dve.tensor_tensor(ll[0:P, t.s], cols[:, :, 0], cols[:, :, 1], ALU.add).then_inc(llr, 1)

            class Once:
                def __call__(self, inst):
                    seq(inst)

                def wait(self):
                    pass
            ll_rows(Step(0, 0, 0), Once())

            def phase5(t, last):
                own5.start(t)
                if not last:
                    ll_rows(next_step(t), own5)
                dve.wait_ge(llr, t.u + 1)
                own5(dve.scalar_tensor_tensor(out=quarter[0:P, 0], in0=ll[0:P, t.s], scalar=-0.25, in1=fb2_bc[0:P, :],
                                              op0=ALU.mult, op1=ALU.add))
                own5.wait()
                dve.wait_ge(f2, t.u + 1)
                dve.scalar_tensor_tensor(out=dlt[0:P, 0], in0=BC[0:P, 0:HL], scalar=0.5, in1=quarter[0:P, 0],
                                         op0=ALU.mult, op1=ALU.add).then_inc(dl, 1)
                dve.wait_ge(dl, t.u + 1)
                dve.wait_ge(xu, t.u + 1)
                for m in (0, 1):
                    o = o4[0:P, t.s, m].rearrange("p (c m) -> p c m", m=2)
                    mm = dve.tensor_tensor(o, o, dlt[0:P, 0].unsqueeze(2).to_broadcast([P, HL, 2]), ALU.add)
                mm.then_inc(o_ok, 1)
            phase_steps(dve, 0, phase5)


IN_SHAPES = {
    "x": (N, D), "src": (E,), "dst": (E,), "L0_gnn_W1": (D, HID), "L0_gnn_b1": (HID,), "L0_gnn_W2": (HID, D),
    "L0_gnn_b2": (D,), "L0_mix_kqv_w": (D, 3 * D), "L0_mix_kqv_b": (3 * D,), "L0_mix_proj_w": (D, D),
    "L0_mix_proj_b": (D,), "L0_mix_n1_g": (D,), "L0_mix_n1_b": (D,), "L0_mix_n2_g": (D,), "L0_mix_n2_b": (D,),
    "L0_mix_mlp_w1": (D, D), "L0_mix_mlp_b1": (D,), "L0_mix_mlp_w2": (D, D), "L0_mix_mlp_b2": (D,),
    "L0_ffn_fc1_b": (HL,), "L0_ffn_fc2_b": (HL,),
}


def shape_constants():
    k = np.arange(128)
    c = {
        "less": (np.arange(P)[:, None] < np.arange(P)[None, :]).astype(np.float16),
        "upper": ((k[:, None] < NT) & (k[:, None] < (k[None, :] % 64))).astype(np.float32),
        "iota_g": np.tile(np.arange(GROUPS, dtype=np.float32), (128, 1)),
        "iota_p": np.tile(np.arange(P, dtype=np.float32), (128, 1)),
        "ident": np.eye(128, dtype=np.float32),
        "blank": np.tile(np.array([0, 128], np.int32), GROUPS),
    }
    weight = np.where(k < 64, 128, 1)[:, None] * ((k % 64)[:, None] == np.arange(NT)[None, :])
    c["pick"] = np.broadcast_to(weight[:, :, None], (128, NT, P)).astype(np.float16)
    at = np.linspace(0.0, 1.0, D, dtype=np.float32) * np.float32(D // 2 - 1)
    low = np.clip(np.floor(at).astype(np.int32), 0, D // 2 - 2)
    w = at - low.astype(np.float32)
    interp = np.zeros((D, D // 2), np.float32)
    interp[np.arange(D), low] = np.float32(1) - w
    interp[np.arange(D), low + 1] += w
    c["interp"] = interp
    return {"c_" + name: np.ascontiguousarray(v) for name, v in c.items()}


def kernel(**inputs):
    import concourse.bacc as bacc
    from concourse.bass_utils import run_bass_kernel_spmd

    arrays = {name: np.ascontiguousarray(inputs[name]) for name in IN_SHAPES}
    arrays["w_t"] = np.ascontiguousarray(np.asarray(inputs["L0_mix_w"]).T)
    arrays["fc1_t"] = np.ascontiguousarray(np.asarray(inputs["L0_ffn_fc1_w"]).T)
    arrays["fc2_t"] = np.ascontiguousarray(np.asarray(inputs["L0_ffn_fc2_w"]).T)
    arrays.update(shape_constants())
    nc = bacc.Bacc("TRN2", target_bir_lowering=False, num_devices=1)
    d = {name: nc.dram_tensor(name, a.shape, mybir.dt.from_np(a.dtype), kind="ExternalInput").ap()
         for name, a in arrays.items()}
    d["out"] = nc.dram_tensor("out", (N, D), F32, kind="ExternalOutput").ap()
    build_program(nc, d)
    result = run_bass_kernel_spmd(nc, [arrays], core_ids=[0])
    return result.results[0]["out"]
```

```python
from contextlib import ExitStack

import numpy as np
import concourse.bass as bass
from concourse import mybir

F32, F16, I32, U16 = mybir.dt.float32, mybir.dt.float16, mybir.dt.int32, mybir.dt.uint16
ALU, ACT = mybir.AluOpType, mybir.ActivationFunctionType

N, D, E = 6250, 512, 100000
P, NT = 125, 50
STEPS = NT // 2
HID, M, HL = 256, 256, 256
KC, KH = D // 128, HID // 128
RW = HID + 1
EC = E // P
EH = EC // 2
PAIRS = (E + NT * 255) // 256
GROUPS = 2 * PAIRS
SG = 20
PB, BATCHES = 6, 3
SP = PB * BATCHES
LAST = PAIRS - SP * (STEPS - 1)
LAST_BATCHES = [min(PB, LAST - i) for i in range(0, LAST, PB)]
ROUND = 12582912.0
EPS1, EPS2, EPS_ATTN = 1e-5, 1e-3, 1e-8
assert 0 < LAST <= SP and EC % (2 * SG) == 0


class Step:

    def __init__(self, phase, j, s):
        self.phase, self.j, self.s = phase, j, s
        self.u = j * 2 + s
        self.g = self.u + 25 * phase

    def uses(self, s=None):
        s = self.s if s is None else s
        return self.j + (13 - s) * self.phase


def phase_steps(eng, phase, emit):
    with eng.Fori(0, STEPS // 2) as j:
        emit(Step(phase, j, 0), False)
        emit(Step(phase, j, 1), False)
    emit(Step(phase, STEPS // 2, 0), True)


def build_program(nc, d):
    ctx = ExitStack()
    with ctx:
        def sb(name, words, dt=F32):
            return ctx.enter_context(nc.sbuf_tensor("sb_" + name, [128, words], dt))

        def new_sem(name):
            return ctx.enter_context(nc.semaphore("s_" + name))

        events, counters = {}, []

        def sem(name):
            counters.append(new_sem(name))
            return counters[-1]

        def wait(eng, s, n):
            if not (isinstance(n, int) and n == 0):
                eng.wait_ge(s, n + 1 if any(s is c for c in counters) else n)

        def ev(name):
            if name not in events:
                events[name] = new_sem("ev_" + name)
            return events[name]

        ACC = sb("acc", NT * RW)
        EDGE_WORDS, KQV_WORDS = 3 * EC + 6 * SG + 40, KC * 3 * D
        WEIGHTS = sb("weights", EDGE_WORDS + KQV_WORDS + 8192)
        EDGE = WEIGHTS[:, 0:EDGE_WORDS]
        KQV = WEIGHTS[:, EDGE_WORDS:EDGE_WORDS + KQV_WORDS]
        LATE = WEIGHTS[:, EDGE_WORDS + KQV_WORDS:]
        STEP = sb("step", 14424)
        CONST = sb("const", 8900)

        def carver(region):
            at = [0]

            def take(*shape, dt=F32):
                n = int(np.prod(shape))
                words = n if dt in (F32, I32) else (n + 1) // 2
                v = region[:, at[0]:at[0] + words]
                at[0] += (words + 7) // 8 * 8
                assert at[0] <= region.shape[1] + 7, (at[0], region.shape)
                if dt is not F32:
                    v = v.bitcast(dt)
                    if dt is F16:
                        v = v[:, 0:n]
                if len(shape) == 2:
                    v = v.rearrange("p (a b) -> p a b", b=shape[1])
                elif len(shape) == 3:
                    v = v.rearrange("p (a b c) -> p a b c", b=shape[1], c=shape[2])
                return v
            return take

        acc = ACC[:, :].rearrange("p (t f) -> p t f", f=RW)
        onehot_a = ACC[:, 0:32 * EC // 2].bitcast(F16).rearrange("p (b j) -> p b j", j=EC)
        kqv_w = KQV[:, :].rearrange("p (c n) -> p c n", c=KC)
        ring_end = BATCHES * 2 * PB * RW
        ring = WEIGHTS[:, 0:ring_end].rearrange("p (h k f) -> p h k f", k=2 * PB, f=RW)
        hit_last = WEIGHTS[:, ring_end:ring_end + 2 * PB * P].rearrange("p (k q) -> p k q", q=P)
        assert ring_end + 2 * PB * P <= EDGE_WORDS + KQV_WORDS + KC * D
        late = carver(LATE)
        proj_w, mlp1_w, mlp2_w = late(KC, D), late(KC, D), late(KC, D)
        gnn2_w, fc1e, fc2_w = late(KH, D), late(2, HL), late(2, HL)
        onehot_b = LATE[:, 0:18 * EC // 2].bitcast(F16).rearrange("p (b j) -> p b j", j=EC)

        def onehot(b):
            return onehot_a[0:P, b] if b < 32 else onehot_b[0:P, b - 32]

        edge = carver(EDGE)
        slot_of, payload = edge(EC, dt=I32), edge(EC, 2, dt=I32)
        stage_slot, stage_pay = edge(2, SG, dt=I32), edge(2, 2 * SG, dt=I32)

        const = carver(CONST)
        ident = const(128)
        w_t, gnn1_w = const(KC, M), const(KC, HID)
        pmat = const(KH, D)
        b1_bc, bv_bc, bvp_bc, mb2_bc, b2_bc, fb2_bc = (
            const(HID), const(D), const(D), const(D), const(D), const(HL))
        ones = const(128)
        neg_half = const(1)
        eps_c = const(2)
        n1g, n1b, n2g, n2b = const(KC), const(KC), const(KC), const(KC)
        kqb, m1b, f1b = const(2 * KC), const(KC), const(2)
        iota_p = const(P)
        pair_off = const(PAIRS, dt=I32)
        sum_x, nmean, ssq = const(NT), const(NT), const(NT)
        s1, s12, rs2, nm1, nm12, tmp_a, tmp_b = (const(NT) for _ in range(7))
        mv = const(NT, 2)
        stat6 = const(2, 6)
        less = const(P, dt=F16)
        strip = const(178, dt=F16)
        ones_h = const(2, dt=F16)
        upper = const(128)
        n_pairs, base, end_g = const(1), const(1), const(1)
        ks_bc = const(M)
        zero_row = const(512)
        mvs, tiny, pool_tiny = const(2, 2), const(1), const(2)
        nms = const(STEPS)

        s0 = carver(STEP)
        src_i, dst_i, src_f, blk_q, blk_h = (
            s0(EC, dt=I32), s0(EC, dt=I32), s0(EC), s0(EC), s0(EC, dt=F16))
        count, incl, first, first_h, pos = s0(EC), s0(EC), s0(EC), s0(EC, dt=F16), s0(EC)
        pick = s0(NT, P, dt=F16)
        iota_g, past = s0(PAIRS), s0(PAIRS, dt=F16)
        vb4 = s0(KC, 128)
        xs = KQV[:, 0:10 * D].rearrange("p (h i f) -> p h i f", h=2, i=5)
        s1_ = carver(STEP)
        x_in, hh = s1_(2, 2, D), s1_(2, 2, D)
        hT = s1_(2, KC, 2 * P)
        kT, sq, sqa, sqb = s1_(KC, 2 * P), s1_(KC, 2 * P), s1_(2, 2 * P), s1_(2 * P)
        kp, kps, rt = s1_(2, M), s1_(2, M), s1_(2, HID)
        nxd = s1_(2)
        qpn, qpT = s1_(2, M), s1_(KH, 2 * P)
        y_out = s1_(2, 2, D)
        den, rden = s1_(2), s1_(2)
        junk = s1_(2, M)
        hk, kptv = x_in[:, 0].rearrange("p a (b c) -> p (a b) c", c=M), x_in[:, 1].rearrange("p a (b c) -> p (a b) c", c=M)
        s3_ = carver(STEP)
        x3, y3, h3, hT3 = s3_(2, 2, D), s3_(2, 2, D), s3_(2, 2, D), s3_(2, KC, 2 * P)
        gT3, z3 = s3_(KC, 2 * P), s3_(2, 2, D)
        hit = [s3_(2 * PB, P), s3_(2 * PB, P), hit_last]
        idx, lane_f = s3_(2, 2 * SP, 2, dt=I32), s3_(2, 2 * SP)
        s4_ = carver(STEP)
        z4, x4, accs, accT = s4_(2, 2, D), s4_(2, 2, D), s4_(2, 2, RW), s4_(2, KH, 2 * P)
        t4, ll, llT, gT4, xn4 = s4_(2, D), s4_(2, HL), s4_(2, P), s4_(2, P), s4_(D)
        dlt = s4_(2, HL)
        o4 = s4_(2, 2, D)
        quarter = s4_(2, HL)
        interp, fc1_t = s4_(KC, HL), s4_(KC, HL)

        bank = [ctx.enter_context(nc.psum_tensor(f"bank{i}", [128, 512], F32)) for i in range(8)]
        BA, BB, BC, BD, BE, BF, BG, BH = bank

        def rows(t):
            return t.rearrange("(p t) f -> p t f", t=NT)

        x_d, out_d = rows(d["x"]), rows(d["out"])
        table = nc.dram_tensor("hidden_rows", [N, RW], F32).ap()
        y_d = nc.dram_tensor("y_rows", [N, D], F32).ap()
        z_d = nc.dram_tensor("z_rows", [N, D], F32).ap()
        x1_d = nc.dram_tensor("x1_rows", [N, D], F32).ap()
        sorted_d = nc.dram_tensor("sorted_edges", [128 * GROUPS, 2], I32).ap()
        sorted_v = sorted_d.rearrange("(p g) e -> p g e", g=GROUPS)
        chunks = lambda t: t.rearrange("(c p) n -> p c n", p=128)
        col = lambda t: t.rearrange("(c p) -> p c", p=128)

        all_engines = sem("phase_end")
        pair = lambda name: [sem(name + "0"), sem(name + "1")]
        e_in, c_in, w_in, late_in, prefill = (sem(n) for n in (
            "edges_in", "sort_consts_in", "weights_in", "late_in", "blank_slots"))
        xs_in, x_ld, y_ld, z_ld, x1_ld = (pair(n) for n in (
            "stat_x_in", "x_in", "y_in", "z_in", "x1_in"))
        r_st, y_st, z_st, x1_st, o_st = (sem("r_stored"), *(pair(n) for n in (
            "y_stored", "z_stored", "x1_stored", "out_stored")))
        idx_in = pair("idx_in")
        scattered = [new_sem(f"scattered{s}") for s in range(2)]
        gathered = [new_sem(f"gathered{k}") for k in range(BATCHES)]
        st_sum, st_mean, st_free = sem("stat_sums"), sem("stat_means"), sem("stat_x_used")
        rank_mm, rank_used, staged = sem("rank_products"), sem("ranks_used"), sem("scatter_staged")
        (h_rows, tr, h_t, feat, feat_c, sqs, xd, nx, wx, ex, r_mm, r_up, r_ok, kadd, hk_mm, qn, qt, qtc,
         y_mm, y_ok, zadd, z_ok, m_mm, hits, g_mm) = (sem(n) for n in (
            "h_rows", "h_transposed", "hT", "features", "features_copied", "square_sums", "xd", "xd_copied",
            "w_products", "exps", "r_products", "r_read", "r_rows", "kp_added", "hk_products", "q_scaled",
            "q_transposed", "qT", "y_products", "y_rows", "z_sums", "z_rows", "mlp2_products", "one_hots",
            "group_products"))
        g_add, lanes = pair("group_added"), sem("lanes")
        ring_free = [sem(f"ring_used{k}") for k in range(BATCHES)]
        a_cp, a_mm = sem("acc_staged"), sem("w2_products")
        accs_tr, accs_deg, x1_ok = pair("acc_stage_transposed"), pair("degrees_used"), pair("x1_rows")
        xo, llr, ll_tr, ll_t, f1, gl, f2, dl, xu, o_ok = (sem(n) for n in (
            "odd_scaled", "ll_rows", "ll_transposed", "llT", "fc1", "gelu", "fc2", "delta", "x1_plus_xn",
            "out_rows"))

        def phase_end(eng, n):
            eng.drain().then_inc(all_engines, 1)
            wait(eng, all_engines, 4 * n)

        ev_fc = sem("fc_in")
        a_t_slot = pair("accT_slot")
        dve_self, pool_self = sem("dve_self"), sem("pool_self")
        dve_own = [sem(f"dve_own{i}") for i in range(5)]

        block = ctx.enter_context(nc.Block())

        @block.sync
        def _(sp):
            for c in counters:
                sp.sem_inc(c, 1)
            sp.sem_inc(ev("counters_set"), 1)
            sp.dma_start(src_i[0:P], d["src"].rearrange("(p j) -> p j", p=P)).then_inc(e_in, 16)
            sp.dma_start(dst_i[0:P], d["dst"].rearrange("(p j) -> p j", p=P)).then_inc(e_in, 16)
            for t, s in ((less[0:P], "less"), (upper[:, :], "upper"), (pick[:, :, :], "pick"),
                         (iota_g[:, :], "iota_g"), (iota_p[:, :], "iota_p"), (ident[:, :], "ident")):
                sp.dma_start(t, d["c_" + s]).then_inc(c_in, 16)
            sp.dma_start(sorted_d.rearrange("(p g) e -> p (g e)", g=GROUPS),
                         d["c_blank"].partition_broadcast(128)).then_inc(prefill, 16)

            def stat_load(j, s):
                wait(sp, st_free, j * 2 + s)
                sp.dma_start(xs[0:P, s], x_d[:, bass.ds(j * 10 + 5 * s, 5), :]).then_inc(xs_in[s], 16)
            with sp.Fori(0, 5) as j:
                stat_load(j, 0)
                stat_load(j, 1)
            wait(sp, st_free, 10)
            for t, s in ((kqv_w, chunks(d["L0_mix_kqv_w"])), (w_t, chunks(d["w_t"])),
                         (gnn1_w, chunks(d["L0_gnn_W1"])), (n1g, col(d["L0_mix_n1_g"])),
                         (n1b, col(d["L0_mix_n1_b"])), (kqb, col(d["L0_mix_kqv_b"][0:2 * D])),
                         (b1_bc, d["L0_gnn_b1"].partition_broadcast(128)),
                         (bv_bc, d["L0_mix_kqv_b"][2 * D:3 * D].partition_broadcast(128)),
                         (bvp_bc, d["L0_mix_proj_b"].partition_broadcast(128)),
                         (mb2_bc, d["L0_mix_mlp_b2"].partition_broadcast(128)),
                         (b2_bc, d["L0_gnn_b2"].partition_broadcast(128)),
                         (fb2_bc, d["L0_ffn_fc2_b"].partition_broadcast(128)),
                         (n2g, col(d["L0_mix_n2_g"])), (n2b, col(d["L0_mix_n2_b"])),
                         (m1b, col(d["L0_mix_mlp_b1"])), (f1b, col(d["L0_ffn_fc1_b"]))):
                sp.dma_start(t[:], s, allow_slow_non_contiguous=True).then_inc(w_in, 16)
            phase_end(sp, 1)

            for t, s in ((proj_w, chunks(d["L0_mix_proj_w"])), (mlp1_w, chunks(d["L0_mix_mlp_w1"])),
                         (mlp2_w, chunks(d["L0_mix_mlp_w2"])), (gnn2_w, chunks(d["L0_gnn_W2"])),
                         (fc2_w, chunks(d["fc2_t"]))):
                sp.dma_start(t[:], s).then_inc(late_in, 16)

            def load_x(j, s):
                sp.dma_start(x_in[0:P, s], x_d[:, bass.ds(j * 4 + 2 * s, 2), :]).then_inc(x_ld[s], 16)

            def attention_io(phase, store):
                for s in (0, 1):
                    load_x(0, s)

                def step(t, more):
                    if more:
                        after = t.j + 1
                        wait(sp, h_rows, t.g + 1)
                        load_x(after, t.s)
                    store(t)
                with sp.Fori(0, STEPS // 2 - 1) as j:
                    step(Step(phase, j, 0), True)
                    step(Step(phase, j, 1), True)
                step(Step(phase, STEPS // 2 - 1, 0), True)
                step(Step(phase, STEPS // 2 - 1, 1), False)
                step(Step(phase, STEPS // 2, 0), False)

            table_v = rows(table)

            def store_r(t):
                wait(sp, r_ok, t.u + 1)
                sp.dma_start(table_v[:, bass.ds(t.u * 2, 2), :], acc[0:P, bass.ds(t.u * 2, 2), :]).then_inc(r_st, 16)
            attention_io(0, store_r)
            wait(sp, r_st, 16 * STEPS)
            phase_end(sp, 2)

            def store_y(t):
                wait(sp, y_ok, t.u + 1)
                sp.dma_start(rows(y_d)[:, bass.ds(t.u * 2, 2), :], y_out[0:P, t.s]).then_inc(y_st[t.s], 16)
            attention_io(1, store_y)
            wait(sp, y_st[0], 16 * 13)
            wait(sp, y_st[1], 16 * 12)
            phase_end(sp, 3)

            for s in (0, 1):
                wait(sp, scattered[s], 16 * EC // 2)

            def load_xd(j, s):
                sp.dma_start(x3[0:P, s], x_d[:, bass.ds(j * 4 + 2 * s, 2), :]).then_inc(x_ld[s], 16)

            def load_yd(j, s):
                sp.dma_start(y3[0:P, s], rows(y_d)[:, bass.ds(j * 4 + 2 * s, 2), :]).then_inc(y_ld[s], 16)

            def load_idx(j, s, n=2 * SP):
                sp.dma_start(idx[:, s, 0:n], sorted_v[:, bass.ds(j * (4 * SP) + s * (2 * SP), n), :]
                             ).then_inc(idx_in[s], 16)

            def mlp_io(t, more, n=2 * SP):
                if more:
                    after = t.j + 1
                    wait(sp, zadd, t.u + 1)
                    load_xd(after, t.s)
                    wait(sp, h_rows, t.g + 1)
                    load_yd(after, t.s)
                    wait(sp, ring_free[BATCHES - 1], t.u + 1)
                    load_idx(after, t.s, n)
                wait(sp, z_ok, t.u + 1)
                sp.dma_start(rows(z_d)[:, bass.ds(t.u * 2, 2), :], z3[0:P, t.s]).then_inc(z_st[t.s], 16)
            for s in (0, 1):
                load_idx(0, s)
                load_xd(0, s)
                load_yd(0, s)
            with sp.Fori(0, STEPS // 2 - 1) as j:
                mlp_io(Step(2, j, 0), True)
                mlp_io(Step(2, j, 1), True)
            mlp_io(Step(2, STEPS // 2 - 1, 0), True, 2 * LAST)
            mlp_io(Step(2, STEPS // 2 - 1, 1), False)
            mlp_io(Step(2, STEPS // 2, 0), False)
            wait(sp, z_st[0], 16 * 13)
            wait(sp, z_st[1], 16 * 12)
            phase_end(sp, 4)

            def tail_io(src, src_v, sems, used, store):
                def load(j, s):
                    sp.dma_start(src[0:P, s], src_v[:, bass.ds(j * 4 + 2 * s, 2), :]).then_inc(sems[s], 16)
                load(0, 0)
                load(0, 1)

                def step(t, more):
                    if more:
                        after = t.j + 1
                        wait(sp, *used(t))
                        load(after, t.s)
                    store(t)
                with sp.Fori(0, STEPS // 2 - 1) as j:
                    step(Step(0, j, 0), True)
                    step(Step(0, j, 1), True)
                step(Step(0, STEPS // 2 - 1, 0), True)
                step(Step(0, STEPS // 2 - 1, 1), False)
                step(Step(0, STEPS // 2, 0), False)

            def store_x1(t):
                wait(sp, x1_ok[t.s], t.j + 1)
                sp.dma_start(rows(x1_d)[:, bass.ds(t.u * 2, 2), :], x4[0:P, t.s]).then_inc(x1_st[t.s], 16)
            sp.dma_start(interp, chunks(d["c_interp"])).then_inc(ev_fc, 16)
            sp.dma_start(fc1_t, chunks(d["fc1_t"])).then_inc(ev_fc, 16)
            tail_io(z4, rows(z_d), z_ld, lambda t: (x1_ok[t.s], t.j + 1), store_x1)
            wait(sp, x1_st[0], 16 * 13)
            wait(sp, x1_st[1], 16 * 12)
            phase_end(sp, 5)

            def store_out(t):
                wait(sp, o_ok, t.u + 1)
                sp.dma_start(out_d[:, bass.ds(t.u * 2, 2), :], o4[0:P, t.s]).then_inc(o_st[t.s], 16)
            tail_io(z4, rows(x1_d), x1_ld, lambda t: (xu, t.u + 1), store_out)
            wait(sp, o_st[0], 16 * 13)
            wait(sp, o_st[1], 16 * 12)

        @block.gpsimd
        def _(pool):
            wait(pool, ev("counters_set"), 1)
            wait(pool, ev("slots"), 1)
            wait(pool, prefill, 16)

            def carry_waits(n):
                wait(pool, pool_self, n + 1)
                pool.tensor_tensor(pool_tiny[0:1, 1:2], pool_tiny[0:1, 0:1], pool_tiny[0:1, 0:1],
                                   ALU.add).then_inc(pool_self, 1)

            pool.memset(pool_tiny[:, :], 0.0).then_inc(pool_self, 1)

            def scatter(j, s):
                wait(pool, scattered[s], j * (16 * SG))
                c = (j * 2 + s) * SG
                pool.tensor_copy(stage_slot[0:P, s], slot_of[0:P, bass.ds(c, SG)]).then_inc(staged, 1)
                pool.tensor_copy(stage_pay[0:P, s], payload.rearrange("p j e -> p (j e)")[0:P, bass.ds(c * 2, 2 * SG)]).then_inc(staged, 1)
                wait(pool, staged, (j * 2 + s) * 2 + 2)
                carry_waits(j * 2 + s)
                for k in range(SG):
                    pool.indirect_dma_start(
                        out=sorted_d, out_offset=bass.IndirectOffsetOnAxis(ap=stage_slot[0:P, s, k:k + 1], axis=0),
                        in_=stage_pay[0:P, s, 2 * k:2 * k + 2], in_offset=None).then_inc(scattered[s], 16)
            scatter(0, 0)
            scatter(0, 1)
            with pool.Fori(1, EC // SG // 2) as j:
                scatter(j, 0)
                scatter(j, 1)

            def gather(t, k, n):
                wait(pool, idx_in[t.s], t.j * 16 + 16)
                wait(pool, ring_free[k], t.u)
                carry_waits(t.u * BATCHES + (EC // SG + k))
                for g in range(2 * n):
                    pool.indirect_dma_start(
                        out=ring[:, k, g], out_offset=None, in_=table,
                        in_offset=bass.IndirectOffsetOnAxis(ap=idx[:, t.s, k * 2 * PB + g, 0:1], axis=0)
                        ).then_inc(gathered[k], 16)

            def gather_step(t, last):
                for k, n in enumerate(LAST_BATCHES if last else [PB] * BATCHES):
                    gather(t, k, n)
            wait(pool, all_engines, 4 * 3)
            phase_steps(pool, 2, gather_step)

            wait(pool, all_engines, 4 * 4)

            def stage_acc(t, last):
                wait(pool, accs_tr[t.s], t.j)
                wait(pool, accs_deg[t.s], t.j)
                pool.tensor_copy(accs[0:P, t.s], acc[0:P, bass.ds(t.u * 2, 2), :]).then_inc(a_cp, 1)
            phase_steps(pool, 0, stage_acc)

        @block.tensor
        def _(pe):
            wait(pe, ev("counters_set"), 1)
            wait(pe, ev("onehot"), 1)
            for b in range(NT):
                for h, bk in ((0, BA), (1, BB)):
                    last = pe.matmul(bk[:, 0:EH], strip[0:P, 49 - b:177 - b], onehot(b)[:, h * EH:(h + 1) * EH],
                                     start=b == 0, stop=b == NT - 1)
            last.then_inc(ev("pe_count"), 1)
            wait(pe, c_in, 6 * 16)
            wait(pe, ev("groups"), 1)
            pe.matmul(BC[:, 0:1], upper[:, :], n_pairs[:, :], start=True, stop=True).then_inc(ev("pe_base"), 1)
            wait(pe, ev("past"), 1)
            pe.matmul(BD[0:1, 0:PAIRS], ones_h[0:NT, 0:1], past[0:NT, :], start=True, stop=True).then_inc(ev("pe_tiles"), 1)
            wait(pe, ev("first"), 1)
            for b in range(NT):
                for h in (0, 1):
                    bk = (BA, BB, BF, BG)[b % 2 * 2 + h]
                    if b >= 2:
                        wait(pe, rank_used, 2 * (b - 2) + h + 1)
                    cols = slice(h * EH, (h + 1) * EH)
                    pe.matmul(bk[0:P, 0:EH], less[0:P, :], onehot(b)[:, cols], start=True, stop=False)
                    pe.matmul(bk[0:P, 0:EH], pick[:, b, :], first_h[:, cols], start=False, stop=True).then_inc(rank_mm, 1)
            wait(pe, ev("bias_in"), 1)
            for c in range(2 * KC):
                for k in range(KC):
                    pe.matmul(BC[:, c:c + 1], kqv_w[:, k, c * 128:(c + 1) * 128], n1b[:, k:k + 1],
                              start=k == 0, stop=k == KC - 1)
            for k in range(KC):
                last = pe.matmul(BD[:, :], vb4[:, k, :], kqv_w[:, k, 2 * D:3 * D], start=k == 0, stop=k == KC - 1)
            last.then_inc(ev("pe_bias"), 1)
            phase_end(pe, 1)

            def transposes(t, rows_sb):
                wait(pe, h_rows, t.g + 1)
                wait(pe, h_t, t.g * 2)
                for bk, cs in ((BF, (0, 1)), (BG, (2, 3))):
                    for i, c in enumerate(cs):
                        for m in (0, 1):
                            last = pe.transpose(bk[:, i * 250 + m * P:i * 250 + m * P + P],
                                                rows_sb[0:P, t.s, m, c * 128:(c + 1) * 128], ident[0:P, 0:P])
                    last.then_inc(tr, 1)

            def next_step(t):
                return Step(t.phase, t.j, 1) if t.s == 0 else Step(t.phase, t.j + 1, 0)

            def features(t, w, off, rhs):
                for i, bk in ((0, BA), (1, BB)):
                    wait(pe, h_t, t.g * 2 + 2)
                    wait(pe, feat_c, t.g * 2 + i)
                    for c in (2 * i, 2 * i + 1):
                        for k in range(KC):
                            last = pe.matmul(bk[:, (c % 2) * 250:(c % 2) * 250 + 2 * P],
                                             w[:, k, off + c * 128:off + (c + 1) * 128], rhs[:, t.s, k, :],
                                             start=k == 0, stop=k == KC - 1)
                    last.then_inc(feat, 1)

            def w_products(t):
                wait(pe, feat_c, t.g * 2 + 2)
                wait(pe, ex, t.g * 2)
                for m in (0, 1):
                    for k in range(KC):
                        last = pe.matmul(BE[0:P, m * M:(m + 1) * M], kT[:, k, m * P:(m + 1) * P], w_t[:, k, :],
                                         start=k == 0, stop=k == KC - 1)
                last.then_inc(wx, 1)
                wait(pe, sqs, t.g + 1)
                for m in (0, 1):
                    last = pe.matmul(BG[0:P, 508 + m:509 + m], sqb[:, m * P:(m + 1) * P], neg_half[:, 0:1],
                                     start=True, stop=True)
                last.then_inc(xd, 1)

            for bk in (BC, BD):
                pe.matmul(bk[:, :], zero_row[0:1, 0:128], zero_row[0:1, 0:512], start=True, stop=False)
            transposes(Step(0, 0, 0), hh)

            def r_product(t, m, bk):
                for k in range(KC):
                    last = pe.matmul(bk[0:P, 0:HID], hT[:, t.s, k, m * P:(m + 1) * P], gnn1_w[:, k, :],
                                     start=k == 0, stop=k == KC - 1)
                last.then_inc(r_mm, 1)

            def phase1(t, last):
                wait(pe, r_up, t.u * 2)
                features(t, kqv_w, 0, hT)
                r_product(t, 0, BH)
                w_products(t)
                r_product(t, 1, BA)
                if not last:
                    wait(pe, nx, t.g + 1)
                    transposes(next_step(t), hh)
                wait(pe, ex, t.g * 2 + 2)
                for k in range(KC):
                    for m in (0, 1):
                        mm = pe.matmul((BC, BD)[k // 2][:, (k % 2) * M:(k % 2 + 1) * M],
                                       hh[0:P, t.s, m, k * 128:(k + 1) * 128], kp[0:P, m, :],
                                       start=False, stop=False)
                mm.then_inc(hk_mm, 1)
            phase_steps(pe, 0, phase1)
            for bk in (BC, BD):
                mm = pe.matmul(bk[:, :], zero_row[0:1, 0:128], zero_row[0:1, 0:512], start=False, stop=True)
            mm.then_inc(ev("pe_hk"), 1)
            wait(pe, kadd, STEPS)
            for m in (0, 1):
                mm = pe.matmul(BE[:, 0:M], ones[0:P, :], kps[0:P, m, :], start=m == 0, stop=m == 1)
            mm.then_inc(ev("pe_ksum"), 1)
            wait(pe, ev("hk"), 1)
            for c in range(KC):
                bk = (BA, BB)[c // 2][:, (c % 2) * M:(c % 2 + 1) * M]
                for k in range(KC):
                    pe.matmul(bk, kqv_w[:, k, 2 * D + c * 128:2 * D + (c + 1) * 128], hk[:, k, :],
                              start=k == 0, stop=False)
                mm = pe.matmul(bk, bv_bc[0:1, c * 128:(c + 1) * 128], ks_bc[0:1, :], start=False, stop=True)
            mm.then_inc(ev("pe_kptv"), 1)
            wait(pe, ev("kptv"), 1)
            wait(pe, late_in, 5 * 16)
            for m in range(KH):
                for c in range(KC):
                    mm = pe.matmul((BF, BH)[m][:, :], kptv[:, c, m * 128:(m + 1) * 128], proj_w[:, c, :],
                                   start=c == 0, stop=c == KC - 1)
            mm.then_inc(ev("pe_pmat"), 1)
            for c in range(KC):
                for k in range(KC):
                    mm = pe.matmul(BG[:, c:c + 1], mlp1_w[:, k, c * 128:(c + 1) * 128], n2b[:, k:k + 1],
                                   start=k == 0, stop=k == KC - 1)
            mm.then_inc(ev("pe_mbias"), 1)
            phase_end(pe, 2)

            transposes(Step(1, 0, 0), hh)

            def v_product(t, m, bk):
                for k in range(KC):
                    pe.matmul(bk[0:P, :], hT[:, t.s, k, m * P:(m + 1) * P], kqv_w[:, k, 2 * D:3 * D],
                              start=k == 0, stop=False)

            def phase2(t, last):
                features(t, kqv_w, D, hT)
                wait(pe, y_ok, t.u)
                v_product(t, 0, BC)
                w_products(t)
                v_product(t, 1, BD)
                wait(pe, qn, t.u + 1)
                wait(pe, qtc, t.u)
                for c in range(KH):
                    for m in (0, 1):
                        mm = pe.transpose(BH[:, c * 250 + m * P:c * 250 + (m + 1) * P],
                                          qpn[0:P, m, c * 128:(c + 1) * 128], ident[0:P, 0:P])
                mm.then_inc(qt, 1)
                if not last:
                    wait(pe, nx, t.g + 1)
                    transposes(next_step(t), hh)
                wait(pe, qtc, t.u + 1)
                for m, bk in ((0, BC), (1, BD)):
                    for c in range(KH):
                        mm = pe.matmul(bk[0:P, :], qpT[:, c, m * P:(m + 1) * P], pmat[:, c, :],
                                       start=False, stop=c == KH - 1)
                mm.then_inc(y_mm, 1)
            phase_steps(pe, 1, phase2)
            phase_end(pe, 3)

            transposes(Step(2, 0, 0), h3)

            def groups(t, k, n):
                i = t.s * BATCHES + k
                wait(pe, hits, t.j * (2 * BATCHES) + i + 1)
                wait(pe, gathered[k], t.u * (32 * PB) + 32 * n)
                for g in range(n):
                    at = i * PB + g
                    wait(pe, g_add[at % 2], t.j * SP + at // 2)
                    for m in (0, 1):
                        mm = pe.matmul((BE, BH)[at % 2][0:P, 0:RW], hit[k][:, 2 * g + m, :], ring[:, k, 2 * g + m, :],
                                       start=m == 0, stop=m == 1)
                    mm.then_inc(g_mm, 1)
                pe.drain().then_inc(ring_free[k], 1)

            def phase3(t, last):
                batches = LAST_BATCHES if last else [PB] * BATCHES
                features(t, mlp1_w, 0, hT3)
                groups(t, 0, batches[0])
                wait(pe, feat_c, t.g * 2 + 2)
                wait(pe, z_ok, t.u)
                for m, bk in ((0, BC), (1, BD)):
                    for k in range(KC):
                        mm = pe.matmul(bk[0:P, :], gT3[:, k, m * P:(m + 1) * P], mlp2_w[:, k, :],
                                       start=k == 0, stop=k == KC - 1)
                mm.then_inc(m_mm, 1)
                groups(t, 1, batches[1])
                if not last:
                    transposes(next_step(t), h3)
                for k in range(2, len(batches)):
                    groups(t, k, batches[k])
            phase_steps(pe, 2, phase3)
            phase_end(pe, 4)

            wait(pe, ev_fc, 32)
            for i in range(2):
                for k in range(KC):
                    mm = pe.matmul(BE[:, i * HL:(i + 1) * HL], interp[:, k, i * 128:(i + 1) * 128], fc1_t[:, k, :],
                                   start=k == 0, stop=k == KC - 1)
            mm.then_inc(ev("pe_fc1"), 1)

            def acc_transposes(t):
                bk = (BF, BG)[t.s]
                wait(pe, a_cp, t.u + 1)
                wait(pe, a_t_slot[t.s], t.j)
                for c in range(KH):
                    for m in (0, 1):
                        mm = pe.transpose(bk[:, c * 250 + m * P:c * 250 + (m + 1) * P],
                                          accs[0:P, t.s, m, c * 128:(c + 1) * 128], ident[0:P, 0:P])
                mm.then_inc(accs_tr[t.s], 1)

            def phase4(t, last):
                if not last:
                    acc_transposes(next_step(t))
                wait(pe, a_t_slot[t.s], t.j + 1)
                wait(pe, x1_ok[t.s], t.j)
                for m in (0, 1):
                    bk = ((BC, BD), (BA, BB))[t.s][m]
                    for c in range(KH):
                        mm = pe.matmul(bk[0:P, :], accT[:, t.s, c, m * P:(m + 1) * P], gnn2_w[:, c, :],
                                       start=c == 0, stop=c == KH - 1)
                mm.then_inc(a_mm, 1)
            acc_transposes(Step(0, 0, 0))
            phase_steps(pe, 0, phase4)
            phase_end(pe, 5)

            def ll_transposes(t):
                wait(pe, llr, t.u + 1)
                wait(pe, ll_t, t.u)
                for c in (0, 1):
                    mm = pe.transpose(BF[:, c * P:(c + 1) * P], ll[0:P, t.s, c * 128:(c + 1) * 128], ident[0:P, 0:P])
                mm.then_inc(ll_tr, 1)

            def phase5(t, last):
                wait(pe, ll_t, t.u + 1)
                wait(pe, gl, t.u)
                for h in (0, 1):
                    for i in (0, 1):
                        mm = pe.matmul(BH[:, h * P:(h + 1) * P], fc1e[:, i, h * 128:(h + 1) * 128], llT[:, i, :],
                                       start=i == 0, stop=i == 1)
                mm.then_inc(f1, 1)
                if not last:
                    ll_transposes(next_step(t))
                wait(pe, gl, t.u + 1)
                wait(pe, dl, t.u)
                for c in (0, 1):
                    mm = pe.matmul(BC[0:P, 0:HL], gT4[:, c, :], fc2_w[:, c, :], start=c == 0, stop=c == 1)
                mm.then_inc(f2, 1)
            ll_transposes(Step(0, 0, 0))
            phase_steps(pe, 0, phase5)

        @block.scalar
        def _(act):
            wait(act, ev("counters_set"), 1)
            wait(act, ev("consts"), 1)

            def stats(j, s):
                wait(act, xs_in[s], j * 16 + 16)
                c = j * 10 + 5 * s
                for i in range(5):
                    act.activation(xs[0:P, s, i], xs[0:P, s, i], ACT.Copy,
                                   accum_out=sum_x[0:P, bass.ds(c + i, 1)]).then_inc(st_sum, 1)
                wait(act, st_sum, (c + 5))
                act.activation(nmean[0:P, bass.ds(c, 5)], sum_x[0:P, bass.ds(c, 5)], ACT.Copy,
                               scale=-1.0 / D).then_inc(st_mean, 1)
                wait(act, st_mean, j * 2 + s + 1)
                for i in range(5):
                    last = act.activation(xs[0:P, s, i], xs[0:P, s, i], ACT.Square, bias=nmean[0:P, bass.ds(c + i, 1)],
                                          accum_out=ssq[0:P, bass.ds(c + i, 1)])
                last.then_inc(st_free, 1)
            with act.Fori(0, 5) as j:
                stats(j, 0)
                stats(j, 1)
            wait(act, st_free, 10)
            act.activation(tmp_a[0:P, :], ssq[0:P, :], ACT.Sqrt, scale=1.0 / D, bias=eps_c[0:P, 0:1]).then_inc(ev("a_s1"), 1)
            wait(act, ev("v_var2"), 1)
            act.activation(rs2[0:P, :], tmp_b[0:P, :], ACT.Sqrt, bias=eps_c[0:P, 1:2]).then_inc(ev("a_s2"), 1)
            phase_end(act, 1)

            def copy_hT(t, dst):
                for i, bk in ((0, BF), (1, BG)):
                    wait(act, tr, t.g * 2 + i + 1)
                    act.copy(dst[:, t.s, 2 * i:2 * i + 2, :].rearrange("p a b -> p (a b)"), bk[:, 0:500]).then_inc(h_t, 1)

            def copy_features(t, biases, off):
                wait(act, wx, t.g)
                wait(act, sqs, t.g)
                for i, bk in ((0, BA), (1, BB)):
                    wait(act, feat, t.g * 2 + i + 1)
                    for c in (2 * i, 2 * i + 1):
                        last = act.activation(kT[:, c, :], bk[:, (c % 2) * 250:(c % 2) * 250 + 250], ACT.Identity,
                                              bias=biases[:, off + c:off + c + 1])
                    last.then_inc(feat_c, 1)

            def exps(t, used):
                wait(act, wx, t.g + 1)
                wait(act, xd, t.g + 1)
                act.copy(nxd[0:P, :], BG[0:P, 508:510]).then_inc(nx, 1)
                wait(act, nx, t.g + 1)
                used(t)
                for m in (0, 1):
                    act.activation(kp[0:P, m], BE[0:P, m * M:(m + 1) * M], ACT.Exp, bias=nxd[0:P, m:m + 1]).then_inc(ex, 1)

            def next_step(t):
                return Step(t.phase, t.j, 1) if t.s == 0 else Step(t.phase, t.j + 1, 0)

            copy_hT(Step(0, 0, 0), hT)

            def phase1(t, last):
                copy_features(t, kqb, 0)

                def used(t):
                    wait(act, hk_mm, t.u)
                    wait(act, kadd, t.u)
                exps(t, used)
                if not last:
                    copy_hT(next_step(t), hT)
            phase_steps(act, 0, phase1)
            phase_end(act, 2)

            copy_hT(Step(1, 0, 0), hT)

            def phase2(t, last):
                copy_features(t, kqb, KC)
                exps(t, lambda t: wait(act, qn, t.u))
                wait(act, qt, t.u + 1)
                wait(act, y_mm, t.u)
                act.copy(qpT.rearrange("p a b -> p (a b)"), BH[:, 0:500]).then_inc(qtc, 1)
                if not last:
                    copy_hT(next_step(t), hT)
            phase_steps(act, 1, phase2)
            phase_end(act, 3)

            act.activation(tmp_a[0:P, :], mv[0:P, :, 1], ACT.Sqrt, bias=eps_c[0:P, 1:2]).then_inc(ev("a_s3"), 1)
            wait(act, ev("v_s3"), 1)

            def norm_rows(t):
                wait(act, y_ld[t.s], t.j * 16 + 16)
                wait(act, tr, t.g * 2 - 2)
                for m in (0, 1):
                    last = act.activation(h3[0:P, t.s, m], y3[0:P, t.s, m], ACT.Identity,
                                          scale=s12[0:P, bass.ds(t.u * 2 + m, 1)], bias=nm12[0:P, bass.ds(t.u * 2 + m, 1)])
                last.then_inc(h_rows, 1)
            norm_rows(Step(2, 0, 0))
            copy_hT(Step(2, 0, 0), hT3)

            def phase3(t, last):
                if not last:
                    norm_rows(next_step(t))
                wait(act, m_mm, t.u)
                for i, bk in ((0, BA), (1, BB)):
                    wait(act, feat, t.g * 2 + i + 1)
                    for c in (2 * i, 2 * i + 1):
                        mm = act.activation(gT3[:, c, :], bk[:, (c % 2) * 250:(c % 2) * 250 + 250], ACT.Gelu,
                                            bias=m1b[:, c:c + 1])
                    mm.then_inc(feat_c, 1)
                if not last:
                    copy_hT(next_step(t), hT3)
            phase_steps(act, 2, phase3)
            phase_end(act, 4)

            wait(act, ev("pe_fc1"), 1)
            act.activation(fc1e.rearrange("p a b -> p (a b)"), BE[:, :], ACT.Copy, scale=0.5).then_inc(ev("a_fc1"), 1)

            def copy_accT(t):
                wait(act, accs_tr[t.s], t.j + 1)
                act.copy(accT[:, t.s].rearrange("p a b -> p (a b)"), (BF, BG)[t.s][:, 0:500]).then_inc(a_t_slot[t.s], 1)
            copy_accT(Step(0, 0, 0))

            def phase4(t, last):
                if not last:
                    wait(act, a_mm, t.u)
                    copy_accT(next_step(t))
            phase_steps(act, 0, phase4)
            phase_end(act, 5)

            act.activation(tmp_a[0:P, :], mv[0:P, :, 1], ACT.Sqrt, bias=eps_c[0:P, 0:1]).then_inc(ev("a_s4"), 1)
            wait(act, ev("v_s4"), 1)

            def odd(t):
                wait(act, x1_ld[t.s], t.j * 16 + 16)
                wait(act, llr, t.u)
                act.activation(xn4[0:P], z4[0:P, t.s, 1], ACT.Identity,
                               scale=s12[0:P, bass.ds(t.u * 2 + 1, 1)], bias=nms[0:P, bass.ds(t.u, 1)]).then_inc(xo, 1)

            def copy_llT(t):
                wait(act, ll_tr, t.u + 1)
                wait(act, f1, t.u)
                act.copy(llT.rearrange("p a b -> p (a b)"), BF[:, 0:2 * P]).then_inc(ll_t, 1)
            odd(Step(0, 0, 0))
            copy_llT(Step(0, 0, 0))

            def phase5(t, last):
                if not last:
                    odd(next_step(t))
                wait(act, f1, t.u + 1)
                wait(act, f2, t.u)
                for h in (0, 1):
                    mm = act.activation(gT4[:, h, :], BH[:, h * P:(h + 1) * P], ACT.Gelu, bias=f1b[:, h:h + 1])
                mm.then_inc(gl, 1)
                if not last:
                    copy_llT(next_step(t))
                wait(act, o_st[t.s], t.j * 16)
                for m in (0, 1):
                    mm = act.activation(o4[0:P, t.s, m], z4[0:P, t.s, m], ACT.Identity,
                                        scale=s1[0:P, bass.ds(t.u * 2 + m, 1)], bias=nm12[0:P, bass.ds(t.u * 2 + m, 1)])
                mm.then_inc(xu, 1)
            phase_steps(act, 0, phase5)

        @block.vector
        def _(dve):
            wait(dve, ev("counters_set"), 1)
            n_self = [0]

            def seq(inst):
                n_self[0] += 1
                inst.then_inc(dve_self, 1)
                wait(dve, dve_self, n_self[0])

            def ts(out, in0, a, op0, b=None, op1=ALU.bypass):
                seq(dve.tensor_scalar(out, in0, a, b, op0, op1))

            dve.memset(ones[:, :], 1.0)
            dve.memset(ones_h[:, :], 1.0)
            dve.memset(neg_half[:, :], -0.5)
            dve.memset(zero_row[:, :], 0.0)
            dve.memset(eps_c[:, 0:1], EPS1)
            seq(dve.memset(eps_c[:, 1:2], EPS2))
            seq(dve.memset(strip[0:P, :], 0.0))
            seq(dve.memset(strip[0:P, 49:50], 1.0))
            seq(dve.memset(strip[0:P, 113:114], 1.0))
            dve.drain().then_inc(ev("consts"), 1)
            wait(dve, e_in, 32)
            seq(dve.tensor_copy(src_f[0:P], src_i[0:P]))
            ts(blk_q[0:P], src_f[0:P], 1.0 / NT, ALU.mult, -0.49, ALU.add)
            ts(blk_q[0:P], blk_q[0:P], ROUND, ALU.add, ROUND, ALU.subtract)
            seq(dve.scalar_tensor_tensor(out=blk_h[0:P], in0=blk_q[0:P], scalar=-float(NT), in1=src_f[0:P],
                                         op0=ALU.mult, op1=ALU.add))
            for b in range(NT):
                last = dve.tensor_scalar(onehot(b), blk_h[0:P], float(b), None, ALU.is_equal)
            last.then_inc(ev("onehot"), 1)
            dve.tensor_copy(payload[0:P, :, 0], dst_i[0:P])
            dve.tensor_copy(payload[0:P, :, 1], blk_q[0:P])
            wait(dve, ev("pe_count"), 1)
            dve.tensor_copy(count[:, 0:EH], BA[:, 0:EH])
            seq(dve.tensor_copy(count[:, EH:EC], BB[:, 0:EH]))
            seq(dve.tensor_tensor_scan(incl[:, :], count[:, :], count[:, :], 0.0, ALU.add, ALU.max))
            ts(n_pairs[:, :], incl[:, EC - 1:EC], 1.0 / 256, ALU.mult, 255.0 / 256 - 0.5 + 1.0 / 512, ALU.add)
            ts(n_pairs[:, :], n_pairs[:, :], ROUND, ALU.add, ROUND, ALU.subtract)
            dve.drain().then_inc(ev("groups"), 1)
            wait(dve, ev("pe_base"), 1)
            seq(dve.tensor_copy(base[:, :], BC[:, 0:1]))
            seq(dve.tensor_tensor(end_g[:, :], base[:, :], n_pairs[:, :], ALU.add))
            wait(dve, c_in, 6 * 16)
            dve.tensor_scalar(past[:, :], iota_g[:, :], end_g[:, 0:1], None, ALU.is_ge).then_inc(ev("past"), 1)
            seq(dve.tensor_tensor(first[:, :], incl[:, :], count[:, :], ALU.subtract))
            ts(base[:, :], base[:, :], 256.0, ALU.mult)
            ts(first[:, :], first[:, :], base[:, 0:1], ALU.add)
            ts(count[:, :], first[:, :], 1.0 / 128, ALU.mult, -0.5 + 1.0 / 256, ALU.add)
            ts(count[:, :], count[:, :], ROUND, ALU.add, ROUND, ALU.subtract)
            dve.tensor_copy(first_h[0:64], count[0:64])
            seq(dve.scalar_tensor_tensor(out=first_h[64:128], in0=count[64:128], scalar=-128.0, in1=first[64:128],
                                         op0=ALU.mult, op1=ALU.add))
            dve.drain().then_inc(ev("first"), 1)
            wait(dve, ev("pe_tiles"), 1)
            seq(dve.tensor_scalar(pair_off[0:1, :], BD[0:1, 0:PAIRS], float(NT - 1), float(RW), ALU.min, ALU.mult))
            for b in range(NT):
                for h in (0, 1):
                    bk = (BA, BB, BF, BG)[b % 2 * 2 + h]
                    cols = slice(h * EH, (h + 1) * EH)
                    if b:
                        wait(dve, rank_used, 2 * b + h - 1)
                    wait(dve, rank_mm, 2 * b + h + 1)
                    dve.copy_predicated(pos[0:P, cols], onehot(b)[:, cols].bitcast(U16), bk[0:P, 0:EH]).then_inc(rank_used, 1)
            wait(dve, rank_used, 2 * NT)
            ts(src_f[0:P], pos[0:P], 1.0 / 128, ALU.mult, -0.5 + 1.0 / 256, ALU.add)
            ts(src_f[0:P], src_f[0:P], ROUND, ALU.add, ROUND, ALU.subtract)
            seq(dve.scalar_tensor_tensor(out=pos[0:P], in0=src_f[0:P], scalar=-128.0, in1=pos[0:P],
                                         op0=ALU.mult, op1=ALU.add))
            seq(dve.scalar_tensor_tensor(out=slot_of[0:P], in0=pos[0:P], scalar=float(GROUPS), in1=src_f[0:P],
                                         op0=ALU.mult, op1=ALU.add))
            dve.drain().then_inc(ev("slots"), 1)

            wait(dve, w_in, 16 * 16)
            for k in range(KC):
                dve.tensor_copy(vb4[:, k, :], n1b[:, k:k + 1].to_broadcast([128, 128]))
            dve.drain().then_inc(ev("bias_in"), 1)
            wait(dve, ev("pe_bias"), 1)
            dve.tensor_tensor(kqb[:, :], kqb[:, :], BC[:, 0:2 * KC], ALU.add)
            seq(dve.tensor_tensor(bv_bc[:, :], bv_bc[:, :], BD[:, :], ALU.add))
            dve.tensor_tensor(bvp_bc[:, :], bvp_bc[:, :], bv_bc[:, :], ALU.add)
            for k in range(KC):
                dve.tensor_scalar(kqv_w[:, k, :], kqv_w[:, k, :], n1g[:, k:k + 1], None, ALU.mult)
            dve.memset(acc[0:P, :, HID:RW], 1.0)
            wait(dve, ev("a_s1"), 1)
            seq(dve.reciprocal(s1[0:P, :], tmp_a[0:P, :]))
            ts(tmp_b[0:P, :], ssq[0:P, :], 1.0 / D, ALU.mult)
            seq(dve.tensor_tensor(tmp_b[0:P, :], tmp_b[0:P, :], s1[0:P, :], ALU.mult))
            seq(dve.tensor_tensor(tmp_b[0:P, :], tmp_b[0:P, :], s1[0:P, :], ALU.mult))
            dve.drain().then_inc(ev("v_var2"), 1)
            wait(dve, ev("a_s2"), 1)
            seq(dve.reciprocal(s12[0:P, :], rs2[0:P, :]))
            seq(dve.tensor_tensor(s12[0:P, :], s12[0:P, :], s1[0:P, :], ALU.mult))
            seq(dve.tensor_tensor(nm12[0:P, :], nmean[0:P, :], s12[0:P, :], ALU.mult))
            phase_end(dve, 1)

            class Chain:

                def __init__(self, s, per):
                    self.sem, self.per = s, per

                def start(self, t):
                    self.t, self.n = t, 0

                def __call__(self, inst):
                    self.n += 1
                    inst.then_inc(self.sem, 1)

                def wait(self):
                    wait(dve, self.sem, self.t.u * self.per + self.n)

            def next_step(t):
                return Step(t.phase, t.j, 1) if t.s == 0 else Step(t.phase, t.j + 1, 0)

            def norm_rows(t):
                wait(dve, x_ld[t.s], t.uses() * 16 + 16)
                for m in (0, 1):
                    last = dve.tensor_scalar(hh[0:P, t.s, m], x_in[0:P, t.s, m], s12[0:P, bass.ds(t.u * 2 + m, 1)],
                                             nm12[0:P, bass.ds(t.u * 2 + m, 1)], ALU.mult, ALU.add)
                last.then_inc(h_rows, 1)

            def square_sums(t, own):
                wait(dve, feat_c, t.g * 2 + 2)
                flat = lambda v: v.rearrange("p a b -> p (a b)")
                own(dve.tensor_tensor(flat(sq), flat(kT), flat(kT), ALU.mult))
                own.wait()
                own(dve.tensor_tensor(flat(sqa), flat(sq[:, 0:2]), flat(sq[:, 2:4]), ALU.add))
                own.wait()
                wait(dve, xd, t.g)
                dve.tensor_tensor(sqb[:, :], sqa[:, 0], sqa[:, 1], ALU.add).then_inc(sqs, 1)

            own1 = Chain(dve_own[0], 2)
            dve.memset(kps[0:P], 0.0)
            norm_rows(Step(0, 0, 0))

            def phase1(t, last):
                own1.start(t)
                if not last:
                    wait(dve, hk_mm, t.u)
                    norm_rows(next_step(t))
                square_sums(t, own1)
                for m, bk in ((0, BH), (1, BA)):
                    wait(dve, r_mm, t.u * 2 + m + 1)
                    dve.scalar_tensor_tensor(out=rt[0:P, m], in0=bk[0:P, 0:HID], scalar=rs2[0:P, bass.ds(t.u * 2 + m, 1)],
                                             in1=b1_bc[0:P, :], op0=ALU.mult, op1=ALU.add).then_inc(r_up, 1)
                wait(dve, r_up, t.u * 2 + 2)
                dve.tensor_scalar(acc[0:P, bass.ds(t.u * 2, 2), 0:HID], rt[0:P], 0.0, None, ALU.max).then_inc(r_ok, 1)
                wait(dve, ex, t.g * 2 + 2)
                wait(dve, kadd, t.u)
                dve.tensor_tensor(kps[0:P], kps[0:P], kp[0:P], ALU.add).then_inc(kadd, 1)
            phase_steps(dve, 0, phase1)

            wait(dve, ev("pe_ksum"), 1)
            for i, bk in ((0, BC), (1, BD)):
                dve.tensor_copy(hk[:, 2 * i:2 * i + 2, :].rearrange("p a b -> p (a b)"), bk[:, :])
            dve.tensor_copy(ks_bc[:, :], BE[:, 0:M])
            dve.drain().then_inc(ev("hk"), 1)
            wait(dve, ev("pe_kptv"), 1)
            for i, bk in ((0, BA), (1, BB)):
                dve.tensor_copy(kptv[:, 2 * i:2 * i + 2, :].rearrange("p a b -> p (a b)"), bk[:, :])
            dve.drain().then_inc(ev("kptv"), 1)
            wait(dve, ev("pe_pmat"), 1)
            for m, bk in ((0, BF), (1, BH)):
                dve.tensor_copy(pmat[:, m, :], bk[:, :])
            wait(dve, ev("pe_mbias"), 1)
            dve.tensor_tensor(m1b[:, :], m1b[:, :], BG[:, 0:KC], ALU.add)
            for k in range(KC):
                dve.tensor_scalar(mlp1_w[:, k, :], mlp1_w[:, k, :], n2g[:, k:k + 1], None, ALU.mult)
            phase_end(dve, 2)

            def row_stats(rows_sb, t, own):
                for m in (0, 1):
                    own(dve.bn_stats(stat6[0:P, m, :], rows_sb[:, m, :]))
                own.wait()
                own(dve.tensor_scalar(tiny[0:1, 0:1], stat6[0:1, 0, 0:1], 1.0, None, ALU.mult))
                for m in (0, 1):
                    own(dve.bn_aggr(mvs[0:P, m, :], stat6[0:P, m, :]))
                own.wait()
                return dve.tensor_copy(mv[0:P, bass.ds(t.u * 2, 2), :], mvs[0:P])

            own2 = Chain(dve_own[1], 13)
            norm_rows(Step(1, 0, 0))

            def phase2(t, last):
                own2.start(t)
                if not last:
                    wait(dve, tr, t.g * 2)
                    norm_rows(next_step(t))
                square_sums(t, own2)
                for m in (0, 1):
                    wait(dve, ex, t.g * 2 + m + 1)
                    own2(dve.scalar_tensor_tensor(out=junk[0:P, m], in0=kp[0:P, m], scalar=1.0, in1=ks_bc[0:P, :],
                                                  op0=ALU.mult, op1=ALU.mult, accum_out=den[0:P, m:m + 1]))
                own2.wait()
                own2(dve.tensor_scalar(den[0:P, :], den[0:P, :], 256.0 * EPS_ATTN, None, ALU.add))
                own2.wait()
                own2(dve.reciprocal(rden[0:P, :], den[0:P, :]))
                own2.wait()
                wait(dve, qt, t.u)
                for m in (0, 1):
                    mm = dve.tensor_scalar(qpn[0:P, m], kp[0:P, m], rden[0:P, m:m + 1], None, ALU.mult)
                mm.then_inc(qn, 1)
                wait(dve, y_mm, t.u + 1)
                wait(dve, y_st[t.s], t.j * 16)
                for m, bk in ((0, BC), (1, BD)):
                    own2(dve.tensor_tensor(y_out[0:P, t.s, m], bk[0:P, :], bvp_bc[0:P, :], ALU.add))
                own2.wait()
                row_stats(y_out[0:P, t.s], t, own2).then_inc(y_ok, 1)
            phase_steps(dve, 1, phase2)
            phase_end(dve, 3)

            def scales(root_done, eps_name):
                wait(dve, ev(root_done), 1)
                seq(dve.reciprocal(s12[0:P, :], tmp_a[0:P, :]))
                seq(dve.scalar_tensor_tensor(out=nm12[0:P, :], in0=mv[0:P, :, 0], scalar=-1.0, in1=s12[0:P, :],
                                             op0=ALU.mult, op1=ALU.mult))

            scales("a_s3", None)
            dve.drain().then_inc(ev("v_s3"), 1)
            own3 = Chain(dve_own[2], 2)

            def step_lanes(t, n=SP):
                wait(dve, idx_in[t.s], t.j * 16 + 16)
                dve.tensor_copy(lane_f[:, t.s, 0:2 * n], idx[:, t.s, 0:2 * n, 1]).then_inc(lanes, 1)

            def one_hots(t, k, n=PB):
                wait(dve, lanes, t.u + 1)
                wait(dve, ring_free[k], t.u)
                dve.tensor_tensor(hit[k][:, 0:2 * n, :], iota_p.unsqueeze(1).to_broadcast([128, 2 * n, P]),
                                  lane_f[:, t.s, k * 2 * PB:(k * PB + n) * 2].unsqueeze(2).to_broadcast([128, 2 * n, P]),
                                  ALU.is_equal).then_inc(hits, 1)

            def add_groups(t, k, n):
                i = t.s * BATCHES + k
                first_pair = t.j * (2 * SP) + i * PB
                _, offs = nc.values_load_multi_w_load_instructions(
                    pair_off[0:1, bass.ds(first_pair, n)], engines=[mybir.EngineType.DVE],
                    min_val=0, max_val=(NT - 1) * RW)
                flat_acc = ACC[0:P, :]
                for g in range(n):
                    at = i * PB + g
                    wait(dve, g_mm, first_pair + g + 1)
                    wait(dve, g_add[1 - at % 2], t.j * SP + (at + 1) // 2)
                    dst = flat_acc[:, bass.ds(offs[g], RW)]
                    dve.tensor_tensor(dst, dst, (BE, BH)[at % 2][0:P, 0:RW], ALU.add).then_inc(g_add[at % 2], 1)

            step_lanes(Step(2, 0, 0))
            one_hots(Step(2, 0, 0), 0)

            def phase3(t, last):
                own3.start(t)
                batches = LAST_BATCHES if last else [PB] * BATCHES
                wait(dve, x_ld[t.s], t.uses() * 16 + 16)
                wait(dve, y_ld[t.s], t.j * 16 + 16)
                wait(dve, z_st[t.s], t.j * 16)
                dve.tensor_tensor(z3[0:P, t.s], x3[0:P, t.s], y3[0:P, t.s], ALU.add).then_inc(zadd, 1)
                wait(dve, zadd, t.u + 1)
                own3(dve.tensor_tensor(z3[0:P, t.s], z3[0:P, t.s], mb2_bc[0:P, :].unsqueeze(1).to_broadcast([P, 2, D]),
                                       ALU.add))
                one_hots(t, 1, batches[1])
                add_groups(t, 0, batches[0])
                if not last:
                    one_hots(t, 2)
                own3.wait()
                wait(dve, m_mm, t.u + 1)
                for m, bk in ((0, BC), (1, BD)):
                    mm = dve.tensor_tensor(z3[0:P, t.s, m], z3[0:P, t.s, m], bk[0:P, :], ALU.add)
                    if m == 0:
                        own3(mm)
                mm.then_inc(z_ok, 1)
                add_groups(t, 1, batches[1])
                if not last:
                    after = next_step(t)
                    step_lanes(after)
                    one_hots(after, 0)
                    add_groups(t, 2, PB)
            phase_steps(dve, 2, phase3)
            phase_end(dve, 4)

            own4 = Chain(dve_own[3], 7)

            def phase4(t, last):
                own4.start(t)
                wait(dve, z_ld[t.s], t.j * 16 + 16)
                wait(dve, a_cp, t.u + 1)
                for m in (0, 1):
                    mm = dve.scalar_tensor_tensor(out=z4[0:P, t.s, m], in0=b2_bc[0:P, :],
                                                  scalar=accs[0:P, t.s, m, HID:RW], in1=z4[0:P, t.s, m],
                                                  op0=ALU.mult, op1=ALU.add)
                mm.then_inc(accs_deg[t.s], 1)
                wait(dve, accs_deg[t.s], t.j + 1)
                wait(dve, a_mm, t.u + 1)
                wait(dve, x1_st[t.s], t.j * 16)
                for m in (0, 1):
                    bk = ((BC, BD), (BA, BB))[t.s][m]
                    own4(dve.tensor_tensor(x4[0:P, t.s, m], z4[0:P, t.s, m], bk[0:P, :], ALU.add))
                own4.wait()
                row_stats(x4[0:P, t.s], t, own4).then_inc(x1_ok[t.s], 1)
            phase_steps(dve, 0, phase4)
            phase_end(dve, 5)

            scales("a_s4", None)
            dve.tensor_scalar(s1[0:P, :], s12[0:P, :], 1.0, None, ALU.add)
            pairs = nm12[0:P, :].rearrange("p (u m) -> p u m", m=2)
            dve.tensor_tensor(nms[0:P, :], pairs[:, :, 0], pairs[:, :, 1], ALU.add)
            dve.tensor_scalar(fb2_bc[:, :], fb2_bc[:, :], 0.5, None, ALU.mult)
            dve.drain().then_inc(ev("v_s4"), 1)
            own5 = Chain(dve_own[4], 2)

            def ll_rows(t, own):
                wait(dve, xo, t.u + 1)
                own(dve.scalar_tensor_tensor(out=t4[0:P, 0], in0=z4[0:P, t.s, 0], scalar=s12[0:P, bass.ds(t.u * 2, 1)],
                                             in1=xn4[0:P], op0=ALU.mult, op1=ALU.add))
                own.wait()
                cols = t4[0:P, 0].rearrange("p (c m) -> p c m", m=2)
                wait(dve, ll_tr, t.u)
                dve.tensor_tensor(ll[0:P, t.s], cols[:, :, 0], cols[:, :, 1], ALU.add).then_inc(llr, 1)

            class Once:
                def __call__(self, inst):
                    seq(inst)

                def wait(self):
                    pass
            ll_rows(Step(0, 0, 0), Once())

            def phase5(t, last):
                own5.start(t)
                if not last:
                    ll_rows(next_step(t), own5)
                wait(dve, llr, t.u + 1)
                own5(dve.scalar_tensor_tensor(out=quarter[0:P, 0], in0=ll[0:P, t.s], scalar=-0.25, in1=fb2_bc[0:P, :],
                                              op0=ALU.mult, op1=ALU.add))
                own5.wait()
                wait(dve, f2, t.u + 1)
                dve.scalar_tensor_tensor(out=dlt[0:P, 0], in0=BC[0:P, 0:HL], scalar=0.5, in1=quarter[0:P, 0],
                                         op0=ALU.mult, op1=ALU.add).then_inc(dl, 1)
                wait(dve, dl, t.u + 1)
                wait(dve, xu, t.u + 1)
                for m in (0, 1):
                    o = o4[0:P, t.s, m].rearrange("p (c m) -> p c m", m=2)
                    mm = dve.tensor_tensor(o, o, dlt[0:P, 0].unsqueeze(2).to_broadcast([P, HL, 2]), ALU.add)
                mm.then_inc(o_ok, 1)
            phase_steps(dve, 0, phase5)


IN_SHAPES = {
    "x": (N, D), "src": (E,), "dst": (E,), "L0_gnn_W1": (D, HID), "L0_gnn_b1": (HID,), "L0_gnn_W2": (HID, D),
    "L0_gnn_b2": (D,), "L0_mix_kqv_w": (D, 3 * D), "L0_mix_kqv_b": (3 * D,), "L0_mix_proj_w": (D, D),
    "L0_mix_proj_b": (D,), "L0_mix_n1_g": (D,), "L0_mix_n1_b": (D,), "L0_mix_n2_g": (D,), "L0_mix_n2_b": (D,),
    "L0_mix_mlp_w1": (D, D), "L0_mix_mlp_b1": (D,), "L0_mix_mlp_w2": (D, D), "L0_mix_mlp_b2": (D,),
    "L0_ffn_fc1_b": (HL,), "L0_ffn_fc2_b": (HL,),
}


def shape_constants():
    k = np.arange(128)
    c = {
        "less": (np.arange(P)[:, None] < np.arange(P)[None, :]).astype(np.float16),
        "upper": ((k[:, None] < NT) & (k[:, None] < (k[None, :] % 64))).astype(np.float32),
        "iota_g": np.tile(np.arange(PAIRS, dtype=np.float32), (128, 1)),
        "iota_p": np.tile(np.arange(P, dtype=np.float32), (128, 1)),
        "ident": np.eye(128, dtype=np.float32),
        "blank": np.tile(np.array([0, 128], np.int32), GROUPS),
    }
    weight = np.where(k < 64, 128, 1)[:, None] * ((k % 64)[:, None] == np.arange(NT)[None, :])
    c["pick"] = np.broadcast_to(weight[:, :, None], (128, NT, P)).astype(np.float16)
    at = np.linspace(0.0, 1.0, D, dtype=np.float32) * np.float32(D // 2 - 1)
    low = np.clip(np.floor(at).astype(np.int32), 0, D // 2 - 2)
    w = at - low.astype(np.float32)
    interp = np.zeros((D, D // 2), np.float32)
    interp[np.arange(D), low] = np.float32(1) - w
    interp[np.arange(D), low + 1] += w
    c["interp"] = interp
    return {"c_" + name: np.ascontiguousarray(v) for name, v in c.items()}


def kernel(**inputs):
    import concourse.bacc as bacc
    from concourse.bass_utils import run_bass_kernel_spmd

    arrays = {name: np.ascontiguousarray(inputs[name]) for name in IN_SHAPES}
    arrays["w_t"] = np.ascontiguousarray(np.asarray(inputs["L0_mix_w"]).T)
    arrays["fc1_t"] = np.ascontiguousarray(np.asarray(inputs["L0_ffn_fc1_w"]).T)
    arrays["fc2_t"] = np.ascontiguousarray(np.asarray(inputs["L0_ffn_fc2_w"]).T)
    arrays.update(shape_constants())
    nc = bacc.Bacc("TRN2", target_bir_lowering=False, num_devices=1)
    d = {name: nc.dram_tensor(name, a.shape, mybir.dt.from_np(a.dtype), kind="ExternalInput").ap()
         for name, a in arrays.items()}
    d["out"] = nc.dram_tensor("out", (N, D), F32, kind="ExternalOutput").ap()
    build_program(nc, d)
    result = run_bass_kernel_spmd(nc, [arrays], core_ids=[0])
    return result.results[0]["out"]
```

```python
from contextlib import ExitStack

import numpy as np
import concourse.bass as bass
from concourse import mybir

F32, F32R, F16, I32, U16 = mybir.dt.float32, mybir.dt.float32r, mybir.dt.float16, mybir.dt.int32, mybir.dt.uint16
ALU, ACT = mybir.AluOpType, mybir.ActivationFunctionType

N, D, E = 6250, 512, 100000
P, NT = 125, 50
STEPS = NT // 2
HID, M, HL = 256, 256, 256
KC, KH = D // 128, HID // 128
RW = HID + 1
EC = E // P
EH = EC // 2
PAIRS = (E + NT * 255) // 256
GROUPS = 2 * PAIRS
SG = 20
PB, BATCHES = 6, 3
SP = PB * BATCHES
LAST = PAIRS - SP * (STEPS - 1)
LAST_BATCHES = [min(PB, LAST - i) for i in range(0, LAST, PB)]
ROUND = 12582912.0
WK, WR, WKW = 0, D, D + HID
WQ, WV, WQW = 0, D, 2 * D
EPS1, EPS2, EPS_ATTN = 1e-5, 1e-3, 1e-8
assert 0 < LAST <= SP and EC % (4 * SG) == 0


class Step:

    def __init__(self, phase, j, s):
        self.phase, self.j, self.s = phase, j, s
        self.u = j * 2 + s
        self.g = self.u + 25 * phase

    def uses(self, s=None):
        s = self.s if s is None else s
        return self.j + (13 - s) * self.phase


def phase_steps(eng, phase, emit):
    with eng.Fori(0, STEPS // 2) as j:
        emit(Step(phase, j, 0), False)
        emit(Step(phase, j, 1), False)
    emit(Step(phase, STEPS // 2, 0), True)


def phase_steps_ahead(eng, phase, emit):
    with eng.Fori(0, STEPS // 2 - 1) as j:
        emit(Step(phase, j, 0), True, False)
        emit(Step(phase, j, 1), True, False)
    emit(Step(phase, STEPS // 2 - 1, 0), True, False)
    emit(Step(phase, STEPS // 2 - 1, 1), False, False)
    emit(Step(phase, STEPS // 2, 0), False, True)


def build_program(nc, d):
    ctx = ExitStack()
    with ctx:
        def sb(name, words, dt=F32):
            return ctx.enter_context(nc.sbuf_tensor("sb_" + name, [128, words], dt))

        def new_sem(name):
            return ctx.enter_context(nc.semaphore("s_" + name))

        events, counters = {}, []

        def sem(name):
            counters.append(new_sem(name))
            return counters[-1]

        def wait(eng, s, n):
            if not (isinstance(n, int) and n == 0):
                eng.wait_ge(s, n + 1 if any(s is c for c in counters) else n)

        def ev(name):
            if name not in events:
                events[name] = new_sem("ev_" + name)
            return events[name]

        ACC = sb("acc", NT * RW)
        EDGE_WORDS, LATE_WORDS, ATT_WORDS = 3 * EC + 6 * SG + 40, 2 * KC * (D + HID + M), 2 * KC * (2 * D + M)
        with ExitStack() as shared:
            WEIGHTS, STEP, CONST = (shared.enter_context(nc.sbuf_tensor("sb_" + name, [128, words], F32)) for name, words in (
                ("weights", LATE_WORDS + EDGE_WORDS + ATT_WORDS), ("step", 12424), ("const", 6850)))
        XT_WORDS = 2 * KC * 2 * P
        W1_PARTS = sb("w1_parts", LATE_WORDS)
        sb("edge_part", EDGE_WORDS)
        W2_PARTS = sb("w2_parts", ATT_WORDS)
        XH, XL = sb("x_high", XT_WORDS), sb("x_low", XT_WORDS)
        sb("others", 12424 + 6850 - 2 * XT_WORDS)
        LATE = WEIGHTS[:, 0:LATE_WORDS]
        EDGE = WEIGHTS[:, LATE_WORDS:LATE_WORDS + EDGE_WORDS]
        ATT = WEIGHTS[:, LATE_WORDS + EDGE_WORDS:]

        def carver(region):
            at = [0]

            def take(*shape, dt=F32):
                n = int(np.prod(shape))
                words = n if dt in (F32, I32) else (n + 1) // 2
                v = region[:, at[0]:at[0] + words]
                at[0] += (words + 7) // 8 * 8
                assert at[0] <= region.shape[1] + 7, (at[0], region.shape)
                if dt is not F32:
                    v = v.bitcast(dt)
                    if dt is F16:
                        v = v[:, 0:n]
                if len(shape) == 2:
                    v = v.rearrange("p (a b) -> p a b", b=shape[1])
                elif len(shape) == 3:
                    v = v.rearrange("p (a b c) -> p a b c", b=shape[1], c=shape[2])
                return v
            return take

        acc = ACC[:, :].rearrange("p (t f) -> p t f", f=RW)
        onehot_a = ACC[:, 0:32 * EC // 2].bitcast(F16).rearrange("p (b j) -> p b j", j=EC)
        w1_parts = W1_PARTS[:, :].rearrange("p (h c n) -> p h c n", h=2, c=KC)
        w2_parts = W2_PARTS[:, :].rearrange("p (h c n) -> p h c n", h=2, c=KC)
        raw_a, raw_b = carver(ATT), carver(ACC)
        k_raw, kt_raw, gnn1_raw, wt_a = raw_a(KC, D), raw_a(KC, D), raw_a(KC, HID), raw_a(KC, M)
        xs = raw_a(2, 2, D)
        q_raw, v_raw, qt_raw, wt_b = raw_b(KC, D), raw_b(KC, D), raw_b(KC, D), raw_b(KC, M)
        folded_k, folded_q, vb_k, vb_q = raw_b(KC, M), raw_b(KC, M), raw_b(KC, 128), raw_b(KC, 128)
        ring_at = carver(WEIGHTS[:, LATE_WORDS:])
        ring = ring_at(BATCHES * 2 * PB, RW).rearrange("p (h k) f -> p h k f", h=BATCHES)
        hit_last, hT3 = ring_at(2 * PB, P), ring_at(2, KC, 2 * P)
        late = carver(LATE)
        proj_w, mlp1_w, mlp2_w = late(KC, D), late(KC, D), late(KC, D)
        gnn2_w, fc1e, fc2_w = late(KH, D), late(2, HL), late(2, HL)
        onehot_b = LATE[:, 0:18 * EC // 2].bitcast(F16).rearrange("p (b j) -> p b j", j=EC)

        def onehot(b):
            return onehot_a[0:P, b] if b < 32 else onehot_b[0:P, b - 32]

        edge = carver(EDGE)
        slot_of, payload = edge(EC, dt=I32), edge(EC, 2, dt=I32)
        stage_slot, stage_pay = edge(2, SG, dt=I32), edge(2, 2 * SG, dt=I32)

        const = carver(CONST)
        ident = const(128)
        pmat = const(KH, D)
        b1_bc, bv_bc, bvp_bc, mb2_bc, b2_bc, fb2_bc = (
            const(HID), const(D), const(D), const(D), const(D), const(HL))
        bk_bc, bkw_bc, bq_bc, bqw_bc = pmat[:, 0], pmat[:, 1, 0:M], mb2_bc, b2_bc[:, 0:M]
        ones = const(128)
        neg_half = const(1)
        eps_c = const(2)
        n1g, n1b, n2g, n2b = const(KC), const(KC), const(KC), const(KC)
        kqb, m1b, f1b, mean_w = const(2 * KC), const(KC), const(2), const(128)
        iota_p = const(P)
        pair_off = const(PAIRS, dt=I32)
        sum_x, nmean, ssq = const(NT), const(NT), const(NT)
        s1, s12, sinv12, nm12, tmp_a, tmp_b = (const(NT) for _ in range(6))
        mv = const(NT, 2)
        stat6 = const(2, 6)
        less = const(P, dt=F16)
        strip = const(178, dt=F16)
        ones_h = const(2, dt=F16)
        upper = const(128)
        n_pairs, base, end_g = const(1), const(1), const(1)
        ks_bc = const(M)
        zero_row = const(512)
        mvs, tiny, quiet, pool_tiny = const(2, 2), const(1), const(2), const(2)

        s0 = carver(STEP)
        src_i, dst_i, src_f, blk_q, blk_h = (
            s0(EC, dt=I32), s0(EC, dt=I32), s0(EC), s0(EC), s0(EC, dt=F16))
        count, incl, first, first_h, pos = s0(EC), s0(EC), s0(EC), s0(EC, dt=F16), s0(EC)
        pick = s0(NT, P, dt=F16)
        iota_g, past = s0(PAIRS), s0(PAIRS, dt=F16)
        vb4 = s0(KC, 128)
        s1_ = carver(STEP)
        s1_(2, KC, 2 * P)
        xt = s1_(2, KC, 2 * P)
        xh, xl = (v[:, :].rearrange("p (s c r) -> p s c r", s=2, c=KC) for v in (XH, XL))
        x_in = s1_(2, 2, D)
        y_out = x_in
        kk, kw, kp, kpn, kps, rt = s1_(2, D), s1_(2, M), s1_(2, M), s1_(2, M), s1_(2, M), s1_(2, HID)
        hsq, nxd, den, rden = s1_(2), s1_(2), s1_(2), s1_(2)
        junk, qpT = s1_(2, M), s1_(KH, 2 * P)
        hk, kptv = x_in[:, 0].rearrange("p a (b c) -> p (a b) c", c=M), x_in[:, 1].rearrange("p a (b c) -> p (a b) c", c=M)
        s3_ = carver(STEP)
        x3, y3, h3, z3 = s3_(2, 2, D), s3_(2, 2, D), s3_(2, 2, D), s3_(2, 2, D)
        gT3 = s3_(KC, 2 * P)
        hit = [s3_(2 * PB, P), s3_(2 * PB, P), hit_last]
        idx, lane_f = s3_(2, 2 * SP, 2, dt=I32), s3_(2, 2 * SP)
        s4_ = carver(STEP)
        z4, x4, accs, accT = s4_(2, 2, D), s4_(2, 2, D), s4_(2, 2, RW), s4_(2, KH, 2 * P)
        t4, ll, llT, gT4, xn4 = s4_(D), s4_(2, HL), s4_(2, P), s4_(2, P), s4_(D)
        dlt, dlm, quarter, o4 = s4_(HL), s4_(2, HL), s4_(HL), s4_(2, 2, D)
        ve, rs, up, nm4, mv4 = s4_(2, 2), s4_(2, 2), s4_(2, 2), s4_(2, 2), s4_(2, 2, 2)
        nms, minus_half = s4_(2), s4_(2)
        interp, fc1_t = (o4[:, h].rearrange("p a (b c) -> p (a b) c", c=HL) for h in (0, 1))

        bank = [ctx.enter_context(nc.psum_tensor(f"bank{i}", [128, 512], F32)) for i in range(8)]
        BA, BB, BC, BD, BE, BF, BG, BH = bank

        def rows(t):
            return t.rearrange("(p t) f -> p t f", t=NT)

        x_d, out_d = rows(d["x"]), rows(d["out"])
        table = nc.dram_tensor("hidden_rows", [N, RW], F32).ap()
        y_d = nc.dram_tensor("y_rows", [N, D], F32).ap()
        z_d = nc.dram_tensor("z_rows", [N, D], F32).ap()
        sorted_d = nc.dram_tensor("sorted_edges", [128 * GROUPS, 2], I32).ap()
        sorted_v = sorted_d.rearrange("(p g) e -> p g e", g=GROUPS)
        chunks = lambda t: t.rearrange("(c p) n -> p c n", p=128)
        kqv = chunks(d["L0_mix_kqv_w"])
        col = lambda t: t.rearrange("(c p) -> p c", p=128)

        all_engines = sem("phase_end")
        pair = lambda name: [sem(name + "0"), sem(name + "1")]
        e_in, c_in, w2_in, v_in, proj_in, late_in, rows_in = (sem(n) for n in (
            "edges_in", "sort_consts_in", "weights2_in", "v_weights_in", "proj_in", "late_in", "late_rows_in"))
        w_in, prefill = new_sem("weights_in"), new_sem("blank_slots")
        xs_in, x_ld, xt_ld, x3_ld, y_ld, z_ld = (pair(n) for n in (
            "stat_x_in", "x_in", "xT_in", "x3_in", "y_in", "z_in"))
        r_st, y_st, z_st, o_st = (sem("r_stored"), *(pair(n) for n in ("y_stored", "z_stored", "out_stored")))
        idx_in = pair("idx_in")
        scattered = [new_sem(f"scattered{s}") for s in range(2)]
        gathered = [new_sem(f"gathered{k}") for k in range(BATCHES)]
        st_sum, st_mean, st_free = sem("stat_sums"), sem("stat_means"), sem("stat_x_used")
        onehots = sem("onehots")
        rank_mm, rank_used, staged = sem("rank_products"), sem("ranks_used"), sem("scatter_staged")
        split, k_mm, k_ok, w_mm, w_ok, sq, ex, nx, v_mm = (sem(n) for n in (
            "x_split", "kq_products", "kq_rows", "kqw_products", "kqw_rows", "kq_squared", "exps",
            "square_sums", "v_products"))
        (h_rows, tr, h_t, feat, feat_c, r_up, r_ok, kadd, hk_mm, qn, qt, qtc,
         y_mm, zadd, z_ok, m_mm, hits, g_mm) = (sem(n) for n in (
            "h_rows", "h_transposed", "hT", "features", "features_copied", "r_read", "r_rows", "kp_added",
            "hk_products", "q_scaled", "q_transposed", "qT", "y_products", "z_sums", "z_rows",
            "mlp2_products", "one_hots", "group_products"))
        g_add, lanes = pair("group_added"), sem("lanes")
        ring_free = [sem(f"ring_used{k}") for k in range(BATCHES)]
        a_cp, a_t, a_mm = sem("acc_staged"), sem("accT"), sem("w2_products")
        y_ok = pair("y_rows")
        accs_tr, accs_deg, x1_ok = pair("acc_stage_transposed"), pair("degrees_used"), pair("x1_rows")
        var_ok, rs_ok, sc_ok, llr, ll_tr, ll_t, f1, gl, f2, dl, dm, xu, o_ok = (sem(n) for n in (
            "x1_variances", "x1_inverse_roots", "x1_scales", "ll_rows", "ll_transposed", "llT", "fc1",
            "gelu", "fc2", "delta", "delta_shifted", "x1_scaled", "out_rows"))

        def phase_end(eng, n):
            eng.drain().then_inc(all_engines, 1)
            wait(eng, all_engines, 4 * n)

        ev_fc = sem("fc_in")
        dve_self, pool_self = sem("dve_self"), sem("pool_self")
        dve_own = [sem(f"dve_own{i}") for i in range(4)]

        block = ctx.enter_context(nc.Block())

        @block.sync
        def _(sp):
            for c in counters:
                sp.sem_inc(c, 1)
            sp.sem_inc(ev("counters_set"), 1)
            sp.dma_start(src_i[0:P], d["src"].rearrange("(p j) -> p j", p=P)).then_inc(e_in, 16)
            sp.dma_start(dst_i[0:P], d["dst"].rearrange("(p j) -> p j", p=P)).then_inc(e_in, 16)
            for t, s in ((less[0:P], "less"), (upper[:, :], "upper"), (pick[:, :, :], "pick"),
                         (iota_g[:, :], "iota_g"), (iota_p[:, :], "iota_p"), (ident[:, :], "ident")):
                sp.dma_start(t, d["c_" + s]).then_inc(c_in, 16)
            def stat_load(j, s):
                sp.dma_start(xs[0:P, s], x_d[:, bass.ds(j * 4 + 2 * s, 2), :]).then_inc(xs_in[s], 16)

            def stat_step(t, more):
                if more:
                    after = t.j + 1
                    wait(sp, st_free, t.u + 1)
                    stat_load(after, t.s)
            stat_load(0, 0)
            stat_load(0, 1)
            sorted_at = 9
            with sp.Fori(0, sorted_at) as j:
                stat_step(Step(0, j, 0), True)
                stat_step(Step(0, j, 1), True)
            wait(sp, ev("slots1"), 1)
            for t, s in ((q_raw, kqv[:, :, D:2 * D]), (qt_raw, chunks(d["kq_t"][D:2 * D, :])),
                         (wt_b, chunks(d["w_t"]))):
                sp.dma_start(t, s).then_inc(w2_in, 16)
            sp.dma_start(v_raw, kqv[:, :, 2 * D:3 * D]).then_inc(v_in, 16)
            with sp.Fori(sorted_at, STEPS // 2 - 1) as j:
                stat_step(Step(0, j, 0), True)
                stat_step(Step(0, j, 1), True)
            stat_step(Step(0, STEPS // 2 - 1, 0), True)
            for t, s in ((fb2_bc, d["L0_ffn_fc2_b"].partition_broadcast(128)), (n2g, col(d["L0_mix_n2_g"])),
                         (n2b, col(d["L0_mix_n2_b"])), (m1b, col(d["L0_mix_mlp_b1"])), (f1b, col(d["L0_ffn_fc1_b"]))):
                sp.dma_start(t[:], s, allow_slow_non_contiguous=True).then_inc(rows_in, 16)
            phase_end(sp, 1)

            def load_rows(j, s):
                sp.dma_start(x_in[0:P, s], x_d[:, bass.ds(j * 4 + 2 * s, 2), :]).then_inc(x_ld[s], 16)

            def load_xt(j, s):
                sp.dma_start(xt[:, s].rearrange("p a b -> p (a b)"),
                             d["x_t"][:, bass.ds(j * (2 * KC * 2 * P) + s * (KC * 2 * P), KC * 2 * P)]).then_inc(xt_ld[s], 16)

            def attention_io(phase, before, store):
                def step(t, more, last):
                    before(t, more, t.j + 1)
                    store(t)
                phase_steps_ahead(sp, phase, step)

            def next_inputs1(t, more, after):
                if more:
                    wait(sp, w_mm, t.g * 2 + 2)
                    load_xt(after, t.s)
                    wait(sp, hk_mm, t.u + 1)
                    load_rows(after, t.s)

            def load_idx(j, s, n=2 * SP):
                sp.dma_start(idx[:, s, 0:n], sorted_v[:, bass.ds(j * (4 * SP) + s * (2 * SP), n), :]
                             ).then_inc(idx_in[s], 16)

            def next_inputs2(t, more, after):
                if more:
                    wait(sp, v_mm, t.u + 1)
                    load_xt(after, t.s)
                elif t.s == 1:
                    for s in (0, 1):
                        wait(sp, scattered[s], 16 * EC // 2)
                    load_idx(0, 0)
                    load_idx(0, 1)
            for s in (0, 1):
                load_xt(0, s)
                load_rows(0, s)

            table_v = rows(table)

            def store_r(t):
                wait(sp, r_ok, t.u + 1)
                sp.dma_start(table_v[:, bass.ds(t.u * 2, 2), :], acc[0:P, bass.ds(t.u * 2, 2), :]).then_inc(r_st, 16)
            attention_io(0, next_inputs1, store_r)
            wait(sp, w_mm, 2 * STEPS)
            for s in (0, 1):
                load_xt(0, s)
            sp.dma_start(proj_w, chunks(d["L0_mix_proj_w"])).then_inc(proj_in, 16)
            for t, s in ((mlp1_w, chunks(d["L0_mix_mlp_w1"])), (mlp2_w, chunks(d["L0_mix_mlp_w2"])),
                         (gnn2_w, chunks(d["L0_gnn_W2"])), (fc2_w, chunks(d["fc2_t"]))):
                sp.dma_start(t[:], s).then_inc(late_in, 16)
            wait(sp, r_st, 16 * STEPS)
            phase_end(sp, 2)

            def store_y(t):
                wait(sp, y_ok[t.s], t.j + 1)
                sp.dma_start(rows(y_d)[:, bass.ds(t.u * 2, 2), :], y_out[0:P, t.s]).then_inc(y_st[t.s], 16)
            attention_io(1, next_inputs2, store_y)

            wait(sp, y_st[0], 16 * 13)
            wait(sp, y_st[1], 16 * 12)
            phase_end(sp, 3)

            def load_xd(j, s):
                sp.dma_start(x3[0:P, s], x_d[:, bass.ds(j * 4 + 2 * s, 2), :]).then_inc(x3_ld[s], 16)

            def load_yd(j, s):
                sp.dma_start(y3[0:P, s], rows(y_d)[:, bass.ds(j * 4 + 2 * s, 2), :]).then_inc(y_ld[s], 16)

            def mlp_io(t, more, n=2 * SP):
                if more:
                    after = t.j + 1
                    wait(sp, zadd, t.u + 1)
                    load_xd(after, t.s)
                    wait(sp, h_rows, t.g + 1)
                    load_yd(after, t.s)
                    wait(sp, ring_free[BATCHES - 1], t.u + 1)
                    load_idx(after, t.s, n)
                wait(sp, z_ok, t.u + 1)
                sp.dma_start(rows(z_d)[:, bass.ds(t.u * 2, 2), :], z3[0:P, t.s]).then_inc(z_st[t.s], 16)
            for s in (0, 1):
                load_xd(0, s)
                load_yd(0, s)
            for t, s in ((mb2_bc, "L0_mix_mlp_b2"), (b2_bc, "L0_gnn_b2")):
                sp.dma_start(t[:, :], d[s].partition_broadcast(128)).then_inc(rows_in, 16)
            with sp.Fori(0, STEPS // 2 - 1) as j:
                mlp_io(Step(0, j, 0), True)
                mlp_io(Step(0, j, 1), True)
            mlp_io(Step(0, STEPS // 2 - 1, 0), True, 2 * LAST)
            mlp_io(Step(0, STEPS // 2 - 1, 1), False)
            mlp_io(Step(0, STEPS // 2, 0), False)
            wait(sp, z_st[0], 16 * 13)
            wait(sp, z_st[1], 16 * 12)
            phase_end(sp, 4)

            sp.dma_start(interp, chunks(d["c_interp"])).then_inc(ev_fc, 16)
            sp.dma_start(fc1_t, chunks(d["fc1_t"])).then_inc(ev_fc, 16)

            def load_z(j, s):
                sp.dma_start(z4[0:P, s], rows(z_d)[:, bass.ds(j * 4 + 2 * s, 2), :]).then_inc(z_ld[s], 16)

            def tail_io(t, more, last):
                if more:
                    after = t.j + 1
                    wait(sp, x1_ok[t.s], t.j + 1)
                    load_z(after, t.s)
                wait(sp, o_ok, t.u + 1)
                sp.dma_start(out_d[:, bass.ds(t.u * 2, 2), :], o4[0:P, t.s]).then_inc(o_st[t.s], 16)
            load_z(0, 0)
            load_z(0, 1)
            phase_steps_ahead(sp, 0, tail_io)
            wait(sp, o_st[0], 16 * 13)
            wait(sp, o_st[1], 16 * 12)

        @block.gpsimd
        def _(pool):
            wait(pool, ev("counters_set"), 1)
            pool.dma_start(sorted_d.rearrange("(p g) e -> p (g e)", g=GROUPS),
                         d["c_blank"].partition_broadcast(128)).then_inc(prefill, 16)

            for t, s in ((k_raw, kqv[:, :, 0:D]), (kt_raw, chunks(d["kq_t"][0:D, :])), (gnn1_raw, chunks(d["L0_gnn_W1"])),
                         (wt_a, chunks(d["w_t"])), (n1g, col(d["L0_mix_n1_g"])),
                         (n1b, col(d["L0_mix_n1_b"])), (kqb, col(d["L0_mix_kqv_b"][0:2 * D])),
                         (b1_bc, d["L0_gnn_b1"].partition_broadcast(128)),
                         (bk_bc, d["L0_mix_kqv_b"][0:D].partition_broadcast(128)),
                         (bq_bc, d["L0_mix_kqv_b"][D:2 * D].partition_broadcast(128)),
                         (bv_bc, d["L0_mix_kqv_b"][2 * D:3 * D].partition_broadcast(128)),
                         (bvp_bc, d["L0_mix_proj_b"].partition_broadcast(128))):
                pool.dma_start(t, s, allow_slow_non_contiguous=True).then_inc(w_in, 16)
            wait(pool, ev("slots0"), 1)
            wait(pool, prefill, 16)

            def carry_waits(n):
                wait(pool, pool_self, n + 1)
                pool.tensor_tensor(pool_tiny[0:1, 1:2], pool_tiny[0:1, 0:1], pool_tiny[0:1, 0:1],
                                   ALU.add).then_inc(pool_self, 1)

            pool.memset(pool_tiny[:, :], 0.0).then_inc(pool_self, 1)

            def scatter(j, s):
                wait(pool, scattered[s], j * (16 * SG))
                c = (j * 2 + s) * SG
                pool.tensor_copy(stage_slot[0:P, s], slot_of[0:P, bass.ds(c, SG)]).then_inc(staged, 1)
                pool.tensor_copy(stage_pay[0:P, s], payload.rearrange("p j e -> p (j e)")[0:P, bass.ds(c * 2, 2 * SG)]).then_inc(staged, 1)
                wait(pool, staged, (j * 2 + s) * 2 + 2)
                carry_waits(j * 2 + s)
                for k in range(SG):
                    pool.indirect_dma_start(
                        out=sorted_d, out_offset=bass.IndirectOffsetOnAxis(ap=stage_slot[0:P, s, k:k + 1], axis=0),
                        in_=stage_pay[0:P, s, 2 * k:2 * k + 2], in_offset=None).then_inc(scattered[s], 16)
            scatter(0, 0)
            scatter(0, 1)
            with pool.Fori(1, EC // SG // 4) as j:
                scatter(j, 0)
                scatter(j, 1)
            wait(pool, ev("slots1"), 1)
            with pool.Fori(EC // SG // 4, EC // SG // 2) as j:
                scatter(j, 0)
                scatter(j, 1)

            def gather(t, k, n):
                wait(pool, idx_in[t.s], t.j * 16 + 16)
                wait(pool, ring_free[k], t.u)
                carry_waits(t.u * BATCHES + (EC // SG + k))
                for g in range(2 * n):
                    pool.indirect_dma_start(
                        out=ring[:, k, g], out_offset=None, in_=table,
                        in_offset=bass.IndirectOffsetOnAxis(ap=idx[:, t.s, k * 2 * PB + g, 0:1], axis=0)
                        ).then_inc(gathered[k], 16)

            def gather_step(t, last):
                for k, n in enumerate(LAST_BATCHES if last else [PB] * BATCHES):
                    gather(t, k, n)
            wait(pool, r_st, 16 * STEPS)
            wait(pool, v_mm, STEPS)
            for s in (0, 1):
                wait(pool, scattered[s], 8 * EC)
            phase_steps(pool, 0, gather_step)

            wait(pool, all_engines, 4 * 4)

            pool.memset(minus_half[:, :], -0.5).then_inc(ev("minus_half"), 1)
            wait(pool, ev("minus_half"), 1)

            def stage_acc(j, s):
                wait(pool, accs_tr[s], j)
                wait(pool, accs_deg[s], j)
                pool.tensor_copy(accs[0:P, s], acc[0:P, bass.ds(j * 4 + s * 2, 2), :]).then_inc(a_cp, 1)

            def roots(t):
                wait(pool, var_ok, t.u + 1)
                pool.tensor_tensor(rs[0:P, t.s], ve[0:P, t.s], minus_half[0:P, :], ALU.pow).then_inc(rs_ok, 1)

            def out_rows(t):
                wait(pool, dm, t.u + 1)
                wait(pool, xu, t.u + 1)
                for m in (0, 1):
                    o = o4[0:P, t.s, m].rearrange("p (c m) -> p c m", m=2)
                    mm = pool.tensor_tensor(o, o, dlm[0:P, m].unsqueeze(2).to_broadcast([P, HL, 2]), ALU.add)
                mm.then_inc(o_ok, 1)

            def pool_tail(t, more, last):
                if more:
                    stage_acc(t.j + 1, t.s)
                if not last:
                    roots(Step(0, t.j, 1) if t.s == 0 else Step(0, t.j + 1, 0))
                out_rows(t)
            stage_acc(0, 0)
            stage_acc(0, 1)
            roots(Step(0, 0, 0))
            phase_steps_ahead(pool, 0, pool_tail)

        @block.tensor
        def _(pe):
            wait(pe, ev("counters_set"), 1)
            wait(pe, ev("consts"), 1)
            for b in range(NT):
                wait(pe, onehots, b + 1)
                for h, bk in ((0, BA), (1, BB)):
                    last = pe.matmul(bk[:, 0:EH], strip[0:P, 49 - b:177 - b], onehot(b)[:, h * EH:(h + 1) * EH],
                                     start=b == 0, stop=b == NT - 1)
            last.then_inc(ev("pe_count"), 1)
            wait(pe, c_in, 6 * 16)
            wait(pe, ev("groups"), 1)
            pe.matmul(BC[:, 0:1], upper[:, :], n_pairs[:, :], start=True, stop=True).then_inc(ev("pe_base"), 1)
            wait(pe, ev("past"), 1)
            pe.matmul(BD[0:1, 0:PAIRS], ones_h[0:NT, 0:1], past[0:NT, :], start=True, stop=True).then_inc(ev("pe_tiles"), 1)
            wait(pe, ev("first"), 1)
            for h in (0, 1):
                cols = slice(h * EH, (h + 1) * EH)
                for b in range(NT):
                    i = h * NT + b
                    bk = (BA, BB, BF, BG)[i % 4]
                    if i >= 4:
                        wait(pe, rank_used, i - 3)
                    pe.matmul(bk[0:P, 0:EH], less[0:P, :], onehot(b)[:, cols], start=True, stop=False)
                    pe.matmul(bk[0:P, 0:EH], pick[:, b, :], first_h[:, cols], start=False, stop=True).then_inc(rank_mm, 1)
            def mean(bk, raw, n):
                for k in range(KC):
                    mm = pe.matmul(bk[:, 0:n], mean_w[:, :], raw[:, k, 0:n], start=k == 0, stop=k == KC - 1)
                return mm

            def bias_row(row, raw):
                for k in range(KC):
                    mm = pe.matmul(row[:, :], vb4[:, k, :], raw[:, k, :], start=k == 0, stop=k == KC - 1)
                return mm

            wait(pe, ev("bias_in"), 1)
            mean(BH, gnn1_raw, HID).then_inc(ev("gnn1_mean"), 1)

            def raw_products(name, raw, raw_t, wt, cols, row, folds):
                bias_row(row, raw)
                for c in range(KC):
                    for k in range(KC):
                        pe.matmul(cols[:, c:c + 1], raw[:, k, c * 128:(c + 1) * 128], n1b[:, k:k + 1],
                                  start=k == 0, stop=k == KC - 1)
                for c in range(KC):
                    for k in range(KC):
                        mm = pe.matmul(folds[c // 2][:, (c % 2) * M:(c % 2 + 1) * M], raw_t[:, k, c * 128:(c + 1) * 128],
                                       wt[:, k, :], start=k == 0, stop=k == KC - 1)
                mm.then_inc(ev(name + "_raw"), 1)

            def means(name, raw, folded, bias, wt, banks):
                wait(pe, ev(name + "_gained"), 1)
                mean(banks[0], raw, D)
                mean(banks[1], folded, M)
                for k in range(KC):
                    mm = pe.matmul(banks[2][:, 0:M], bias[:, k, :], wt[:, k, :], start=k == 0, stop=k == KC - 1)
                mm.then_inc(ev(name + "_mean"), 1)
            raw_products("k", k_raw, kt_raw, wt_a, BC, BD, (BA, BB))
            wait(pe, w2_in, 3 * 16)
            wait(pe, ev("gnn1_split"), 1)
            raw_products("q", q_raw, qt_raw, wt_b, BH, BG, (BE, BF))
            means("k", k_raw, folded_k, vb_k, wt_a, (BA, BB, BC))
            wait(pe, v_in, 16)
            bias_row(BD, v_raw).then_inc(ev("v_raw"), 1)
            means("q", q_raw, folded_q, vb_q, wt_b, (BE, BF, BG))
            wait(pe, ev("v_gained"), 1)
            mean(BH, v_raw, D).then_inc(ev("v_mean"), 1)
            phase_end(pe, 1)

            def next_step(t):
                return Step(t.phase, t.j, 1) if t.s == 0 else Step(t.phase, t.j + 1, 0)

            def product(bk, t, m, parts, off, n):
                rhs = lambda h, c: parts[:, h, c, off:off + n].bitcast(F32R)
                for c in range(KC):
                    high, low = (v[:, t.s, c, m * P:(m + 1) * P].bitcast(F32R) for v in (xh, xl))
                    pe.matmul(bk, high, rhs(0, c), start=c == 0, stop=False)
                    pe.matmul(bk, high, rhs(1, c), start=False, stop=False)
                    mm = pe.matmul(bk, low, rhs(0, c), start=False, stop=c == KC - 1)
                return mm

            for bk in (BC, BD):
                pe.matmul(bk[:, :], zero_row[0:1, 0:128], zero_row[0:1, 0:512], start=True, stop=False)

            def kr_products(t, m):
                if m == 0:
                    wait(pe, split, t.g + 1)
                wait(pe, k_ok, t.g * 2)
                product((BA, BE)[m][0:P, :], t, m, w1_parts, WK, D).then_inc(k_mm, 1)
                wait(pe, w_ok, t.g * 2)
                wait(pe, r_up, t.u * 2)
                product((BB, BF)[m][0:P, :], t, m, w1_parts, WR, HID + M).then_inc(w_mm, 1)

            def phase1(t, last):
                kr_products(t, 1)
                if not last:
                    kr_products(next_step(t), 0)
                wait(pe, x_ld[t.s], t.j * 16 + 16)
                wait(pe, kadd, t.u + 1)
                for k in range(KC):
                    for m in (0, 1):
                        mm = pe.matmul((BC, BD)[k // 2][:, (k % 2) * M:(k % 2 + 1) * M],
                                       x_in[0:P, t.s, m, k * 128:(k + 1) * 128], kpn[0:P, m, :],
                                       start=False, stop=False)
                mm.then_inc(hk_mm, 1)
            kr_products(Step(0, 0, 0), 0)
            phase_steps(pe, 0, phase1)
            for bk in (BC, BD):
                mm = pe.matmul(bk[:, :], zero_row[0:1, 0:128], zero_row[0:1, 0:512], start=False, stop=True)
            mm.then_inc(ev("pe_hk"), 1)
            for m in (0, 1):
                mm = pe.matmul(BE[:, 0:M], ones[0:P, :], kps[0:P, m, :], start=m == 0, stop=m == 1)
            mm.then_inc(ev("pe_ksum"), 1)
            wait(pe, ev("hk"), 1)
            for c in range(KC):
                bk = (BA, BB)[c // 2][:, (c % 2) * M:(c % 2 + 1) * M]
                for k in range(KC):
                    for h in (0, 1):
                        pe.matmul(bk, w2_parts[:, h, k, WV + c * 128:WV + (c + 1) * 128], hk[:, k, :],
                                  start=k == 0 and h == 0, stop=False)
                mm = pe.matmul(bk, bv_bc[0:1, c * 128:(c + 1) * 128], ks_bc[0:1, :], start=False, stop=True)
            mm.then_inc(ev("pe_kptv"), 1)
            wait(pe, ev("kptv"), 1)
            wait(pe, proj_in, 16)
            for m in range(KH):
                for c in range(KC):
                    mm = pe.matmul((BF, BH)[m][:, :], kptv[:, c, m * 128:(m + 1) * 128], proj_w[:, c, :],
                                   start=c == 0, stop=c == KC - 1)
            mm.then_inc(ev("pe_pmat"), 1)
            phase_end(pe, 2)

            def q_products(t, m):
                if m == 0:
                    wait(pe, split, t.g + 1)
                    wait(pe, w_ok, t.g * 2)
                wait(pe, k_ok, t.g * 2)
                product((BA, BE)[m][0:P, :], t, m, w2_parts, WQ, D).then_inc(k_mm, 1)
                product(BB[0:P, m * M:(m + 1) * M], t, m, w2_parts, WQW, M).then_inc(w_mm, 1)

            def phase2(t, last):
                banks = ((BC, BD), (BG, BH))[t.s]
                wait(pe, y_ok[t.s], t.j)
                for m in (0, 1):
                    rhs = lambda h, c: w2_parts[:, h, c, WV:WV + D].bitcast(F32R)
                    for c in range(KC):
                        high, low = (v[:, t.s, c, m * P:(m + 1) * P].bitcast(F32R) for v in (xh, xl))
                        pe.matmul(banks[m][0:P, :], high, rhs(0, c), start=c == 0, stop=False)
                        pe.matmul(banks[m][0:P, :], high, rhs(1, c), start=False, stop=False)
                        mm = pe.matmul(banks[m][0:P, :], low, rhs(0, c), start=False, stop=False)
                mm.then_inc(v_mm, 1)
                if not last:
                    q_products(next_step(t), 0)
                wait(pe, qn, t.u + 1)
                wait(pe, qtc, t.u)
                for c in range(KH):
                    for m in (0, 1):
                        mm = pe.transpose(BF[:, c * 250 + m * P:c * 250 + (m + 1) * P],
                                          kpn[0:P, m, c * 128:(c + 1) * 128], ident[0:P, 0:P])
                mm.then_inc(qt, 1)
                if not last:
                    q_products(next_step(t), 1)
                wait(pe, qtc, t.u + 1)
                for m in (0, 1):
                    for c in range(KH):
                        mm = pe.matmul(banks[m][0:P, :], qpT[:, c, m * P:(m + 1) * P], pmat[:, c, :],
                                       start=False, stop=c == KH - 1)
                mm.then_inc(y_mm, 1)
            q_products(Step(1, 0, 0), 0)
            q_products(Step(1, 0, 0), 1)
            phase_steps(pe, 1, phase2)
            wait(pe, late_in, 4 * 16)
            wait(pe, rows_in, 5 * 16)
            for c in range(KC):
                for k in range(KC):
                    mm = pe.matmul(BE[:, c:c + 1], mlp1_w[:, k, c * 128:(c + 1) * 128], n2b[:, k:k + 1],
                                   start=k == 0, stop=k == KC - 1)
            mm.then_inc(ev("pe_mbias"), 1)
            phase_end(pe, 3)

            def transposes(t, rows_sb):
                wait(pe, h_rows, t.g + 1)
                wait(pe, h_t, t.g * 2)
                for bk, cs in ((BF, (0, 1)), (BG, (2, 3))):
                    for i, c in enumerate(cs):
                        for m in (0, 1):
                            last = pe.transpose(bk[:, i * 250 + m * P:i * 250 + m * P + P],
                                                rows_sb[0:P, t.s, m, c * 128:(c + 1) * 128], ident[0:P, 0:P])
                    last.then_inc(tr, 1)

            def features(t, w, off, rhs):
                for i, bk in ((0, BA), (1, BB)):
                    wait(pe, h_t, t.g * 2 + 2)
                    wait(pe, feat_c, t.g * 2 + i)
                    for c in (2 * i, 2 * i + 1):
                        for k in range(KC):
                            last = pe.matmul(bk[:, (c % 2) * 250:(c % 2) * 250 + 2 * P],
                                             w[:, k, off + c * 128:off + (c + 1) * 128], rhs[:, t.s, k, :],
                                             start=k == 0, stop=k == KC - 1)
                    last.then_inc(feat, 1)

            transposes(Step(0, 0, 0), h3)

            def groups(t, k, n):
                i = t.s * BATCHES + k
                wait(pe, hits, t.j * (2 * BATCHES) + i + 1)
                wait(pe, gathered[k], t.u * (32 * PB) + 32 * n)
                for g in range(n):
                    at = i * PB + g
                    wait(pe, g_add[at % 2], t.j * SP + at // 2)
                    for m in (0, 1):
                        mm = pe.matmul((BE, BH)[at % 2][0:P, 0:RW], hit[k][:, 2 * g + m, :], ring[:, k, 2 * g + m, :],
                                       start=m == 0, stop=m == 1)
                    mm.then_inc(g_mm, 1)
                pe.drain().then_inc(ring_free[k], 1)

            def phase3(t, last):
                batches = LAST_BATCHES if last else [PB] * BATCHES
                features(t, mlp1_w, 0, hT3)
                if not last:
                    groups(t, 0, batches[0])
                wait(pe, feat_c, t.g * 2 + 2)
                wait(pe, z_ok, t.u)
                for m, bk in ((0, BC), (1, BD)):
                    for k in range(KC):
                        mm = pe.matmul(bk[0:P, :], gT3[:, k, m * P:(m + 1) * P], mlp2_w[:, k, :],
                                       start=k == 0, stop=k == KC - 1)
                mm.then_inc(m_mm, 1)
                if last:
                    groups(t, 0, batches[0])
                groups(t, 1, batches[1])
                if not last:
                    transposes(next_step(t), h3)
                for k in range(2, len(batches)):
                    groups(t, k, batches[k])
            phase_steps(pe, 0, phase3)
            phase_end(pe, 4)

            def acc_transposes(t):
                wait(pe, a_cp, t.u + 1)
                wait(pe, a_t, t.u)
                for c in range(KH):
                    for m in (0, 1):
                        mm = pe.transpose(BF[:, c * 250 + m * P:c * 250 + (m + 1) * P],
                                          accs[0:P, t.s, m, c * 128:(c + 1) * 128], ident[0:P, 0:P])
                mm.then_inc(accs_tr[t.s], 1)

            def w2_products(t):
                wait(pe, a_t, t.u + 1)
                wait(pe, x1_ok[t.s], t.j)
                for m in (0, 1):
                    bk = ((BC, BD), (BA, BB))[t.s][m]
                    for c in range(KH):
                        mm = pe.matmul(bk[0:P, :], accT[:, t.s, c, m * P:(m + 1) * P], gnn2_w[:, c, :],
                                       start=c == 0, stop=c == KH - 1)
                mm.then_inc(a_mm, 1)

            def phase4(t, more, last):
                wait(pe, llr, t.u + 1)
                wait(pe, ll_t, t.u)
                for c in (0, 1):
                    mm = pe.transpose(BE[:, c * P:(c + 1) * P], ll[0:P, t.s, c * 128:(c + 1) * 128], ident[0:P, 0:P])
                mm.then_inc(ll_tr, 1)
                wait(pe, ll_t, t.u + 1)
                wait(pe, gl, t.u)
                for h in (0, 1):
                    for i in (0, 1):
                        mm = pe.matmul(BH[:, h * P:(h + 1) * P], fc1e[:, i, h * 128:(h + 1) * 128], llT[:, i, :],
                                       start=i == 0, stop=i == 1)
                mm.then_inc(f1, 1)
                if more:
                    acc_transposes(Step(0, t.j + 1, t.s))
                wait(pe, gl, t.u + 1)
                wait(pe, dl, t.u)
                for c in (0, 1):
                    mm = pe.matmul(BG[0:P, 0:HL], gT4[:, c, :], fc2_w[:, c, :], start=c == 0, stop=c == 1)
                mm.then_inc(f2, 1)
                if more:
                    w2_products(Step(0, t.j + 1, t.s))
            for s in (0, 1):
                acc_transposes(Step(0, 0, s))
                w2_products(Step(0, 0, s))
            wait(pe, ev_fc, 32)
            for i in range(2):
                for k in range(i, i + 3):
                    mm = pe.matmul(BE[:, i * HL:(i + 1) * HL], interp[:, k, i * 128:(i + 1) * 128], fc1_t[:, k, :],
                                   start=k == i, stop=k == i + 2)
            mm.then_inc(ev("pe_fc1"), 1)
            wait(pe, ev("a_fc1"), 1)
            phase_steps_ahead(pe, 0, phase4)

        @block.scalar
        def _(act):
            wait(act, ev("counters_set"), 1)
            wait(act, ev("consts"), 1)

            def stats(t, last):
                wait(act, xs_in[t.s], t.j * 16 + 16)
                for i in (0, 1):
                    act.activation(xs[0:P, t.s, i], xs[0:P, t.s, i], ACT.Copy,
                                   accum_out=sum_x[0:P, bass.ds(t.u * 2 + i, 1)]).then_inc(st_sum, 1)
                wait(act, st_sum, t.u * 2 + 2)
                act.activation(nmean[0:P, bass.ds(t.u * 2, 2)], sum_x[0:P, bass.ds(t.u * 2, 2)], ACT.Copy,
                               scale=-1.0 / D).then_inc(st_mean, 1)
                wait(act, st_mean, t.u + 1)
                for i in (0, 1):
                    mm = act.activation(xs[0:P, t.s, i], xs[0:P, t.s, i], ACT.Square, bias=nmean[0:P, bass.ds(t.u * 2 + i, 1)],
                                        accum_out=ssq[0:P, bass.ds(t.u * 2 + i, 1)])
                mm.then_inc(st_free, 1)
            phase_steps(act, 0, stats)
            wait(act, st_free, STEPS)
            act.activation(tmp_a[0:P, :], ssq[0:P, :], ACT.Sqrt, scale=1.0 / D, bias=eps_c[0:P, 0:1]).then_inc(ev("a_s1"), 1)
            wait(act, ev("v_var2"), 1)
            act.activation(sinv12[0:P, :], tmp_b[0:P, :], ACT.Sqrt, bias=eps_c[0:P, 1:2]).then_inc(ev("a_s2"), 1)
            phase_end(act, 1)

            def copy_hT(t, dst):
                for i, bk in ((0, BF), (1, BG)):
                    wait(act, tr, t.g * 2 + i + 1)
                    act.copy(dst[:, t.s, 2 * i:2 * i + 2, :].rearrange("p a b -> p (a b)"), bk[:, 0:500]).then_inc(h_t, 1)

            def exps(t, used):
                for m in (0, 1):
                    wait(act, k_ok, t.g * 2 + m + 1)
                    act.activation(kk[0:P, m], kk[0:P, m], ACT.Square, scale=0.5 ** 0.5,
                                   accum_out=hsq[0:P, m:m + 1]).then_inc(sq, 1)
                wait(act, sq, t.g * 2 + 2)
                act.activation(nxd[0:P, :], hsq[0:P, :], ACT.Copy, scale=-1.0).then_inc(nx, 1)
                wait(act, nx, t.g + 1)
                used(t)
                for m in (0, 1):
                    wait(act, w_ok, t.g * 2 + m + 1)
                    act.activation(kp[0:P, m], kw[0:P, m], ACT.Exp, bias=nxd[0:P, m:m + 1]).then_inc(ex, 1)

            def next_step(t):
                return Step(t.phase, t.j, 1) if t.s == 0 else Step(t.phase, t.j + 1, 0)

            phase_steps(act, 0, lambda t, last: exps(t, lambda t: wait(act, kadd, t.u)))
            phase_end(act, 2)

            def phase2(t, last):
                exps(t, lambda t: wait(act, qn, t.u))
                wait(act, qt, t.u + 1)
                wait(act, y_mm, t.u)
                act.copy(qpT.rearrange("p a b -> p (a b)"), BF[:, 0:500]).then_inc(qtc, 1)
            phase_steps(act, 1, phase2)
            phase_end(act, 3)

            act.activation(tmp_a[0:P, :], mv[0:P, :, 1], ACT.Sqrt, bias=eps_c[0:P, 1:2]).then_inc(ev("a_s3"), 1)
            wait(act, ev("v_s3"), 1)

            def norm_rows(t):
                wait(act, y_ld[t.s], t.j * 16 + 16)
                wait(act, tr, t.g * 2)
                for m in (0, 1):
                    last = act.activation(h3[0:P, t.s, m], y3[0:P, t.s, m], ACT.Identity,
                                          scale=s12[0:P, bass.ds(t.u * 2 + m, 1)], bias=nm12[0:P, bass.ds(t.u * 2 + m, 1)])
                last.then_inc(h_rows, 1)
            norm_rows(Step(0, 0, 0))
            copy_hT(Step(0, 0, 0), hT3)

            def phase3(t, last):
                if not last:
                    norm_rows(next_step(t))
                wait(act, m_mm, t.u)
                for i, bk in ((0, BA), (1, BB)):
                    wait(act, feat, t.g * 2 + i + 1)
                    for c in (2 * i, 2 * i + 1):
                        mm = act.activation(gT3[:, c, :], bk[:, (c % 2) * 250:(c % 2) * 250 + 250], ACT.Gelu,
                                            bias=m1b[:, c:c + 1])
                    mm.then_inc(feat_c, 1)
                if not last:
                    copy_hT(next_step(t), hT3)
            phase_steps(act, 0, phase3)
            phase_end(act, 4)

            def copy_accT(t):
                wait(act, accs_tr[t.s], t.j + 1)
                wait(act, a_mm, t.u)
                act.copy(accT[:, t.s].rearrange("p a b -> p (a b)"), BF[:, 0:500]).then_inc(a_t, 1)

            def scaled_rows(t):
                wait(act, sc_ok, t.u + 1)
                wait(act, o_st[t.s], t.j * 16)
                for m in (0, 1):
                    mm = act.activation(o4[0:P, t.s, m], x4[0:P, t.s, m], ACT.Copy, scale=up[0:P, t.s, m:m + 1])
                mm.then_inc(xu, 1)

            def phase4(t, more, last):
                wait(act, ll_tr, t.u + 1)
                wait(act, f1, t.u)
                act.copy(llT.rearrange("p a b -> p (a b)"), BE[:, 0:2 * P]).then_inc(ll_t, 1)
                wait(act, f1, t.u + 1)
                wait(act, f2, t.u)
                for h in (0, 1):
                    mm = act.activation(gT4[:, h, :], BH[:, h * P:(h + 1) * P], ACT.Gelu, bias=f1b[:, h:h + 1])
                mm.then_inc(gl, 1)
                if more:
                    copy_accT(Step(0, t.j + 1, t.s))
                if not last:
                    scaled_rows(next_step(t))
            copy_accT(Step(0, 0, 0))
            copy_accT(Step(0, 0, 1))
            wait(act, ev("pe_fc1"), 1)
            act.activation(fc1e.rearrange("p a b -> p (a b)"), BE[:, :], ACT.Copy, scale=0.5).then_inc(ev("a_fc1"), 1)
            scaled_rows(Step(0, 0, 0))
            phase_steps_ahead(act, 0, phase4)

        @block.vector
        def _(dve):
            wait(dve, ev("counters_set"), 1)
            n_self = [0]

            def seq(inst):
                n_self[0] += 1
                inst.then_inc(dve_self, 1)
                wait(dve, dve_self, n_self[0])

            def ts(out, in0, a, op0, b=None, op1=ALU.bypass):
                seq(dve.tensor_scalar(out, in0, a, b, op0, op1))

            dve.memset(ones[:, :], 1.0)
            dve.memset(ones_h[:, :], 1.0)
            dve.memset(neg_half[:, :], -0.5)
            dve.memset(zero_row[:, :], 0.0)
            dve.memset(eps_c[:, 0:1], EPS1)
            dve.memset(mean_w[:, :], 1.0 / D)
            seq(dve.memset(eps_c[:, 1:2], EPS2))
            seq(dve.memset(strip[0:P, :], 0.0))
            seq(dve.memset(strip[0:P, 49:50], 1.0))
            seq(dve.memset(strip[0:P, 113:114], 1.0))
            dve.drain().then_inc(ev("consts"), 1)
            wait(dve, e_in, 32)
            seq(dve.tensor_copy(src_f[0:P], src_i[0:P]))
            ts(blk_q[0:P], src_f[0:P], 1.0 / NT, ALU.mult, -0.49, ALU.add)
            ts(blk_q[0:P], blk_q[0:P], ROUND, ALU.add, ROUND, ALU.subtract)
            seq(dve.scalar_tensor_tensor(out=blk_h[0:P], in0=blk_q[0:P], scalar=-float(NT), in1=src_f[0:P],
                                         op0=ALU.mult, op1=ALU.add))
            for b in range(NT):
                dve.tensor_scalar(onehot(b), blk_h[0:P], float(b), None, ALU.is_equal).then_inc(onehots, 1)
            dve.tensor_copy(payload[0:P, :, 0], dst_i[0:P])
            dve.tensor_copy(payload[0:P, :, 1], blk_q[0:P])
            wait(dve, ev("pe_count"), 1)
            dve.tensor_copy(count[:, 0:EH], BA[:, 0:EH])
            seq(dve.tensor_copy(count[:, EH:EC], BB[:, 0:EH]))
            seq(dve.tensor_tensor_scan(incl[:, :], count[:, :], count[:, :], 0.0, ALU.add, ALU.max))
            ts(n_pairs[:, :], incl[:, EC - 1:EC], 1.0 / 256, ALU.mult, 255.0 / 256 - 0.5 + 1.0 / 512, ALU.add)
            ts(n_pairs[:, :], n_pairs[:, :], ROUND, ALU.add, ROUND, ALU.subtract)
            dve.drain().then_inc(ev("groups"), 1)
            wait(dve, ev("pe_base"), 1)
            seq(dve.tensor_copy(base[:, :], BC[:, 0:1]))
            seq(dve.tensor_tensor(end_g[:, :], base[:, :], n_pairs[:, :], ALU.add))
            wait(dve, c_in, 6 * 16)
            dve.tensor_scalar(past[:, :], iota_g[:, :], end_g[:, 0:1], None, ALU.is_ge).then_inc(ev("past"), 1)
            seq(dve.tensor_tensor(first[:, :], incl[:, :], count[:, :], ALU.subtract))
            ts(base[:, :], base[:, :], 256.0, ALU.mult)
            ts(first[:, :], first[:, :], base[:, 0:1], ALU.add)
            ts(count[:, :], first[:, :], 1.0 / 128, ALU.mult, -0.5 + 1.0 / 256, ALU.add)
            ts(count[:, :], count[:, :], ROUND, ALU.add, ROUND, ALU.subtract)
            dve.tensor_copy(first_h[0:64], count[0:64])
            seq(dve.scalar_tensor_tensor(out=first_h[64:128], in0=count[64:128], scalar=-128.0, in1=first[64:128],
                                         op0=ALU.mult, op1=ALU.add))
            dve.drain().then_inc(ev("first"), 1)
            wait(dve, ev("pe_tiles"), 1)
            seq(dve.tensor_scalar(pair_off[0:1, :], BD[0:1, 0:PAIRS], float(NT - 1), float(RW), ALU.min, ALU.mult))
            seq(dve.memset(pos[0:P], 0.0))
            seq(dve.memset(count[0:P], 0.0))
            for h in (0, 1):
                cols = slice(h * EH, (h + 1) * EH)
                for b in range(NT):
                    i = h * NT + b
                    if b > 1:
                        wait(dve, rank_used, i - 1)
                    wait(dve, rank_mm, i + 1)
                    dve.copy_predicated((pos, count)[b % 2][0:P, cols], onehot(b)[:, cols].bitcast(U16),
                                        (BA, BB, BF, BG)[i % 4][0:P, 0:EH]).then_inc(rank_used, 1)
                wait(dve, rank_used, (h + 1) * NT)
                at, group = pos[0:P, cols], src_f[0:P, cols]
                seq(dve.tensor_tensor(at, at, count[0:P, cols], ALU.add))
                ts(group, at, 1.0 / 128, ALU.mult, -0.5 + 1.0 / 256, ALU.add)
                ts(group, group, ROUND, ALU.add, ROUND, ALU.subtract)
                seq(dve.scalar_tensor_tensor(out=at, in0=group, scalar=-128.0, in1=at, op0=ALU.mult, op1=ALU.add))
                seq(dve.scalar_tensor_tensor(out=slot_of[0:P, cols], in0=at, scalar=float(GROUPS), in1=group,
                                             op0=ALU.mult, op1=ALU.add))
                dve.drain().then_inc(ev(f"slots{h}"), 1)

            def centre_and_split(raw, bk, n, parts, off):
                seq(dve.tensor_tensor(raw, raw, bk[:, 0:n].unsqueeze(1).to_broadcast([128, KC, n]), ALU.subtract))
                high, low = (parts[:, h, :, off:off + n] for h in (0, 1))
                seq(dve.tensor_copy(high.bitcast(F32R), raw))
                seq(dve.tensor_tensor(low.bitcast(F32R), raw, high, ALU.subtract))

            def gain(raw):
                for k in range(KC):
                    mm = dve.tensor_scalar(raw[:, k, :], raw[:, k, :], n1g[:, k:k + 1], None, ALU.mult)
                return mm

            wait(dve, w_in, 12 * 16)
            for k in range(KC):
                dve.tensor_copy(vb4[:, k, :], n1b[:, k:k + 1].to_broadcast([128, 128]))
            dve.drain().then_inc(ev("bias_in"), 1)
            wait(dve, ev("gnn1_mean"), 1)
            centre_and_split(gnn1_raw, BH, HID, w1_parts, WR)
            dve.drain().then_inc(ev("gnn1_split"), 1)

            def gains(name, raw, folded, bias, row, kq_cols, cols, row_bank, folds):
                wait(dve, ev(name + "_raw"), 1)
                dve.tensor_tensor(row[:, :], row[:, :], row_bank[:, :], ALU.add)
                seq(dve.tensor_tensor(kq_cols, kq_cols, cols[:, 0:KC], ALU.add))
                for k in range(KC):
                    dve.tensor_copy(bias[:, k, :], kq_cols[:, k:k + 1].to_broadcast([128, 128]))
                for c in range(KC):
                    dve.tensor_scalar(folded[:, c, :], folds[c // 2][:, (c % 2) * M:(c % 2 + 1) * M],
                                      n1g[:, c:c + 1], None, ALU.mult)
                seq(gain(raw))
                dve.drain().then_inc(ev(name + "_gained"), 1)

            def splits(name, raw, folded, w_row, banks, parts, off, off_w):
                wait(dve, ev(name + "_mean"), 1)
                dve.tensor_copy(w_row[:, :], banks[2][:, 0:M])
                centre_and_split(raw, banks[0], D, parts, off)
                centre_and_split(folded, banks[1], M, parts, off_w)

            gains("k", k_raw, folded_k, vb_k, bk_bc, kqb[:, 0:KC], BC, BD, (BA, BB))
            gains("q", q_raw, folded_q, vb_q, bq_bc, kqb[:, KC:2 * KC], BH, BG, (BE, BF))
            splits("k", k_raw, folded_k, bkw_bc, (BA, BB, BC), w1_parts, WK, WKW)
            wait(dve, ev("v_raw"), 1)
            seq(dve.tensor_tensor(bv_bc[:, :], bv_bc[:, :], BD[:, :], ALU.add))
            dve.tensor_tensor(bvp_bc[:, :], bvp_bc[:, :], bv_bc[:, :], ALU.add)
            seq(gain(v_raw))
            dve.drain().then_inc(ev("v_gained"), 1)
            wait(dve, st_free, STEPS)
            splits("q", q_raw, folded_q, bqw_bc, (BE, BF, BG), w2_parts, WQ, WQW)
            wait(dve, ev("v_mean"), 1)
            centre_and_split(v_raw, BH, D, w2_parts, WV)
            seq(dve.memset(acc[0:P, :, HID:RW], 1.0))
            wait(dve, ev("a_s1"), 1)
            seq(dve.reciprocal(s1[0:P, :], tmp_a[0:P, :]))
            ts(tmp_b[0:P, :], ssq[0:P, :], 1.0 / D, ALU.mult)
            seq(dve.tensor_tensor(tmp_b[0:P, :], tmp_b[0:P, :], s1[0:P, :], ALU.mult))
            seq(dve.tensor_tensor(tmp_b[0:P, :], tmp_b[0:P, :], s1[0:P, :], ALU.mult))
            dve.drain().then_inc(ev("v_var2"), 1)
            wait(dve, ev("a_s2"), 1)
            seq(dve.reciprocal(s12[0:P, :], sinv12[0:P, :]))
            seq(dve.tensor_tensor(s12[0:P, :], s12[0:P, :], s1[0:P, :], ALU.mult))
            seq(dve.reciprocal(sinv12[0:P, :], s12[0:P, :]))
            phase_end(dve, 1)

            class Chain:

                def __init__(self, s, per):
                    self.sem, self.per = s, per

                def start(self, t):
                    self.t, self.n = t, 0

                def __call__(self, inst):
                    self.n += 1
                    inst.then_inc(self.sem, 1)

                def wait(self):
                    wait(dve, self.sem, self.t.u * self.per + self.n)

            def next_step(t):
                return Step(t.phase, t.j, 1) if t.s == 0 else Step(t.phase, t.j + 1, 0)

            def split_x(t, used, value, own):
                wait(dve, xt_ld[t.s], t.uses() * 16 + 16)
                wait(dve, used, value)
                own(dve.tensor_copy(xh[:, t.s].bitcast(F32R), xt[:, t.s]))
                own.wait()
                dve.tensor_tensor(xl[:, t.s].bitcast(F32R), xt[:, t.s], xh[:, t.s], ALU.subtract).then_inc(split, 1)

            def kq_rows(t, m, row):
                wait(dve, k_mm, t.g * 2 + m + 1)
                wait(dve, sq, t.g * 2)
                dve.scalar_tensor_tensor(out=kk[0:P, m], in0=(BA, BE)[m][0:P, :], scalar=s12[0:P, bass.ds(t.u * 2 + m, 1)],
                                         in1=row[0:P, :], op0=ALU.mult, op1=ALU.add).then_inc(k_ok, 1)

            def kqw_rows(t, m, bk, row, ready):
                wait(dve, w_mm, t.g * 2 + ready)
                wait(dve, ex, t.g * 2)
                dve.scalar_tensor_tensor(out=kw[0:P, m], in0=bk, scalar=s12[0:P, bass.ds(t.u * 2 + m, 1)],
                                         in1=row[0:P, :], op0=ALU.mult, op1=ALU.add).then_inc(w_ok, 1)

            own1 = Chain(dve_own[0], 2)

            class Once:
                def __call__(self, inst):
                    seq(inst)

                def wait(self):
                    pass
            seq(dve.memset(kps[0:P], 0.0))
            split_x(Step(0, 0, 0), split, 0, Once())

            def phase1(t, last):
                own1.start(t)
                if not last:
                    split_x(next_step(t), w_mm, t.g * 2, own1)
                for m in (0, 1):
                    kq_rows(t, m, bk_bc)
                    kqw_rows(t, m, (BB, BF)[m][0:P, HID:HID + M], bkw_bc, m + 1)
                    wait(dve, r_ok, t.u)
                    dve.scalar_tensor_tensor(out=rt[0:P, m], in0=(BB, BF)[m][0:P, 0:HID], scalar=s1[0:P, bass.ds(t.u * 2 + m, 1)],
                                             in1=b1_bc[0:P, :], op0=ALU.mult, op1=ALU.add).then_inc(r_up, 1)
                wait(dve, r_up, t.u * 2 + 2)
                dve.tensor_scalar(acc[0:P, bass.ds(t.u * 2, 2), 0:HID], rt[0:P], 0.0, None, ALU.max).then_inc(r_ok, 1)
                wait(dve, ex, t.g * 2 + 2)
                wait(dve, kadd, t.u)
                own1(dve.tensor_tensor(kps[0:P], kps[0:P], kp[0:P], ALU.add))
                wait(dve, hk_mm, t.u)
                for m in (0, 1):
                    mm = dve.tensor_scalar(kpn[0:P, m], kp[0:P, m], s12[0:P, bass.ds(t.u * 2 + m, 1)], None, ALU.mult)
                mm.then_inc(kadd, 1)
            phase_steps(dve, 0, phase1)

            wait(dve, ev("pe_ksum"), 1)
            for i, bk in ((0, BC), (1, BD)):
                dve.tensor_copy(hk[:, 2 * i:2 * i + 2, :].rearrange("p a b -> p (a b)"), bk[:, :])
            dve.tensor_copy(ks_bc[:, :], BE[:, 0:M])
            dve.drain().then_inc(ev("hk"), 1)
            for s in (0, 1):
                split_x(Step(1, 0, s), split, STEPS, Once())
            wait(dve, ev("pe_kptv"), 1)
            for i, bk in ((0, BA), (1, BB)):
                dve.tensor_copy(kptv[:, 2 * i:2 * i + 2, :].rearrange("p a b -> p (a b)"), bk[:, :])
            dve.drain().then_inc(ev("kptv"), 1)
            wait(dve, ev("pe_pmat"), 1)
            for m, bk in ((0, BF), (1, BH)):
                dve.tensor_copy(pmat[:, m, :], bk[:, :])
            phase_end(dve, 2)

            def row_stats(rows_sb, t, own):
                for m in (0, 1):
                    own(dve.bn_stats(stat6[0:P, m, :], rows_sb[:, m, :]))
                own.wait()
                own(dve.tensor_scalar(tiny[0:1, 0:1], stat6[0:1, 0, 0:1], 1.0, None, ALU.mult))
                for m in (0, 1):
                    own(dve.bn_aggr(mvs[0:P, m, :], stat6[0:P, m, :]))
                own.wait()
                return dve.tensor_copy(mv[0:P, bass.ds(t.u * 2, 2), :], mvs[0:P])

            own2 = Chain(dve_own[1], 13)

            def q_rows(t):
                for m in (0, 1):
                    kq_rows(t, m, bq_bc)
                for m in (0, 1):
                    kqw_rows(t, m, BB[0:P, m * M:(m + 1) * M], bqw_bc, 2)
            q_rows(Step(1, 0, 0))

            def phase2(t, more, last):
                own2.start(t)
                for m in (0, 1):
                    wait(dve, ex, t.g * 2 + m + 1)
                    own2(dve.scalar_tensor_tensor(out=junk[0:P, m], in0=kp[0:P, m], scalar=1.0, in1=ks_bc[0:P, :],
                                                  op0=ALU.mult, op1=ALU.mult, accum_out=den[0:P, m:m + 1]))
                own2.wait()
                own2(dve.tensor_scalar(den[0:P, :], den[0:P, :], 256.0 * EPS_ATTN, None, ALU.add))
                own2.wait()
                own2(dve.reciprocal(rden[0:P, :], den[0:P, :]))
                own2.wait()
                own2(dve.tensor_tensor(rden[0:P, :], rden[0:P, :], sinv12[0:P, bass.ds(t.u * 2, 2)], ALU.mult))
                own2.wait()
                wait(dve, qt, t.u)
                for m in (0, 1):
                    mm = dve.tensor_scalar(kpn[0:P, m], kp[0:P, m], rden[0:P, m:m + 1], None, ALU.mult)
                mm.then_inc(qn, 1)
                if not last:
                    q_rows(next_step(t))
                if more:
                    split_x(Step(1, t.j + 1, t.s), v_mm, t.u + 1, own2)
                else:
                    own2(dve.memset(quiet[0:1, last:last + 1], 0.0))
                wait(dve, y_mm, t.u + 1)
                wait(dve, y_st[t.s], t.j * 16)
                for m, bk in enumerate(((BC, BD), (BG, BH))[t.s]):
                    own2(dve.scalar_tensor_tensor(out=y_out[0:P, t.s, m], in0=bk[0:P, :], scalar=s12[0:P, bass.ds(t.u * 2 + m, 1)],
                                                  in1=bvp_bc[0:P, :], op0=ALU.mult, op1=ALU.add))
                own2.wait()
                row_stats(y_out[0:P, t.s], t, own2).then_inc(y_ok[t.s], 1)
            phase_steps_ahead(dve, 1, phase2)
            wait(dve, ev("pe_mbias"), 1)
            dve.tensor_tensor(m1b[:, :], m1b[:, :], BE[:, 0:KC], ALU.add)
            for k in range(KC):
                dve.tensor_scalar(mlp1_w[:, k, :], mlp1_w[:, k, :], n2g[:, k:k + 1], None, ALU.mult)
            phase_end(dve, 3)

            def scales(root_done):
                wait(dve, ev(root_done), 1)
                seq(dve.reciprocal(s12[0:P, :], tmp_a[0:P, :]))
                seq(dve.scalar_tensor_tensor(out=nm12[0:P, :], in0=mv[0:P, :, 0], scalar=-1.0, in1=s12[0:P, :],
                                             op0=ALU.mult, op1=ALU.mult))

            scales("a_s3")
            dve.drain().then_inc(ev("v_s3"), 1)
            own3 = Chain(dve_own[2], 2)

            def step_lanes(t, n=SP):
                wait(dve, idx_in[t.s], t.j * 16 + 16)
                dve.tensor_copy(lane_f[:, t.s, 0:2 * n], idx[:, t.s, 0:2 * n, 1]).then_inc(lanes, 1)

            def one_hots(t, k, n=PB):
                wait(dve, lanes, t.u + 1)
                wait(dve, ring_free[k], t.u)
                dve.tensor_tensor(hit[k][:, 0:2 * n, :], iota_p.unsqueeze(1).to_broadcast([128, 2 * n, P]),
                                  lane_f[:, t.s, k * 2 * PB:(k * PB + n) * 2].unsqueeze(2).to_broadcast([128, 2 * n, P]),
                                  ALU.is_equal).then_inc(hits, 1)

            def add_groups(t, k, n):
                i = t.s * BATCHES + k
                first_pair = t.j * (2 * SP) + i * PB
                _, offs = nc.values_load_multi_w_load_instructions(
                    pair_off[0:1, bass.ds(first_pair, n)], engines=[mybir.EngineType.DVE],
                    min_val=0, max_val=(NT - 1) * RW)
                flat_acc = ACC[0:P, :]
                for g in range(n):
                    at = i * PB + g
                    wait(dve, g_mm, first_pair + g + 1)
                    wait(dve, g_add[1 - at % 2], t.j * SP + (at + 1) // 2)
                    dst = flat_acc[:, bass.ds(offs[g], RW)]
                    dve.tensor_tensor(dst, dst, (BE, BH)[at % 2][0:P, 0:RW], ALU.add).then_inc(g_add[at % 2], 1)

            step_lanes(Step(0, 0, 0))
            one_hots(Step(0, 0, 0), 0)
            wait(dve, rows_in, 7 * 16)

            def phase3(t, last):
                own3.start(t)
                batches = LAST_BATCHES if last else [PB] * BATCHES
                wait(dve, x3_ld[t.s], t.j * 16 + 16)
                wait(dve, y_ld[t.s], t.j * 16 + 16)
                wait(dve, z_st[t.s], t.j * 16)
                dve.tensor_tensor(z3[0:P, t.s], x3[0:P, t.s], y3[0:P, t.s], ALU.add).then_inc(zadd, 1)
                wait(dve, zadd, t.u + 1)
                own3(dve.tensor_tensor(z3[0:P, t.s], z3[0:P, t.s], mb2_bc[0:P, :].unsqueeze(1).to_broadcast([P, 2, D]),
                                       ALU.add))
                one_hots(t, 1, batches[1])
                if not last:
                    add_groups(t, 0, batches[0])
                    one_hots(t, 2)
                own3.wait()
                wait(dve, m_mm, t.u + 1)
                for m, bk in ((0, BC), (1, BD)):
                    mm = dve.tensor_tensor(z3[0:P, t.s, m], z3[0:P, t.s, m], bk[0:P, :], ALU.add)
                    if m == 0:
                        own3(mm)
                mm.then_inc(z_ok, 1)
                if last:
                    add_groups(t, 0, batches[0])
                add_groups(t, 1, batches[1])
                if not last:
                    after = next_step(t)
                    step_lanes(after)
                    one_hots(after, 0)
                    add_groups(t, 2, PB)
            phase_steps(dve, 0, phase3)
            phase_end(dve, 4)

            own4 = Chain(dve_own[3], 10)
            seq(dve.tensor_scalar(fb2_bc[:, :], fb2_bc[:, :], 0.5, None, ALU.mult))

            def add_b2(t):
                wait(dve, z_ld[t.s], t.j * 16 + 16)
                wait(dve, a_cp, t.u + 1)
                for m in (0, 1):
                    mm = dve.scalar_tensor_tensor(out=z4[0:P, t.s, m], in0=b2_bc[0:P, :],
                                                  scalar=accs[0:P, t.s, m, HID:RW], in1=z4[0:P, t.s, m],
                                                  op0=ALU.mult, op1=ALU.add)
                mm.then_inc(accs_deg[t.s], 1)

            def x1_rows(t, free, own):
                wait(dve, accs_deg[t.s], t.j + 1)
                wait(dve, a_mm, t.u + 1)
                wait(dve, xu, free)
                for m in (0, 1):
                    bk = ((BC, BD), (BA, BB))[t.s][m]
                    mm = dve.tensor_tensor(x4[0:P, t.s, m], z4[0:P, t.s, m], bk[0:P, :], ALU.add)
                mm.then_inc(x1_ok[t.s], 1)
                wait(dve, x1_ok[t.s], t.j + 1)
                for m in (0, 1):
                    own(dve.bn_stats(stat6[0:P, m, :], x4[0:P, t.s, m]))
                own.wait()
                own(dve.tensor_scalar(tiny[0:1, 0:1], stat6[0:1, 0, 0:1], 1.0, None, ALU.mult))
                for m in (0, 1):
                    own(dve.bn_aggr(mv4[0:P, t.s, m, :], stat6[0:P, m, :]))
                own.wait()
                dve.tensor_scalar(ve[0:P, t.s], mv4[0:P, t.s, :, 1], EPS1, None, ALU.add).then_inc(var_ok, 1)

            def ll_rows(t, free, own):
                wait(dve, rs_ok, t.u + 1)
                own(dve.scalar_tensor_tensor(out=nm4[0:P, t.s], in0=mv4[0:P, t.s, :, 0], scalar=-1.0, in1=rs[0:P, t.s],
                                             op0=ALU.mult, op1=ALU.mult))
                dve.tensor_scalar(up[0:P, t.s], rs[0:P, t.s], 1.0, None, ALU.add).then_inc(sc_ok, 1)
                own.wait()
                own(dve.tensor_scalar(nms[0:P, t.s:t.s + 1], nm4[0:P, t.s, 0:1], nm4[0:P, t.s, 1:2], 2.0, ALU.add, ALU.mult))
                own(dve.tensor_scalar(xn4[0:P], x4[0:P, t.s, 1], rs[0:P, t.s, 1:2], None, ALU.mult))
                own.wait()
                own(dve.scalar_tensor_tensor(out=t4[0:P], in0=x4[0:P, t.s, 0], scalar=rs[0:P, t.s, 0:1],
                                             in1=xn4[0:P], op0=ALU.mult, op1=ALU.add))
                own.wait()
                cols = t4[0:P].rearrange("p (c m) -> p c m", m=2)
                wait(dve, ll_tr, free)
                dve.scalar_tensor_tensor(out=ll[0:P, t.s], in0=cols[:, :, 0], scalar=nms[0:P, t.s:t.s + 1], in1=cols[:, :, 1],
                                         op0=ALU.add, op1=ALU.add).then_inc(llr, 1)

            def phase4(t, last):
                own4.start(t)
                if not last:
                    add_b2(next_step(t))
                wait(dve, llr, t.u + 1)
                own4(dve.scalar_tensor_tensor(out=quarter[0:P], in0=ll[0:P, t.s], scalar=-0.25, in1=fb2_bc[0:P, :],
                                              op0=ALU.mult, op1=ALU.add))
                if not last:
                    x1_rows(next_step(t), t.u, own4)
                else:
                    own4.wait()
                wait(dve, f2, t.u + 1)
                dve.scalar_tensor_tensor(out=dlt[0:P], in0=BG[0:P, 0:HL], scalar=0.5, in1=quarter[0:P],
                                         op0=ALU.mult, op1=ALU.add).then_inc(dl, 1)
                wait(dve, dl, t.u + 1)
                wait(dve, o_ok, t.u)
                for m in (0, 1):
                    mm = dve.tensor_scalar(dlm[0:P, m], dlt[0:P], nm4[0:P, t.s, m:m + 1], None, ALU.add)
                mm.then_inc(dm, 1)
                if not last:
                    ll_rows(next_step(t), t.u, own4)
            add_b2(Step(0, 0, 0))
            x1_rows(Step(0, 0, 0), 0, Once())
            ll_rows(Step(0, 0, 0), 0, Once())
            phase_steps(dve, 0, phase4)


IN_SHAPES = {
    "x": (N, D), "src": (E,), "dst": (E,), "L0_gnn_W1": (D, HID), "L0_gnn_b1": (HID,), "L0_gnn_W2": (HID, D),
    "L0_gnn_b2": (D,), "L0_mix_kqv_w": (D, 3 * D), "L0_mix_kqv_b": (3 * D,), "L0_mix_proj_w": (D, D),
    "L0_mix_proj_b": (D,), "L0_mix_n1_g": (D,), "L0_mix_n1_b": (D,), "L0_mix_n2_g": (D,), "L0_mix_n2_b": (D,),
    "L0_mix_mlp_w1": (D, D), "L0_mix_mlp_b1": (D,), "L0_mix_mlp_w2": (D, D), "L0_mix_mlp_b2": (D,),
    "L0_ffn_fc1_b": (HL,), "L0_ffn_fc2_b": (HL,),
}


def shape_constants():
    k = np.arange(128)
    c = {
        "less": (np.arange(P)[:, None] < np.arange(P)[None, :]).astype(np.float16),
        "upper": ((k[:, None] < NT) & (k[:, None] < (k[None, :] % 64))).astype(np.float32),
        "iota_g": np.tile(np.arange(PAIRS, dtype=np.float32), (128, 1)),
        "iota_p": np.tile(np.arange(P, dtype=np.float32), (128, 1)),
        "ident": np.eye(128, dtype=np.float32),
        "blank": np.tile(np.array([0, 128], np.int32), GROUPS),
    }
    weight = np.where(k < 64, 128, 1)[:, None] * ((k % 64)[:, None] == np.arange(NT)[None, :])
    c["pick"] = np.broadcast_to(weight[:, :, None], (128, NT, P)).astype(np.float16)
    at = np.linspace(0.0, 1.0, D, dtype=np.float32) * np.float32(D // 2 - 1)
    low = np.clip(np.floor(at).astype(np.int32), 0, D // 2 - 2)
    w = at - low.astype(np.float32)
    interp = np.zeros((D, D // 2), np.float32)
    interp[np.arange(D), low] = np.float32(1) - w
    interp[np.arange(D), low + 1] += w
    c["interp"] = interp
    return {"c_" + name: np.ascontiguousarray(v) for name, v in c.items()}


def kernel(**inputs):
    import concourse.bacc as bacc
    from concourse.bass_utils import run_bass_kernel_spmd

    arrays = {name: np.ascontiguousarray(inputs[name]) for name in IN_SHAPES}
    x = arrays["x"].reshape(P, STEPS, 2, KC, 128)
    arrays["x_t"] = np.ascontiguousarray(x.transpose(4, 1, 3, 2, 0)).reshape(128, N * KC)
    arrays["kq_t"] = np.ascontiguousarray(arrays["L0_mix_kqv_w"][:, 0:2 * D].T)
    arrays["w_t"] = np.ascontiguousarray(np.asarray(inputs["L0_mix_w"]).T)
    arrays["fc1_t"] = np.ascontiguousarray(np.asarray(inputs["L0_ffn_fc1_w"]).T)
    arrays["fc2_t"] = np.ascontiguousarray(np.asarray(inputs["L0_ffn_fc2_w"]).T)
    arrays.update(shape_constants())
    nc = bacc.Bacc("TRN2", target_bir_lowering=False, num_devices=1)
    d = {name: nc.dram_tensor(name, a.shape, mybir.dt.from_np(a.dtype), kind="ExternalInput").ap()
         for name, a in arrays.items()}
    d["out"] = nc.dram_tensor("out", (N, D), F32, kind="ExternalOutput").ap()
    build_program(nc, d)
    result = run_bass_kernel_spmd(nc, [arrays], core_ids=[0])
    return result.results[0]["out"]
```
